# Optimizing a Trainium2 kernel written in Bass

```python
import numpy as np
import jax
import jax.numpy as jnp

def _softmax(x, axis=-1):
    return jax.nn.softmax(x, axis=axis)

def _gelu(x):
    return jax.nn.gelu(x, approximate=True)

def _silu(x):
    return jax.nn.silu(x)

def _sigmoid(x):
    return jax.nn.sigmoid(x)

def _layernorm(x, axis=-1, eps=1e-05):
    m = jnp.mean(x, axis=axis, keepdims=True)
    v = jnp.var(x, axis=axis, keepdims=True)
    return (x - m) / jnp.sqrt(v + eps)

def _scatter_add(tgt, idx, src, axis=0):
    return tgt.at[idx].add(src)

def _segment_sum(src, seg, n):
    return jax.ops.segment_sum(src, seg, n)
kernel_name = 'mk_flamingo_gated_d2_seqx_r4_b9f3e1'

def setup_inputs(seed: int=0):
    np.random.seed(seed)
    _w = jnp.asarray

    def _rec_inputs():
        import jax
        import jax.numpy as jnp
        _rk = jax.random.key(seed)
        x = -0.0003929 + 0.9999 * jax.random.normal(jax.random.fold_in(_rk, 1), (32, 112, 256), jnp.float32)
        _lenS = 112 - jax.random.randint(jax.random.fold_in(_rk, 7), (32,), 0, max(1, 112 // 4) + 1, jnp.int32)
        _lenS2 = 375 - jax.random.randint(jax.random.fold_in(_rk, 8), (32,), 0, max(1, 375 // 4) + 1, jnp.int32)
        _ctx_512P = jax.random.normal(jax.random.fold_in(_rk, 11), (32, 16, 128), jnp.float32)
        _ctx_512c = jax.random.dirichlet(jax.random.fold_in(_rk, 511), 0.3 * jnp.ones((16,), jnp.float32), (32, 375))
        _ctx_512t = jnp.einsum('bsk,bkd->bsd', _ctx_512c, _ctx_512P)
        _ctx_512t = _ctx_512t * jax.lax.rsqrt(jnp.mean(jnp.square(_ctx_512t)) + 1e-12) * 0.953939
        ctx_512 = -1.39393e-06 + 0.999914 * (_ctx_512t + 0.3 * jax.random.normal(jax.random.fold_in(_rk, 611), (32, 375, 128), jnp.float32))
        _g = jax.random.normal(jax.random.fold_in(_rk, 9001), (2, 2), jnp.float32)
        _g = jnp.sign(_g) * jnp.maximum(jnp.abs(_g), 1.0) + (_g == 0) * 1.0
        g_xattn = _g[0]
        g_ffn = _g[1]
        return (x, ctx_512, g_xattn, g_ffn)
    x, ctx_512, g_xattn, g_ffn = _rec_inputs()

    def _L0_xattn_setup():
        import jax, jax.numpy as jnp
        import numpy as np
        HEADS = 16
        D_MODEL = 256
        IMG_MODEL = 128
        D_K = D_MODEL // HEADS
        key = jax.random.key(seed)
        ks = jax.random.split(key, 12)
        B, LQ, LKV = (8, 512, 256)
        s_dm = 1.0 / np.sqrt(D_MODEL)
        s_im = 1.0 / np.sqrt(IMG_MODEL)
        return {'q': jax.random.normal(ks[0], (B, LQ, D_MODEL), jnp.float32), 'k': jax.random.normal(ks[1], (B, LKV, IMG_MODEL), jnp.float32), 'v': jax.random.normal(ks[2], (B, LKV, IMG_MODEL), jnp.float32), 'Wq': jax.random.normal(ks[3], (D_MODEL, D_MODEL), jnp.float32) * s_dm, 'bq': jnp.zeros((D_MODEL,), jnp.float32), 'Wk': jax.random.normal(ks[4], (IMG_MODEL, D_MODEL), jnp.float32) * s_im, 'bk': jnp.zeros((D_MODEL,), jnp.float32), 'Wv': jax.random.normal(ks[5], (IMG_MODEL, D_MODEL), jnp.float32) * s_im, 'bv': jnp.zeros((D_MODEL,), jnp.float32), 'Wo': jax.random.normal(ks[6], (D_MODEL, D_MODEL), jnp.float32) * s_dm, 'bo': jnp.zeros((D_MODEL,), jnp.float32)}
    _L0_xattn_all = _L0_xattn_setup()
    _L0_xattn_in = {k: v for k, v in _L0_xattn_all.items() if k in ('Wq', 'bq', 'Wk', 'bk', 'Wv', 'bv', 'Wo', 'bo')}
    del _L0_xattn_all

    def _L0_ffn_setup():
        import jax, jax.numpy as jnp
        import numpy as np
        from jax import lax
        T, B, I, M, O = (64, 64, 256, 256, 256)

        def _xavier(key, shape):
            fan_out, fan_in = shape
            limit = float(np.sqrt(6.0 / (fan_in + fan_out)))
            return jax.random.uniform(key, shape, jnp.float32, -limit, limit)
        key = jax.random.key(seed)
        ks = jax.random.split(key, 9)
        x = jax.random.normal(ks[0], (T, B, I), jnp.float32)
        return {'x': x, 'wf': _xavier(ks[1], (M, I)), 'uf': _xavier(ks[2], (M, M)), 'bf': jnp.zeros((M,), jnp.float32), 'wi': _xavier(ks[3], (M, I)), 'ui': _xavier(ks[4], (M, M)), 'bi': jnp.zeros((M,), jnp.float32), 'wc': _xavier(ks[5], (M, I)), 'uc': _xavier(ks[6], (M, M)), 'bc': jnp.zeros((M,), jnp.float32), 'wo': _xavier(ks[7], (O, I)), 'uo': _xavier(ks[8], (O, M)), 'bo': jnp.zeros((O,), jnp.float32), 'in_c': jnp.zeros((M,), jnp.float32)}
    _L0_ffn_all = _L0_ffn_setup()
    _L0_ffn_in = {k: v for k, v in _L0_ffn_all.items() if k in ('wf', 'uf', 'bf', 'wi', 'ui', 'bi', 'wc', 'uc', 'bc', 'wo', 'uo', 'bo', 'in_c')}
    del _L0_ffn_all

    def _L1_xattn_setup():
        import jax, jax.numpy as jnp
        import numpy as np
        NUM_HEADS = 16
        HEAD_DIM = 64
        Q_DIM = 256
        KV_DIM = 128
        INNER = NUM_HEADS * HEAD_DIM
        key = jax.random.key(seed)
        ks = jax.random.split(key, 7)
        B, N, M = (32, 128, 512)
        q = jax.random.normal(ks[0], (B, N, Q_DIM), dtype=jnp.float32)
        kv = jax.random.normal(ks[1], (B, M, KV_DIM), dtype=jnp.float32)
        Wq = jax.random.normal(ks[2], (Q_DIM, INNER), dtype=jnp.float32) / np.sqrt(Q_DIM)
        Wk = jax.random.normal(ks[3], (KV_DIM, INNER), dtype=jnp.float32) / np.sqrt(KV_DIM)
        Wv = jax.random.normal(ks[4], (KV_DIM, INNER), dtype=jnp.float32) / np.sqrt(KV_DIM)
        Wo = jax.random.normal(ks[5], (INNER, Q_DIM), dtype=jnp.float32) / np.sqrt(INNER)
        bo = jax.random.normal(ks[6], (Q_DIM,), dtype=jnp.float32) * 0.01
        return {'q': q, 'kv': kv, 'Wq': Wq, 'Wk': Wk, 'Wv': Wv, 'Wo': Wo, 'bo': bo}
    _L1_xattn_all = _L1_xattn_setup()
    _L1_xattn_in = {k: v for k, v in _L1_xattn_all.items() if k in ('Wq', 'Wk', 'Wv', 'Wo', 'bo')}
    del _L1_xattn_all

    def _L1_ffn_setup():
        import jax, jax.numpy as jnp
        import numpy as np
        TOP_K = 8
        key = jax.random.key(seed)
        ks = jax.random.split(key, 6)
        B, S, D, F, E = (2, 256, 256, 128, 64)
        x = jax.random.normal(ks[0], (B, S, D), dtype=jnp.float32)
        centroids = jax.random.normal(ks[1], (E, D), dtype=jnp.float32) * 0.05
        expert_biases = jnp.zeros((E,), dtype=jnp.float32)
        Ws_up = jax.random.normal(ks[2], (D, F), dtype=jnp.float32) / np.sqrt(D)
        Ws_down = jax.random.normal(ks[3], (F, D), dtype=jnp.float32) / np.sqrt(F)
        W_up = jax.random.normal(ks[4], (E, D, F), dtype=jnp.float32) / np.sqrt(D)
        W_down = jax.random.normal(ks[5], (E, F, D), dtype=jnp.float32) / np.sqrt(F)
        return {'x': x, 'centroids': centroids, 'expert_biases': expert_biases, 'Ws_up': Ws_up, 'Ws_down': Ws_down, 'W_up': W_up, 'W_down': W_down}
    _L1_ffn_all = _L1_ffn_setup()
    _L1_ffn_in = {k: v for k, v in _L1_ffn_all.items() if k in ('centroids', 'expert_biases', 'Ws_up', 'Ws_down', 'W_up', 'W_down')}
    del _L1_ffn_all
    return {'x': x, 'ctx_512': ctx_512, 'g_xattn': g_xattn, 'g_ffn': g_ffn, 'L0_xattn_Wq': _L0_xattn_in['Wq'], 'L0_xattn_bq': _L0_xattn_in['bq'], 'L0_xattn_Wk': _L0_xattn_in['Wk'], 'L0_xattn_bk': _L0_xattn_in['bk'], 'L0_xattn_Wv': _L0_xattn_in['Wv'], 'L0_xattn_bv': _L0_xattn_in['bv'], 'L0_xattn_Wo': _L0_xattn_in['Wo'], 'L0_xattn_bo': _L0_xattn_in['bo'], 'L0_ffn_wf': _L0_ffn_in['wf'], 'L0_ffn_uf': _L0_ffn_in['uf'], 'L0_ffn_bf': _L0_ffn_in['bf'], 'L0_ffn_wi': _L0_ffn_in['wi'], 'L0_ffn_ui': _L0_ffn_in['ui'], 'L0_ffn_bi': _L0_ffn_in['bi'], 'L0_ffn_wc': _L0_ffn_in['wc'], 'L0_ffn_uc': _L0_ffn_in['uc'], 'L0_ffn_bc': _L0_ffn_in['bc'], 'L0_ffn_wo': _L0_ffn_in['wo'], 'L0_ffn_uo': _L0_ffn_in['uo'], 'L0_ffn_bo': _L0_ffn_in['bo'], 'L0_ffn_in_c': _L0_ffn_in['in_c'], 'L1_xattn_Wq': _L1_xattn_in['Wq'], 'L1_xattn_Wk': _L1_xattn_in['Wk'], 'L1_xattn_Wv': _L1_xattn_in['Wv'], 'L1_xattn_Wo': _L1_xattn_in['Wo'], 'L1_xattn_bo': _L1_xattn_in['bo'], 'L1_ffn_centroids': _L1_ffn_in['centroids'], 'L1_ffn_expert_biases': _L1_ffn_in['expert_biases'], 'L1_ffn_Ws_up': _L1_ffn_in['Ws_up'], 'L1_ffn_Ws_down': _L1_ffn_in['Ws_down'], 'L1_ffn_W_up': _L1_ffn_in['W_up'], 'L1_ffn_W_down': _L1_ffn_in['W_down']}

def reference(x, ctx_512, g_xattn, g_ffn, L0_xattn_Wq, L0_xattn_bq, L0_xattn_Wk, L0_xattn_bk, L0_xattn_Wv, L0_xattn_bv, L0_xattn_Wo, L0_xattn_bo, L0_ffn_wf, L0_ffn_uf, L0_ffn_bf, L0_ffn_wi, L0_ffn_ui, L0_ffn_bi, L0_ffn_wc, L0_ffn_uc, L0_ffn_bc, L0_ffn_wo, L0_ffn_uo, L0_ffn_bo, L0_ffn_in_c, L1_xattn_Wq, L1_xattn_Wk, L1_xattn_Wv, L1_xattn_Wo, L1_xattn_bo, L1_ffn_centroids, L1_ffn_expert_biases, L1_ffn_Ws_up, L1_ffn_Ws_down, L1_ffn_W_up, L1_ffn_W_down):
    import jax
    import jax.numpy as jnp

    def _L0_xattn_ref(q, k, v, Wq, bq, Wk, bk, Wv, bv, Wo, bo):
        import jax, jax.numpy as jnp
        import numpy as np
        HEADS = 16
        D_MODEL = 256
        IMG_MODEL = 128
        D_K = D_MODEL // HEADS
        B, LQ, _ = q.shape
        LKV = k.shape[1]
        qh = (q @ Wq + bq).reshape(B, LQ, HEADS, D_K).transpose(0, 2, 1, 3)
        kh = (k @ Wk + bk).reshape(B, LKV, HEADS, D_K).transpose(0, 2, 1, 3)
        vh = (v @ Wv + bv).reshape(B, LKV, HEADS, D_K).transpose(0, 2, 1, 3)
        scale = 1.0 / np.sqrt(D_K)
        scores = jnp.einsum('bhqd,bhkd->bhqk', qh, kh) * scale
        attn = jax.nn.softmax(scores, axis=-1)
        out = jnp.einsum('bhqk,bhkd->bhqd', attn, vh)
        concat = out.transpose(0, 2, 1, 3).reshape(B, LQ, D_MODEL)
        return concat @ Wo + bo

    def _L0_ffn_ref(x, wf, uf, bf, wi, ui, bi, wc, uc, bc, wo, uo, bo, in_c):
        import jax, jax.numpy as jnp
        import numpy as np
        from jax import lax
        T, B, I, M, O = (64, 64, 256, 256, 256)

        def _xavier(key, shape):
            fan_out, fan_in = shape
            limit = float(np.sqrt(6.0 / (fan_in + fan_out)))
            return jax.random.uniform(key, shape, jnp.float32, -limit, limit)
        batch = x.shape[1]
        c0 = jnp.broadcast_to(in_c, (batch, in_c.shape[0]))

        def step(c, xt):
            ft = jax.nn.sigmoid(xt @ wf.T + c @ uf.T + bf)
            it = jax.nn.sigmoid(xt @ wi.T + c @ ui.T + bi)
            gt = jnp.tanh(xt @ wc.T + c @ uc.T + bc)
            c = ft * c + it * gt
            return (c, None)
        c_final, _ = lax.scan(step, c0, x)
        h = jnp.tanh(jnp.einsum('tbi,oi->tbo', x, wo) + c_final @ uo.T + bo)
        return h

    def _L1_xattn_ref(q, kv, Wq, Wk, Wv, Wo, bo):
        import jax, jax.numpy as jnp
        import numpy as np
        NUM_HEADS = 16
        HEAD_DIM = 64
        Q_DIM = 256
        KV_DIM = 128
        INNER = NUM_HEADS * HEAD_DIM
        B, N, _ = q.shape
        M = kv.shape[1]
        scale = HEAD_DIM ** (-0.5)
        qh = (q @ Wq).reshape(B, N, NUM_HEADS, HEAD_DIM).transpose(0, 2, 1, 3)
        kh = (kv @ Wk).reshape(B, M, NUM_HEADS, HEAD_DIM).transpose(0, 2, 1, 3)
        vh = (kv @ Wv).reshape(B, M, NUM_HEADS, HEAD_DIM).transpose(0, 2, 1, 3)
        scores = jnp.einsum('bhnd,bhmd->bhnm', qh, kh) * scale
        attn = jax.nn.softmax(scores, axis=-1)
        out = jnp.einsum('bhnm,bhmd->bhnd', attn, vh)
        out = out.transpose(0, 2, 1, 3).reshape(B, N, INNER)
        return out @ Wo + bo

    def _L1_ffn_ref(x, centroids, expert_biases, Ws_up, Ws_down, W_up, W_down):
        import jax, jax.numpy as jnp
        import numpy as np
        TOP_K = 8
        B, S, D = x.shape
        E = centroids.shape[0]
        T = B * S
        xf = x.reshape(T, D)
        shared = jax.nn.silu(xf @ Ws_up) @ Ws_down
        aff = xf @ centroids.T
        biased = aff + expert_biases
        _, idx = jax.lax.top_k(biased, TOP_K)
        sel = jnp.take_along_axis(aff, idx, axis=1)
        w = jax.nn.sigmoid(sel)
        w = w / (jnp.sum(w, axis=-1, keepdims=True) + 1e-08)
        cw = jnp.zeros((T, E), dtype=x.dtype).at[jnp.arange(T)[:, None], idx].add(w)
        h = jax.nn.silu(jnp.einsum('td,edf->etf', xf, W_up))
        y = jnp.einsum('etf,efd->etd', h, W_down)
        routed = jnp.einsum('etd,te->td', y, cw)
        return (shared + routed).reshape(B, S, D)
    x = x + jnp.tanh(g_xattn[0]) * _L0_xattn_ref(_layernorm(x, axis=-1), ctx_512, ctx_512, L0_xattn_Wq, L0_xattn_bq, L0_xattn_Wk, L0_xattn_bk, L0_xattn_Wv, L0_xattn_bv, L0_xattn_Wo, L0_xattn_bo)
    x = x + jnp.tanh(g_ffn[0]) * _L0_ffn_ref(_layernorm(x, axis=-1), L0_ffn_wf, L0_ffn_uf, L0_ffn_bf, L0_ffn_wi, L0_ffn_ui, L0_ffn_bi, L0_ffn_wc, L0_ffn_uc, L0_ffn_bc, L0_ffn_wo, L0_ffn_uo, L0_ffn_bo, L0_ffn_in_c)
    x = x + jnp.tanh(g_xattn[1]) * _L1_xattn_ref(_layernorm(x, axis=-1), ctx_512, L1_xattn_Wq, L1_xattn_Wk, L1_xattn_Wv, L1_xattn_Wo, L1_xattn_bo)
    x = x + jnp.tanh(g_ffn[1]) * _L1_ffn_ref(_layernorm(x, axis=-1), L1_ffn_centroids, L1_ffn_expert_biases, L1_ffn_Ws_up, L1_ffn_Ws_down, L1_ffn_W_up, L1_ffn_W_down)
    return x

_drawn_inputs = setup_inputs


def setup_inputs(seed=0):
    import zlib

    import numpy as np

    out = dict(_drawn_inputs(seed))
    spreads = {'g_ffn': (-1.0, 0.537),
     'L0_xattn_bq': (0.0, 0.321),
     'L0_xattn_bk': (0.0, 0.8),
     'L0_xattn_bv': (0.0, 0.1),
     'L0_xattn_bo': (0.0, 0.1),
     'L0_ffn_bf': (0.0, 0.52),
     'L0_ffn_bi': (0.0, 0.492),
     'L0_ffn_bc': (0.0, 0.1),
     'L0_ffn_bo': (0.0, 0.1),
     'L0_ffn_in_c': (0.0, 0.8),
     'L1_ffn_expert_biases': (0.0, 0.1)}
    factors = {'L1_xattn_bo': 4.172}
    for name, (base, spread) in spreads.items():
        noise = np.random.default_rng([zlib.crc32(name.encode()), seed]).standard_normal(out[name].shape)
        drawn = base * np.exp(spread * noise) if base else spread * noise
        out[name] = jnp.asarray(drawn.astype(out[name].dtype))
    for name, factor in factors.items():
        out[name] = (out[name] * factor).astype(out[name].dtype)
    return out
```

```python
from contextlib import ExitStack

import concourse.bass as bass
from concourse import mybir
from concourse.alu_op_type import AluOpType as ALU

F32 = mybir.dt.float32
ACT = mybir.ActivationFunctionType
AX = mybir.AxisListType.X

P = 128
LN_EPS = 1e-5
TOP_K = 8
GONE = -3.0e38
BANKS = 8
RING = 4
LEAD = 2
GH = 4

ORDER_A = [
    (1, "post", "wo"), (4, "post", "lnT"), (5, "post", "gates_fi"), (6, "post", "gate_g"), (7, "post", "h_in"),
    (8, "pre", "xT"), (9, "pre", "q"), (10, "pre", "ctxT"), (11, "pre", "k0"), (12, "pre", "k1"),
    (13, "pre", "v01"), (14, "pre", "v2"),
]
ORDER_C = [
    (2, "post", "ho3"), (3, "post", "wo"), (4, "pre", "xT"), (5, "pre", "q0"), (6, "own", "ho0"),
    (7, "post", "lnT"), (8, "post", "router"), (9, "pre", "q1"), (10, "own", "ho1"), (11, "pre", "q2"),
    (11, "pre", "ctxT"), (12, "pre", "q3"), (13, "post", "cwT"), (14, "own", "ho2"),
]


def wait(eng, sem, value):
    if isinstance(value, int) and value <= 0:
        return
    eng.wait_ge(sem, value)


def wait_apart(eng, sem, value, spare):
    wait(eng, sem, value)
    eng.tensor_copy(spare[:, 0:1], spare[:, 1:2])


class Uses:

    def __init__(self, order, n_seq):
        self.order, self.n_seq = order, n_seq
        self.n = {k: sum(x[1] == k for x in order) for k in ("pre", "post", "own")}

    def before(self, i, name):
        n, const = self.n, isinstance(i, int)
        if const and i < 0:
            base, has = 0, {"pre"}
        elif const and i == 0:
            base, has = n["pre"], {"pre", "own"}
        elif const and i == self.n_seq:
            base, has = self.n_seq * (n["pre"] + n["own"]) + (i - 1) * n["post"], {"post"}
        else:
            base = i * (n["pre"] + n["own"] + n["post"]) + (n["pre"] - n["post"])
            has = {"own", "post"} | ({"pre"} if not (const and i == self.n_seq - 1) else set())
        k = 0
        for _, kind, x in self.order:
            if x == name:
                return base + k
            k += kind in has
        raise KeyError(name)

    def out(self, j, name):
        if isinstance(j, int) and j < 0:
            return 0
        kind = next(k for _, k, x in self.order if x == name)
        return self.before(j + {"pre": -1, "post": 1, "own": 0}[kind], name) + 1

    def run(self, hooks, i, h, par, first=False, last=False):
        for slot, kind, name in self.order:
            if (h is not None and slot != h) or name not in hooks:
                continue
            if (kind == "post" and first) or (kind == "pre" and last):
                continue
            if h is None and kind != ("pre" if first else "post"):
                continue
            j = i + {"pre": 1, "post": -1, "own": 0}[kind]
            hooks[name](j, par if kind == "own" else 1 - par, self.before(i, name))


def walk(eng, n_seq, body):
    body(0, 0, True, False)
    body(1, 1, False, False)
    with eng.Fori(1, n_seq // 2 - 1) as pair:
        body(pair * 2, 0, False, False)
        body(pair * 2 + 1, 1, False, False)
    body(n_seq - 2, 0, False, False)
    body(n_seq - 1, 1, False, True)


def bcast(v, n, p=P):
    return v.rearrange("(o n) -> o n", o=1).to_broadcast([p, n])


def seq(a, j):
    return a[bass.ds(j, 1)].rearrange("o q d -> (o q) d")


def flat(a):
    return a.rearrange("p a b -> p (a b)")


def allocate(nc, es, t):
    def sb(name, shape):
        return es.enter_context(nc.sbuf_tensor(name, shape, F32))

    NB, NQ, D = t["x"].shape
    H = 16
    INNER = t["L1_xattn_Wq"].shape[1]
    E = t["L1_ffn_W_up"].shape[0]
    CC = D // P
    w = dict(
        ident=sb("ident", [P, P]),
        g_tanh=sb("g_tanh", [P, 4]),
        neg_half=sb("neg_half", [P, 1]),
        head_mask=sb("head_mask", [P, 8]),
        tgbo=[sb(f"tgbo{n}", [P, D]) for n in range(2)],
        cf=sb("cf", [P, D]),
        cenT=sb("cenT", [P, CC, E]),
        ebias=sb("ebias", [P, E]),
        mqk=sb("mqk", [P, CC, H, P]),
        wv1=sb("wv1", [P, INNER]),
        wo1=sb("wo1", [P, INNER // P, D]),
    )
    return w


def allocate_a(nc, es, t):
    def sb(name, shape):
        return es.enter_context(nc.sbuf_tensor(name, shape, F32))

    NB, NQ, D = t["x"].shape
    CC = D // P
    w = dict(
        wq0=sb("wq0", [P, CC, D]), wk0=sb("wk0", [P, D]), wv0=sb("wv0", [P, D]),
        wo0=sb("wo0", [P, 16 // GH, D]),
        bq0=sb("bq0", [P, CC]), bk0=sb("bk0", [P, CC]), bv0=sb("bv0", [P, 2 * D]),
        gate_bias=sb("gate_bias", [P, 3, CC]), bo_ffn=sb("bo_ffn", [P, D]),
        cT=sb("cT", [P, CC, NQ]),
    )
    for n in GATE_WEIGHTS:
        w[n + "T"] = sb(n + "T", [P, CC, D])
    return w


GATE_WEIGHTS = ["wf", "wi", "wc", "wo", "uf", "ui", "uc", "uo"]


def setup(nc, t, w, bank):
    NB, NQ, D = t["x"].shape
    H, CC = 16, D // P
    DK0 = D // H
    INNER = t["L1_xattn_Wq"].shape[1]
    DK1 = INNER // H
    PAIRS = INNER // P
    E = t["L1_ffn_W_up"].shape[0]
    with ExitStack() as es:
        def sb(name, shape):
            return es.enter_context(nc.sbuf_tensor(name, shape, F32))

        def sem(name):
            return es.enter_context(nc.semaphore(name))

        wq1, wk1 = sb("wq1", [P, CC, INNER]), sb("wk1", [P, INNER])
        wq1T, wk1T = sb("wq1T", [P, PAIRS, D]), sb("wk1T", [P, PAIRS, P])
        cen, bo_raw, g_raw = sb("cen", [E, D]), sb("bo_raw", [P, 2, D]), sb("g_raw", [P, 4])
        in_c, nat = sb("in_c", [P, CC]), sb("nat", [P, 2, CC, D])
        loaded, consts, wo0_zeroed = sem("loaded"), sem("consts"), sem("wo0_zeroed")
        g_ready, scaled = sem("g_ready"), sem("scaled")
        nat_in = [sem(f"nat_in{n}") for n in range(2)]
        written, evacuated, state = sem("set_written"), sem("set_evacuated"), sem("state_zeroed")

        chunked = "(c p) n -> p c n"
        column = "(c p) -> p c"
        loads = [
            (g_raw[:, 0:2], bcast(t["g_xattn"], 2)), (g_raw[:, 2:4], bcast(t["g_ffn"], 2)),
            (w["wq0"][:], t["L0_xattn_Wq"].rearrange(chunked, p=P)),
            (w["wk0"][:], t["L0_xattn_Wk"]), (w["wv0"][:], t["L0_xattn_Wv"]),
            (w["bv0"][:, 0:D], bcast(t["L0_xattn_bv"], D)), (w["bv0"][:, D:2 * D], bcast(t["L0_xattn_bv"], D)),
            (bo_raw[:, 0, :], bcast(t["L0_xattn_bo"], D)), (bo_raw[:, 1, :], bcast(t["L1_xattn_bo"], D)),
            (w["bo_ffn"][:], bcast(t["L0_ffn_bo"], D)), (w["ebias"][:], bcast(t["L1_ffn_expert_biases"], E)),
            (wq1[:], t["L1_xattn_Wq"].rearrange(chunked, p=P)),
            (wk1[:], t["L1_xattn_Wk"]), (w["wv1"][:], t["L1_xattn_Wv"]),
            (w["wo1"][:], t["L1_xattn_Wo"].rearrange(chunked, p=P)), (cen[:], t["L1_ffn_centroids"]),
        ]
        columns = [
            (w["bq0"], "L0_xattn_bq"), (w["bk0"], "L0_xattn_bk"), (w["gate_bias"][:, 0, :], "L0_ffn_bf"),
            (w["gate_bias"][:, 1, :], "L0_ffn_bi"), (w["gate_bias"][:, 2, :], "L0_ffn_bc"), (in_c, "L0_ffn_in_c"),
        ]
        wo0_rows = t["L0_xattn_Wo"].rearrange("(g j d) n -> j d g n", g=H // GH, j=GH)
        n_loads = len(loads) + CC * len(columns) + GH

        with nc.Block() as block:

            @block.sync
            def _(sp):
                for n, name in enumerate(GATE_WEIGHTS):
                    if n >= 2:
                        sp.wait_ge(written, n - 1)
                    sp.dma_start(nat[:, n % 2], t[f"L0_ffn_{name}"].rearrange(chunked, p=P)).then_inc(nat_in[n % 2], 16)
                    if n == 1:
                        for dst, src in loads:
                            sp.dma_start(dst, src).then_inc(loaded, 16)
                        for dst, name2 in columns:
                            for c in range(CC):
                                sp.dma_start(dst[:, c:c + 1], t[name2][c * P:(c + 1) * P].rearrange("(p o) -> p o", o=1)).then_inc(loaded, 16)
                        sp.wait_ge(wo0_zeroed, 1)
                        for j in range(GH):
                            sp.dma_start(w["wo0"][32 * j:32 * j + DK0, :, :], wo0_rows[j]).then_inc(loaded, 16)

            @block.gpsimd
            def _(pool):
                ident, mask = w["ident"], w["head_mask"]
                nc.gpsimd.memset(ident[:], 0.0).then_inc(consts, 1)
                nc.gpsimd.memset(mask[:], 1.0).then_inc(consts, 1)
                nc.gpsimd.memset(w["neg_half"][:], -0.5).then_inc(consts, 1)
                pool.wait_ge(consts, 3)
                nc.gpsimd.affine_select(out=ident[:], in_=ident[:], compare_op=ALU.not_equal, fill=1.0, base=0,
                                        pattern=[[-1, P]], channel_multiplier=1).then_inc(consts, 1)
                nc.gpsimd.affine_select(out=mask[:], in_=mask[:], compare_op=ALU.is_ge, fill=0.0, base=0,
                                        pattern=[[-DK0, 8]], channel_multiplier=1).then_inc(consts, 1)
                pool.wait_ge(consts, 5)
                nc.gpsimd.affine_select(out=mask[:], in_=mask[:], compare_op=ALU.is_ge, fill=0.0, base=DK0 - 1,
                                        pattern=[[DK0, 8]], channel_multiplier=-1).then_inc(consts, 1)

            @block.scalar
            def _(act):
                act.wait_ge(loaded, 16 * n_loads)
                nc.scalar.activation(w["g_tanh"][:], g_raw[:], ACT.Tanh).then_inc(g_ready, 1)

            @block.tensor
            def _(pe):
                used = [0]

                def start():
                    n = used[0]
                    used[0] += 1
                    if n >= BANKS:
                        pe.wait_ge(evacuated, n - BANKS + 1)
                    return bank[n % BANKS]

                ident = w["ident"]
                pe.wait_ge(consts, 6)
                for n in range(len(GATE_WEIGHTS)):
                    b = start()
                    pe.wait_ge(nat_in[n % 2], 16 * (n // 2 + 1))
                    for ic in range(CC):
                        for mc in range(CC):
                            mm = pe.transpose(b[:, ic * D + mc * P:ic * D + mc * P + P],
                                              nat[:, n % 2, mc, ic * P:(ic + 1) * P], ident[:])
                    mm.then_inc(written, 1)
                pe.wait_ge(loaded, 16 * n_loads)
                b = start()
                for ic in range(CC):
                    mm = pe.transpose(b[:, ic * E:(ic + 1) * E], cen[:, ic * P:(ic + 1) * P], ident[:E, :E])
                mm.then_inc(written, 1)
                for j in range(0, PAIRS, 2):
                    b = start()
                    for jj in range(2):
                        for cc in range(CC):
                            mm = pe.transpose(b[:, jj * D + cc * P:jj * D + cc * P + P],
                                              wq1[:, cc, (j + jj) * P:(j + jj + 1) * P], ident[:])
                    mm.then_inc(written, 1)
                for j in range(0, PAIRS, 4):
                    b = start()
                    for jj in range(4):
                        mm = pe.transpose(b[:, jj * P:(jj + 1) * P], wk1[:, (j + jj) * P:(j + jj + 1) * P], ident[:])
                    mm.then_inc(written, 1)
                pe.wait_ge(evacuated, used[0])
                for j in range(0, PAIRS, 2):
                    for hh in range(2):
                        b = start()
                        r = slice(DK1 * hh, DK1 * (hh + 1))
                        for cc in range(CC):
                            for jj in range(2):
                                mm = pe.matmul(b[:, (cc * 2 + jj) * P:(cc * 2 + jj + 1) * P],
                                               wq1T[r, j + jj, cc * P:(cc + 1) * P], wk1T[r, j + jj, :], start=True, stop=True)
                        mm.then_inc(written, 1)

            @block.vector
            def _(dve):
                nc.vector.memset(w["wo0"][:], 0.0).then_inc(wo0_zeroed, 1)
                nc.vector.memset(w["cT"][:], 0.0).then_inc(state, 1)
                used = [0]

                def evacuate(dst, n, parts=()):
                    b = bank[used[0] % BANKS]
                    used[0] += 1
                    dve.wait_ge(written, used[0])
                    src = b[:, 0:n]
                    if parts:
                        src = src.rearrange("p (c j d) -> p c j d", c=parts[0], j=parts[1])
                    nc.vector.tensor_copy(dst, src).then_inc(evacuated, 1)

                for name in GATE_WEIGHTS:
                    evacuate(flat(w[name + "T"][:]), CC * D)
                evacuate(flat(w["cenT"][:]), CC * E)
                for j in range(0, PAIRS, 2):
                    evacuate(flat(wq1T[:, j:j + 2, :]), 2 * D)
                for j in range(0, PAIRS, 4):
                    evacuate(flat(wk1T[:, j:j + 4, :]), 4 * P)
                for j in range(0, PAIRS, 2):
                    for hh in range(2):
                        evacuate(w["mqk"][:, :, 2 * j + hh:2 * j + hh + 3:2, :], 512, (CC, 2))
                dve.wait_ge(g_ready, 1)
                for n in range(2):
                    nc.vector.tensor_scalar(w["tgbo"][n][:], bo_raw[:, n, :], w["g_tanh"][:, n:n + 1], None, ALU.mult).then_inc(scaled, 1)
                nc.vector.tensor_scalar(w["gate_bias"][:, 0:2, :], w["gate_bias"][:, 0:2, :], 0.5, None, ALU.mult).then_inc(scaled, 1)
                nc.vector.tensor_scalar(w["bq0"][:], w["bq0"][:], float(DK0) ** -0.5, None, ALU.mult).then_inc(scaled, 1)
                dve.wait_ge(state, 1)
                for c in range(CC):
                    nc.vector.tensor_scalar(w["cT"][:, c, :], w["cT"][:, c, :], in_c[:, c:c + 1], None, ALU.add).then_inc(scaled, 1)
                dve.wait_ge(scaled, 4 + CC)


def attention_phase(nc, t, w, bank, x1pre_d, cwT_d, layer, XT=None, X3=None):
    A = layer == 0
    x, ctx = t["x"], t["ctx_512"]
    NB, NQ, D = x.shape
    NK = ctx.shape[1]
    H, CC = 16, D // P
    DK0, DK1 = D // H, t["L1_xattn_Wq"].shape[1] // H
    PAIRS = H * DK1 // P
    KP = 125
    KC = NK // KP
    E = t["L1_ffn_W_up"].shape[0]
    NG = H // GH
    assert D == 2 * P and ctx.shape[2] == P and KP * KC == NK and GH * NQ <= 512 and DK1 == 64
    uses = Uses(ORDER_A if A else ORDER_C, NB)
    s_bank, pt_bank, pv_bank, misc = bank[0:3], bank[3:5], bank[5:7], bank[7]
    S_OF = [h % 3 for h in range(H - 1)] + [1]
    ident, g_tanh = w["ident"], w["g_tanh"]
    N_ROUTER = 11

    def loads(j, par):
        return (j - par) * 8 + 16

    def scores_bank_last(h):
        before = [k for k in range(h) if S_OF[k] == S_OF[h]]
        return before[-1] if before else max(k for k in range(H) if S_OF[k] == S_OF[h]) - H

    with ExitStack() as es:
        def sb(name, shape):
            return es.enter_context(nc.sbuf_tensor(f"{name}_{layer}", shape, F32))

        def sem(name):
            return es.enter_context(nc.semaphore(f"{name}_{layer}"))

        qs = [sb(f"qs{n}", [P, H, NQ]) for n in range(2)]
        kT = [sb(f"kT{n}", [P, 2 if A else 1, NK]) for n in range(2)]
        ctxn = [sb(f"ctxn{n}", [KP, KC, P]) for n in range(2)]
        xt = [sb(f"xt{n}", [NQ, D if A else 2 * D]) for n in range(2)]
        xres = [sb(f"xres{n}", [NQ, D]) for n in range(2)]
        xln, x1ln = sb("xln", [NQ, D]), sb("x1ln", [NQ, D])
        xT, x1T = sb("xT", [P, CC, NQ]), sb("x1T", [P, CC, NQ])
        stage = sb("stage", [NQ, 2 * D])
        prob = sb("prob", [NQ, RING, NK + 1])
        pT = sb("pT", [KP, RING, KC * NQ])
        oT = [sb(f"oT{n}", [P, NG if A else PAIRS, NQ]) for n in range(2)]
        stats, spare = sb("stats", [NQ, 2, 16]), sb("spare", [NQ, 2])
        nmax, rsum, rinv = sb("nmax", [NQ, RING]), sb("rsum", [NQ, RING]), sb("rinv", [NQ, RING])
        if A:
            vals = [sb(f"vals{n}", [KP, KC, H, 32]) for n in range(2)]
            ctxT, qT = sb("ctxT", [P, NK]), sb("qT", [P, CC, NQ])
            gates, upd = sb("gates", [P, 3, CC, NQ]), sb("upd", [P, 3, CC * NQ])
        else:
            agg = [sb(f"agg{n}", [P, GH * NQ]) for n in range(2)]
            h_in, h_out = sb("h_in", [NQ, D]), sb("h_out", [NQ, D])
            rt, rts = sb("rt", [NQ, 8, E]), sb("rts", [NQ, 16])
            cwT = sb("cwT", [E, NQ])

        x_in, ctx_in = ([sem(f"{a}{n}") for n in range(2)] for a in ("x_in", "ctx_in"))
        stored = sem("stored")
        scored, maxed, exped, inverted, normed = sem("scored"), sem("maxed"), sem("exped"), sem("inverted"), sem("normed")
        turned, pT_ready, valued, group_out = sem("turned"), sem("pT_ready"), sem("valued"), sem("group_out")
        misc_full, misc_free = sem("misc_full"), sem("misc_free")
        x_stats, x_rstd, x_normed, xres_ready = sem("x_stats"), sem("x_rstd"), sem("x_normed"), sem("xres_ready")
        y_stats, y_rstd, y_normed = sem("y_stats"), sem("y_rstd"), sem("y_normed")
        spare_set = sem("spare_set")
        masked, updated, padded = sem("masked"), sem("updated"), sem("padded")
        h_in_ready, h_ready, x2_ready = sem("h_in_ready"), sem("h_ready"), sem("x2_ready")
        routed, sig_exp, kept = sem("routed"), sem("sig_exp"), sem("kept")

        with nc.Block() as block:

            @block.sync
            def _(sp):
                def load(j, par):
                    wait(sp, x_normed, j - 1)
                    wait(sp, xres_ready, j - 1)
                    sp.dma_start(xt[par][:], seq(x if A else x1pre_d, j)).then_inc(x_in[par], 16)
                    if A:
                        wait(sp, misc_free, uses.out(j - 2, "ctxT"))
                    else:
                        wait(sp, valued, H * (j - 1))
                    sp.dma_start(ctxn[par][:], ctx[bass.ds(j, 1)].rearrange("o (c p) d -> p (o c) d", p=KP)).then_inc(ctx_in[par], 16)

                def store(p):
                    if A:
                        sp.wait_ge(misc_free, uses.out(p, "h_in"))
                        sp.dma_start(seq(x1pre_d, p), stage[:]).then_inc(stored, 16)
                    else:
                        sp.wait_ge(misc_free, uses.out(p, "cwT"))
                        sp.dma_start(cwT_d[:, bass.ds(p * NQ, NQ)], cwT[:]).then_inc(stored, 16)

                load(0, 0)
                load(1, 1)

                def body(i, par, first, last):
                    if not first:
                        store(i - 1)
                    if not (isinstance(i, int) and i + 2 >= NB):
                        load(i + 2, par)

                walk(nc.sync, NB, body)
                store(NB - 1)
                sp.wait_ge(stored, 16 * NB)

            @block.tensor
            def _(pe):
                def scores(i, par, h):
                    wait(pe, exped, H * i + scores_bank_last(h) + 1)
                    if h == 0:
                        if A:
                            pe.wait_ge(masked, CC * (i + 1))
                            pe.wait_ge(misc_free, uses.out(i, "k1"))
                        else:
                            pe.wait_ge(misc_free, uses.out(i, "q3"))
                    pe.matmul(s_bank[S_OF[h]][:NQ, :NK], qs[par][:, h, :], kT[par][:, h // 8 if A else 0, :],
                              start=True, stop=True).then_inc(scored, 1)

                def turn(i, h):
                    wait(pe, pT_ready, H * i + h - 1)
                    pe.wait_ge(normed, H * i + h + 1)
                    for c in range(KC):
                        mm = pe.transpose(pt_bank[h % 2][:KP, c * NQ:(c + 1) * NQ],
                                          prob[:, h % RING, c * KP:(c + 1) * KP], ident[:NQ, :NQ])
                    mm.then_inc(turned, 1)

                def values(i, par, h):
                    g = h // GH
                    b = pv_bank[g % 2]
                    if h % GH == 0:
                        wait(pe, group_out, NG * i + g - 1)
                    if h == 0 and A:
                        pe.wait_ge(misc_free, uses.out(i, "v2"))
                    pe.wait_ge(pT_ready, H * i + h + 1)
                    for c in range(KC):
                        rhs = pT[:, h % RING, c * NQ:(c + 1) * NQ]
                        if A:
                            o = 32 * (h % GH)
                            mm = pe.matmul(b[o:o + 32, 0:NQ], vals[par][:, c, h, :], rhs, start=(c == 0), stop=(c == KC - 1))
                        else:
                            mm = pe.matmul(b[:, (h % GH) * NQ:(h % GH + 1) * NQ], ctxn[par][:, c, :], rhs,
                                           start=(c == 0), stop=(c == KC - 1))
                    mm.then_inc(valued, 1)

                def use(n):
                    wait(pe, misc_free, n)

                def transposed(src, ready):
                    def f(j, par, n):
                        use(n)
                        pe.wait_ge(ready, j + 1)
                        for c in range(CC):
                            mm = pe.transpose(misc[:, c * NQ:(c + 1) * NQ], src[:, c * P:(c + 1) * P], ident[:NQ, :NQ])
                        mm.then_inc(misc_full, 1)
                    return f

                def q(j, par, n):
                    use(n)
                    for m in range(CC):
                        for c in range(CC):
                            mm = pe.matmul(misc[:, m * NQ:(m + 1) * NQ], w["wq0"][:, c, m * P:(m + 1) * P], xT[:, c, :],
                                           start=(c == 0), stop=(c == CC - 1))
                    mm.then_inc(misc_full, 1)

                def ctx_transposed(j, par, n):
                    use(n)
                    pe.wait_ge(ctx_in[par], loads(j, par))
                    for c in range(KC):
                        mm = pe.transpose(misc[:, c * KP:(c + 1) * KP], ctxn[par][:, c, :], ident[:KP, :KP])
                    mm.then_inc(misc_full, 1)

                def k(m):
                    def f(j, par, n):
                        use(n)
                        pe.matmul(misc[:, :NK], w["wk0"][:, m * P:(m + 1) * P], ctxT[:], start=True, stop=True).then_inc(misc_full, 1)
                    return f

                def v(cs):
                    def f(j, par, n):
                        use(n)
                        for a, c in enumerate(cs):
                            mm = pe.matmul(misc[:KP, a * D:(a + 1) * D], ctxT[:, c * KP:(c + 1) * KP], w["wv0"][:],
                                           start=True, stop=True)
                        mm.then_inc(misc_full, 1)
                    return f

                def wo(p, par, n):
                    use(n)
                    if A:
                        pe.wait_ge(group_out, NG * (p + 1))
                    weights, parts = (w["wo0"], NG) if A else (w["wo1"], PAIRS)
                    for c in range(parts):
                        mm = pe.matmul(misc[:NQ, :D], oT[par][:, c, :], weights[:, c, :], start=(c == 0), stop=(c == parts - 1))
                    mm.then_inc(misc_full, 1)

                def gate(names):
                    def f(p, par, n):
                        use(n)
                        wait(pe, updated, 4 * p)
                        for a, g in enumerate(names):
                            for m in range(CC):
                                o = misc[:, (a * CC + m) * NQ:(a * CC + m + 1) * NQ]
                                for c in range(CC):
                                    pe.matmul(o, w[f"w{g}T"][:, c, m * P:(m + 1) * P], x1T[:, c, :], start=(c == 0), stop=False)
                                for c in range(CC):
                                    mm = pe.matmul(o, w[f"u{g}T"][:, c, m * P:(m + 1) * P], w["cT"][:, c, :], start=False, stop=(c == CC - 1))
                        mm.then_inc(misc_full, 1)
                    return f

                def h_into(p, par, n):
                    use(n)
                    for c in range(CC):
                        mm = pe.matmul(misc[:NQ, :D], x1T[:, c, :], w["woT"][:, c, :], start=(c == 0), stop=(c == CC - 1))
                    mm.then_inc(misc_full, 1)

                def qh(g):
                    def f(j, par, n):
                        use(n)
                        for a in range(GH):
                            for c in range(CC):
                                mm = pe.matmul(misc[:, a * NQ:(a + 1) * NQ], w["mqk"][:, c, g * GH + a, :], xT[:, c, :],
                                               start=(c == 0), stop=(c == CC - 1))
                        mm.then_inc(misc_full, 1)
                    return f

                def head_out(g):
                    def f(i, par, n):
                        use(n)
                        pe.wait_ge(group_out, NG * i + g + 1)
                        for a in range(GH):
                            h, o = g * GH + a, DK1 * (a % 2)
                            mm = pe.matmul(misc[o:o + DK1, (a // 2) * NQ:(a // 2 + 1) * NQ], w["wv1"][:, h * DK1:(h + 1) * DK1],
                                           agg[g % 2][:, a * NQ:(a + 1) * NQ], start=True, stop=True)
                        mm.then_inc(misc_full, 1)
                    return f

                def router(p, par, n):
                    use(n)
                    for c in range(CC):
                        mm = pe.matmul(misc[:NQ, :E], x1T[:, c, :], w["cenT"][:, c, :], start=(c == 0), stop=(c == CC - 1))
                    mm.then_inc(misc_full, 1)

                def weights_transposed(p, par, n):
                    use(n)
                    pe.wait_ge(routed, N_ROUTER * (p + 1))
                    pe.transpose(misc[:, :NQ], rt[:, 6:8, :].rearrange("q a e -> q (a e)"), ident[:NQ, :NQ]).then_inc(misc_full, 1)

                hooks = {"xT": transposed(xln, x_normed), "ctxT": ctx_transposed, "wo": wo, "lnT": transposed(x1ln, y_normed)}
                if A:
                    hooks |= {"q": q, "k0": k(0), "k1": k(1), "v01": v((0, 1)), "v2": v((2,)),
                              "gates_fi": gate("fi"), "gate_g": gate("c"), "h_in": h_into}
                else:
                    hooks |= {"router": router, "cwT": weights_transposed}
                    hooks |= {f"q{g}": qh(g) for g in range(NG)} | {f"ho{g}": head_out(g) for g in range(NG)}

                uses.run(hooks, -1, None, 1, first=True)
                if A:
                    pe.wait_ge(padded, 2)
                for h in range(LEAD):
                    scores(0, 0, h)

                def body(i, par, first, last):
                    for h in range(H):
                        if h + LEAD < H:
                            scores(i, par, h + LEAD)
                        elif not last:
                            scores(i + 1, 1 - par, h + LEAD - H)
                        turn(i, h)
                        if h:
                            values(i, par, h - 1)
                        elif not first:
                            values(i - 1, 1 - par, H - 1)
                        uses.run(hooks, i, h, par, first, last)

                walk(nc.tensor, NB, body)
                values(NB - 1, 1, H - 1)
                uses.run(hooks, NB, None, 0, last=True)
                if A:
                    pe.wait_ge(updated, 4 * NB)
                    use(uses.out(NB - 1, "h_in"))
                    for c in range(CC):
                        mm = pe.matmul(misc[:NQ, :D], w["cT"][:, c, :], w["uoT"][:, c, :], start=(c == 0), stop=(c == CC - 1))
                    mm.then_inc(misc_full, 1)

            def full(eng, n):
                eng.wait_ge(misc_full, n + 1)

            @block.scalar
            def _(act):
                def exponentials(i, h):
                    r = h % RING
                    act.wait_ge(maxed, H * i + h + 1)
                    wait(act, turned, H * i + h + 1 - RING)
                    nc.scalar.activation(prob[:, r, :NK], s_bank[S_OF[h]][:NQ, :NK], ACT.Exp, bias=nmax[:, r:r + 1],
                                         accum_out=rsum[:, r:r + 1]).then_inc(exped, 1)

                def keep_turned(i, h):
                    act.wait_ge(turned, H * i + h + 1)
                    wait(act, valued, H * i + h + 1 - RING)
                    nc.scalar.copy(pT[:, h % RING, :], pt_bank[h % 2][:KP, :KC * NQ]).then_inc(pT_ready, 1)

                def group(i, par, g):
                    act.wait_ge(valued, H * i + GH * (g + 1))
                    if A:
                        wait(act, misc_free, uses.out(i - 2, "wo"))
                        nc.scalar.copy(oT[par][:, g, :], pv_bank[g % 2][:, :NQ]).then_inc(group_out, 1)
                    else:
                        wait(act, misc_free, uses.out(i - 1, f"ho{g + 2}") if g < 2 else uses.out(i, f"ho{g - 2}"))
                        nc.scalar.copy(agg[g % 2][:], pv_bank[g % 2][:, :GH * NQ]).then_inc(group_out, 1)

                def q(j, par, n):
                    full(act, n)
                    wait(act, masked, CC * j)
                    for c in range(CC):
                        a = nc.scalar.activation(qT[:, c, :], misc[:, c * NQ:(c + 1) * NQ], ACT.Identity,
                                                 bias=w["bq0"][:, c:c + 1], scale=float(DK0) ** -0.5)
                    a.then_inc(misc_free, 1)

                def k(m):
                    def f(j, par, n):
                        full(act, n)
                        wait(act, scored, H * (j - 1))
                        nc.scalar.activation(kT[par][:, m, :], misc[:, :NK], ACT.Identity, bias=w["bk0"][:, m:m + 1]).then_inc(misc_free, 1)
                    return f

                def gates_fi(p, par, n):
                    full(act, n)
                    wait(act, updated, 4 * p)
                    for a in range(2):
                        for m in range(CC):
                            ins = nc.scalar.activation(gates[:, a, m, :], misc[:, (a * CC + m) * NQ:(a * CC + m + 1) * NQ],
                                                       ACT.Tanh, bias=w["gate_bias"][:, a, m:m + 1], scale=0.5)
                    ins.then_inc(misc_free, 1)

                def gate_g(p, par, n):
                    full(act, n)
                    for m in range(CC):
                        ins = nc.scalar.activation(gates[:, 2, m, :], misc[:, m * NQ:(m + 1) * NQ], ACT.Tanh,
                                                   bias=w["gate_bias"][:, 2, m:m + 1])
                    ins.then_inc(misc_free, 1)

                def h_into(p, par, n):
                    full(act, n)
                    wait(act, stored, 16 * p)
                    nc.scalar.copy(stage[:, D:2 * D], misc[:NQ, :D]).then_inc(misc_free, 1)

                def qh(g):
                    def f(j, par, n):
                        full(act, n)
                        wait(act, scored, H * (j - 1))
                        nc.scalar.activation(flat(qs[par][:, g * GH:(g + 1) * GH, :]), misc[:, :GH * NQ], ACT.Copy,
                                             scale=float(DK1) ** -0.5).then_inc(misc_free, 1)
                    return f

                def tanh_h(j):
                    act.wait_ge(h_in_ready, j + 1)
                    wait(act, x2_ready, j)
                    nc.scalar.activation(h_out[:], h_in[:], ACT.Tanh).then_inc(h_ready, 1)

                def sigmoid_exp(p):
                    act.wait_ge(routed, N_ROUTER * p + 1)
                    nc.scalar.activation(rt[:, 1, :], rt[:, 0, :], ACT.Exp, scale=-1.0).then_inc(sig_exp, 1)

                if A:
                    hooks = {"q": q, "k0": k(0), "k1": k(1), "gates_fi": gates_fi, "gate_g": gate_g, "h_in": h_into}
                else:
                    hooks = {f"q{g}": qh(g) for g in range(NG)}
                    hooks["router"] = lambda p, par, n: sigmoid_exp(p)
                    tanh_h(0)
                uses.run(hooks, -1, None, 1, first=True)
                for h in range(LEAD):
                    exponentials(0, h)

                def body(i, par, first, last):
                    for h in range(H):
                        if h + LEAD < H:
                            exponentials(i, h + LEAD)
                        elif not last:
                            exponentials(i + 1, h + LEAD - H)
                        keep_turned(i, h)
                        if h and h % GH == 0:
                            group(i, par, h // GH - 1)
                        if h == 0 and not first:
                            group(i - 1, 1 - par, NG - 1)
                        if not A and h == 0 and not last:
                            tanh_h(i + 1)
                        uses.run(hooks, i, h, par, first, last)

                walk(nc.scalar, NB, body)
                group(NB - 1, 1, NG - 1)
                uses.run(hooks, NB, None, 0, last=True)

            @block.vector
            def _(dve):
                def maximum(i, h):
                    r = h % RING
                    dve.wait_ge(scored, H * i + h + 1)
                    nc.vector.tensor_reduce(nmax[:, r:r + 1], s_bank[S_OF[h]][:NQ, :NK], AX, ALU.max, negate=True).then_inc(maxed, 1)

                def normalise(i, h):
                    r = h % RING
                    dve.wait_ge(exped, H * i + h + 1)
                    nc.vector.reciprocal(rinv[:, r:r + 1], rsum[:, r:r + 1]).then_inc(inverted, 1)
                    dve.wait_ge(inverted, H * i + h + 1)
                    nc.vector.tensor_scalar(prob[:, r, :NK], prob[:, r, :NK], rinv[:, r:r + 1], None, ALU.mult).then_inc(normed, 1)

                def norm(src, dst, st, j, counted, rstd, done):
                    nc.vector.bn_stats(st[:, 0:6], src).then_inc(counted, 1)
                    wait_apart(dve, counted, 3 * j + 1, spare)
                    nc.vector.bn_aggr(st[:, 6:8], st[:, 0:6]).then_inc(counted, 1)
                    dve.wait_ge(counted, 3 * j + 2)
                    nc.vector.tensor_scalar(st[:, 8:9], st[:, 7:8], LN_EPS, None, ALU.add).then_inc(counted, 1)
                    dve.wait_ge(rstd, j + 1)
                    nc.vector.tensor_scalar(dst[:], src, st[:, 6:7], st[:, 9:10], ALU.subtract, ALU.mult).then_inc(done, 1)

                def norm_x(j, par):
                    src = xt[par][:, 0:D]
                    dve.wait_ge(x_in[par], loads(j, par))
                    if not A:
                        wait(dve, h_ready, j)
                        nc.vector.tensor_tensor(h_in[:], xt[par][:, D:2 * D], w["cf"][:NQ, :], ALU.add).then_inc(h_in_ready, 1)
                        dve.wait_ge(h_ready, j + 1)
                        nc.vector.scalar_tensor_tensor(out=src, in0=h_out[:], scalar=g_tanh[:NQ, 2:3], in1=src,
                                                       op0=ALU.mult, op1=ALU.add).then_inc(x2_ready, 1)
                        dve.wait_ge(x2_ready, j + 1)
                    norm(src, xln, stats[:, 0, :], j, x_stats, x_rstd, x_normed)

                def norm_y(p):
                    dve.wait_ge(misc_free, uses.out(p, "wo"))
                    norm(stage[:, 0:D], x1ln, stats[:, 1, :], p, y_stats, y_rstd, y_normed)

                def keep_xT(j, par, n):
                    full(dve, n)
                    nc.vector.tensor_copy(flat(xT[:]), misc[:, :CC * NQ]).then_inc(misc_free, 1)

                def keep_ctxT(j, par, n):
                    full(dve, n)
                    if not A:
                        wait(dve, scored, H * (j - 1))
                    nc.vector.tensor_copy(ctxT[:] if A else kT[par][:, 0, :], misc[:, :NK]).then_inc(misc_free, 1)

                def keep_v(cs):
                    def f(j, par, n):
                        full(dve, n)
                        if isinstance(j, int) and j == 0:
                            dve.wait_ge(padded, 2)
                        wait(dve, valued, H * (j - 1))
                        for a, c in enumerate(cs):
                            ins = nc.vector.tensor_tensor(
                                vals[par][:, c, :, 0:DK0], misc[:KP, a * D:(a + 1) * D].rearrange("p (h d) -> p h d", h=H),
                                w["bv0"][:KP, 0:D].rearrange("p (h d) -> p h d", h=H), ALU.add)
                        ins.then_inc(misc_free, 1)
                    return f

                def residual(p, par, n):
                    full(dve, n)
                    dve.wait_ge(xres_ready, p + 1)
                    if A:
                        wait(dve, stored, 16 * p)
                    else:
                        wait(dve, kept, 2 * p)
                    nc.vector.scalar_tensor_tensor(out=stage[:, 0:D], in0=misc[:NQ, :D], scalar=g_tanh[:NQ, layer:layer + 1],
                                                   in1=xres[par][:], op0=ALU.mult, op1=ALU.add).then_inc(misc_free, 1)

                def keep_lnT(p, par, n):
                    full(dve, n)
                    if not A:
                        wait(dve, kept, 2 * p)
                    nc.vector.tensor_copy(flat(x1T[:]), misc[:, :CC * NQ]).then_inc(misc_free, 1)

                def update(p):
                    dve.wait_ge(misc_free, uses.out(p, "gate_g"))
                    f, i, g = (flat(gates[:, a]) for a in range(3))
                    c = flat(w["cT"][:])
                    nc.vector.scalar_tensor_tensor(out=upd[:, 0, :], in0=f, scalar=1.0, in1=c, op0=ALU.add, op1=ALU.mult).then_inc(updated, 1)
                    nc.vector.scalar_tensor_tensor(out=upd[:, 1, :], in0=i, scalar=1.0, in1=g, op0=ALU.add, op1=ALU.mult).then_inc(updated, 1)
                    dve.wait_ge(updated, 4 * p + 2)
                    nc.vector.tensor_tensor(upd[:, 2, :], upd[:, 0, :], upd[:, 1, :], ALU.add).then_inc(updated, 1)
                    dve.wait_ge(updated, 4 * p + 3)
                    nc.vector.tensor_scalar(c, upd[:, 2, :], 0.5, None, ALU.mult).then_inc(updated, 1)

                def keep_heads(g):
                    def f(i, par, n):
                        full(dve, n)
                        wait(dve, misc_free, uses.out(i - 2, "wo"))
                        nc.vector.tensor_copy(flat(oT[par][:, 2 * g:2 * g + 2, :]), misc[:, :2 * NQ]).then_inc(misc_free, 1)
                    return f

                def route(p):
                    done = [1]

                    def step(ins):
                        ins.then_inc(routed, 1)
                        done[0] += 1
                        wait_apart(dve, routed, N_ROUTER * p + done[0], spare)

                    dve.wait_ge(routed, N_ROUTER * p + 1)
                    step(nc.vector.tensor_tensor(rt[:, 2, :], rt[:, 0, :], w["ebias"][:NQ, :], ALU.add))
                    step(nc.vector.max(rts[:, 0:TOP_K], rt[:, 2, :]))
                    step(nc.vector.match_replace(rt[:, 3, :], rts[:, 0:TOP_K], rt[:, 2, :], GONE))
                    step(nc.vector.tensor_tensor(rt[:, 4, :], rt[:, 3, :], rt[:, 2, :], ALU.not_equal))
                    dve.wait_ge(sig_exp, p + 1)
                    step(nc.vector.tensor_scalar(rt[:, 5, :], rt[:, 1, :], 1.0, None, ALU.add))
                    step(nc.vector.reciprocal(rt[:, 7, :], rt[:, 5, :]))
                    step(nc.vector.scalar_tensor_tensor(out=rt[:, 5, :], in0=rt[:, 7, :], scalar=1.0, in1=rt[:, 4, :],
                                                        op0=ALU.mult, op1=ALU.mult, accum_out=rts[:, 8:9]))
                    step(nc.vector.tensor_scalar(rts[:, 9:10], rts[:, 8:9], 1e-8, None, ALU.add))
                    step(nc.vector.reciprocal(rts[:, 10:11], rts[:, 9:10]))
                    nc.vector.tensor_scalar(rt[:, 6, :], rt[:, 5, :], rts[:, 10:11], None, ALU.mult).then_inc(routed, 1)

                def keep_affinity(p, par, n):
                    full(dve, n)
                    wait(dve, misc_free, uses.out(p - 1, "cwT"))
                    nc.vector.tensor_copy(rt[:, 0, :], misc[:NQ, :E]).then_inc(misc_free, 1)
                    dve.wait_ge(misc_free, n + 1)
                    nc.vector.tensor_copy(rts[:, 11:12], rt[:, 0, 0:1]).then_inc(routed, 1)
                    route(p)

                def keep_cwT(p, par, n):
                    full(dve, n)
                    wait(dve, stored, 16 * p)
                    nc.vector.tensor_copy(cwT[:], misc[:E, :NQ]).then_inc(misc_free, 1)

                hooks = {"xT": keep_xT, "ctxT": keep_ctxT, "wo": residual, "lnT": keep_lnT}
                if A:
                    hooks |= {"v01": keep_v((0, 1)), "v2": keep_v((2,))}
                else:
                    hooks |= {"router": keep_affinity, "cwT": keep_cwT} | {f"ho{g}": keep_heads(g) for g in range(NG)}
                x_slot, y_slot = (5, 1) if A else (0, 3)

                nc.vector.memset(spare[:], 0.0).then_inc(spare_set, 1)
                dve.wait_ge(spare_set, 1)
                norm_x(0, 0)
                uses.run(hooks, -1, None, 1, first=True)
                for h in range(LEAD):
                    maximum(0, h)
                normalise(0, 0)

                def body(i, par, first, last):
                    for h in range(H):
                        if h + LEAD < H:
                            maximum(i, h + LEAD)
                        elif not last:
                            maximum(i + 1, h + LEAD - H)
                        if h + 1 < H:
                            normalise(i, h + 1)
                        elif not last:
                            normalise(i + 1, 0)
                        uses.run(hooks, i, h, par, first, last)
                        if h == y_slot and not first:
                            norm_y(i - 1)
                        if h == x_slot and not last:
                            norm_x(i + 1, 1 - par)
                        if A and h == 7 and not first:
                            update(i - 1)

                walk(nc.vector, NB, body)
                for _, kind, name in uses.order:
                    if kind == "post":
                        if name in hooks:
                            hooks[name](NB - 1, 1, uses.before(NB, name))
                        if name == "wo":
                            norm_y(NB - 1)
                        if name == "gate_g":
                            update(NB - 1)
                if A:
                    n = uses.out(NB - 1, "h_in")
                    full(dve, n)
                    nc.vector.tensor_tensor(w["cf"][:NQ, :], misc[:NQ, :D], w["bo_ffn"][:NQ, :], ALU.add).then_inc(misc_free, 1)
                    dve.wait_ge(misc_free, n + 1)

            @block.gpsimd
            def _(pool):
                def power(st, j, counted, rstd):
                    pool.wait_ge(counted, 3 * j + 3)
                    nc.gpsimd.tensor_tensor(st[:, 9:10], st[:, 8:9], w["neg_half"][:NQ, :], ALU.pow).then_inc(rstd, 1)

                def residual_x(j, par):
                    if A:
                        pool.wait_ge(x_in[par], loads(j, par))
                    else:
                        pool.wait_ge(x2_ready, j + 1)
                    wait(pool, misc_free, uses.out(j - 2, "wo"))
                    nc.gpsimd.tensor_tensor(xres[par][:], xt[par][:, 0:D], w["tgbo"][layer][:NQ, :], ALU.add).then_inc(xres_ready, 1)

                def mask(j, par):
                    pool.wait_ge(misc_free, uses.out(j, "q"))
                    wait(pool, scored, H * (j - 1))
                    for c in range(CC):
                        nc.gpsimd.tensor_tensor(qs[par][:, 8 * c:8 * c + 8, :],
                                                qT[:, c, :].unsqueeze(1).to_broadcast([P, 8, NQ]),
                                                w["head_mask"][:].unsqueeze(2).to_broadcast([P, 8, NQ]), ALU.mult).then_inc(masked, 1)

                def keep(p):
                    pool.wait_ge(misc_free, uses.out(p, "lnT"))
                    nc.gpsimd.tensor_copy(X3[:, bass.ds(p, 1), :].rearrange("q o d -> q (o d)"), stage[:, 0:D]).then_inc(kept, 1)
                    nc.gpsimd.tensor_copy(XT[:, :, bass.ds(p * NQ, NQ)], x1T[:]).then_inc(kept, 1)

                def before(j, par):
                    power(stats[:, 0, :], j, x_stats, x_rstd)
                    residual_x(j, par)
                    if A:
                        mask(j, par)

                def after(p):
                    power(stats[:, 1, :], p, y_stats, y_rstd)
                    if not A:
                        keep(p)

                if A:
                    for n in range(2):
                        nc.gpsimd.memset(vals[n][:], 0.0).then_inc(padded, 1)
                before(0, 0)

                def body(i, par, first, last):
                    if A and not first:
                        after(i - 1)
                    if not last:
                        before(i + 1, 1 - par)
                    if not A and not first:
                        after(i - 1)

                walk(nc.gpsimd, NB, body)
                after(NB - 1)


def expert_phase(nc, t, w, bank, cwT_d, XT, X3, out):
    NB, NQ, D = t["x"].shape
    CC = D // P
    E, _, F = t["L1_ffn_W_up"].shape
    TILES = 8
    GROUPS = NB // TILES
    TOK = TILES * NQ
    PARTS = 2
    TP = TOK // PARTS
    AHEAD = 4
    h_bank = [bank[0:2], bank[2:4]]
    acc = bank[4:8]
    assert TP <= 512 and F == P
    up, down = t["L1_ffn_W_up"], t["L1_ffn_W_down"]
    def passed(g, e):
        return PARTS * (g * STEPS + e + 2 - AHEAD - isinstance(e, int)) if g or not isinstance(e, int) else 0

    with ExitStack() as es:
        def sb(name, shape):
            return es.enter_context(nc.sbuf_tensor(name, shape, F32))

        def sem(name):
            return es.enter_context(nc.semaphore(name))

        wup = sb("wup", [P, AHEAD, CC, F])
        wdn = sb("wdn", [P, AHEAD, D])
        sup, sdn = sb("sup", [P, CC, F]), sb("sdn", [P, D])
        cw_row = sb("cw_row", [1, AHEAD, TOK])
        cw_all = sb("cw_all", [P, AHEAD, TOK])
        hid = sb("hid", [P, 2, PARTS, TP])
        hw = sb("hw", [P, 2, PARTS, TP])
        res = sb("res", [NQ, 2, D])
        spare = sb("spare", [1, 2])
        spare_set = sem("spare_set")
        shared_in = sem("shared_in")
        w_in = [sem(f"w_in{n}") for n in range(AHEAD)]
        spread, upped, silued, weighted, downed = sem("spread"), sem("upped"), sem("silued"), sem("weighted"), sem("downed")
        summed, written = sem("summed"), [sem(f"written{n}") for n in range(2)]
        STEPS = E + 1

        with nc.Block() as block:

            @block.sync
            def _(sp):
                sp.dma_start(sup[:], t["L1_ffn_Ws_up"].rearrange("(c p) f -> p c f", p=P)).then_inc(shared_in, 16)
                sp.dma_start(sdn[:], t["L1_ffn_Ws_down"]).then_inc(shared_in, 16)

                def store(g):
                    for n in range(g * TILES, (g + 1) * TILES):
                        sp.wait_ge(summed, n + 1)
                        sp.dma_start(out[n], res[:, n % 2, :]).then_inc(written[n % 2], 16)

                for g in range(GROUPS):
                    def load(e, b):
                        wait(sp, downed, passed(g, e))
                        sp.dma_start(wup[:, b], up[bass.ds(e, 1)].rearrange("o (c p) f -> p (o c) f", p=P)).then_inc(w_in[b], 16)
                        sp.dma_start(wdn[:, b, :], down[bass.ds(e, 1)].rearrange("o p d -> p (o d)")).then_inc(w_in[b], 16)
                        sp.dma_start(cw_row[:, b, :], cwT_d[bass.ds(e, 1), g * TOK:(g + 1) * TOK]).then_inc(w_in[b], 16)
                    for e in range(AHEAD):
                        load(e, e)
                    if g:
                        store(g - 1)
                    with nc.sync.Fori(1, E // AHEAD) as m:
                        for b in range(AHEAD):
                            load(m * AHEAD + b, b)
                store(GROUPS - 1)
                for n in range(2):
                    sp.wait_ge(written[n], 16 * (NB // 2))

            @block.gpsimd
            def _(pool):
                nc.gpsimd.memset(spare[:], 0.0).then_inc(spare_set, 1)
                pool.wait_ge(spare_set, 1)
                for g in range(GROUPS):
                    def expert(e, b):
                        pool.wait_ge(w_in[b], 48 * ((e - b) // AHEAD + g * (E // AHEAD) + 1) if isinstance(e, int)
                                     else 48 * (g * (E // AHEAD) + 1) + (48 // AHEAD) * (e - b))
                        wait(pool, weighted, passed(g, e))
                        wait(pool, spare_set, g * E + e + 1)
                        nc.gpsimd.tensor_tensor(spare[:, 0:1], spare[:, 1:2], spare[:, 1:2], ALU.add).then_inc(spare_set, 1)
                        nc.gpsimd.partition_broadcast(cw_all[:, b, :], cw_row[0:1, b, :]).then_inc(spread, 1)
                    for e in range(AHEAD):
                        expert(e, e)
                    with nc.gpsimd.Fori(1, E // AHEAD) as m:
                        for b in range(AHEAD):
                            expert(m * AHEAD + b, b)

            @block.tensor
            def _(pe):
                pe.wait_ge(shared_in, 32)
                for g in range(GROUPS):
                    def ups(s, par, weights):
                        for k in range(PARTS):
                            wait(pe, silued, PARTS * (g * STEPS + s - 2) + k + 1)
                            for c in range(CC):
                                mm = pe.matmul(h_bank[par][k][:, :TP], weights[:, c, :],
                                               XT[:, c, g * TOK + k * TP:g * TOK + (k + 1) * TP], start=(c == 0), stop=(c == CC - 1))
                            mm.then_inc(upped, 1)

                    def downs(s, par, weights, first, last):
                        for k in range(PARTS):
                            pe.wait_ge(weighted, PARTS * (g * STEPS + s) + k + 1)
                            for a in range(TILES // PARTS):
                                tile = k * (TILES // PARTS) + a
                                mm = pe.matmul(acc[tile // 2][:NQ, (tile % 2) * D:(tile % 2 + 1) * D],
                                               hw[:, par, k, a * NQ:(a + 1) * NQ], weights,
                                               start=(first and tile % 2 == 0), stop=last, skip_group_check=True)
                            mm.then_inc(downed, 1)

                    def arrived(e, b):
                        pe.wait_ge(w_in[b], 48 * ((e - b) // AHEAD + g * (E // AHEAD) + 1) if isinstance(e, int)
                                   else 48 * (g * (E // AHEAD) + 1) + (48 // AHEAD) * (e - b))

                    def step(e, b, last=False):
                        if not last:
                            nxt = (b + 1) % AHEAD
                            arrived(e + 1, nxt)
                            ups(e + 2, b % 2, wup[:, nxt])
                        downs(e + 1, (b + 1) % 2, wdn[:, b, :], False, last)

                    ups(0, 0, sup)
                    arrived(0, 0)
                    ups(1, 1, wup[:, 0])
                    if g:
                        pe.wait_ge(summed, TILES * g)
                    downs(0, 0, sdn[:], True, False)
                    with nc.tensor.Fori(0, E // AHEAD - 1) as m:
                        for b in range(AHEAD):
                            step(m * AHEAD + b, b)
                    for b in range(AHEAD):
                        step(E - AHEAD + b, b, last=(b == AHEAD - 1))

            def steps(eng, one):
                for g in range(GROUPS):
                    one(g, 0, 0, None)
                    for e in range(AHEAD):
                        one(g, e + 1, (e + 1) % 2, e)
                    with eng.Fori(1, E // AHEAD) as m:
                        for b in range(AHEAD):
                            one(g, m * AHEAD + b + 1, (b + 1) % 2, b)
                    yield g

            @block.scalar
            def _(act):
                def silu(g, s, par, b):
                    for k in range(PARTS):
                        act.wait_ge(upped, PARTS * (g * STEPS + s) + k + 1)
                        wait(act, weighted, PARTS * (g * STEPS + s - 2) + k + 1)
                        nc.scalar.activation(hid[:, par, k, :], h_bank[par][k][:, :TP], ACT.Silu).then_inc(silued, 1)

                for g in steps(nc.scalar, silu):
                    pass

            @block.vector
            def _(dve):
                def weight(g, s, par, b):
                    for k in range(PARTS):
                        dve.wait_ge(silued, PARTS * (g * STEPS + s) + k + 1)
                        wait(dve, downed, PARTS * (g * STEPS + s - 2) + k + 1)
                        if b is None:
                            nc.vector.tensor_copy(hw[:, par, k, :], hid[:, par, k, :]).then_inc(weighted, 1)
                        else:
                            dve.wait_ge(spread, g * E + s)
                            nc.vector.tensor_tensor(hw[:, par, k, :], hid[:, par, k, :], cw_all[:, b, k * TP:(k + 1) * TP],
                                                    ALU.mult).then_inc(weighted, 1)

                for g in steps(nc.vector, weight):
                    dve.wait_ge(downed, PARTS * STEPS * (g + 1))
                    for tile in range(TILES):
                        n = g * TILES + tile
                        wait(dve, written[n % 2], 16 * (n // 2))
                        nc.vector.scalar_tensor_tensor(out=res[:, n % 2, :], in0=acc[tile // 2][:NQ, (tile % 2) * D:(tile % 2 + 1) * D],
                                                       scalar=w["g_tanh"][:NQ, 3:4], in1=X3[:, n, :], op0=ALU.mult, op1=ALU.add).then_inc(summed, 1)


def build_kernel(nc, t, out):
    NB, NQ, D = t["x"].shape
    E = t["L1_ffn_W_up"].shape[0]
    x1pre_d = nc.dram_tensor("x1_and_h_in", [NB, NQ, 2 * D], F32).ap()
    cwT_d = nc.dram_tensor("expert_weights_T", [E, NB * NQ], F32).ap()
    with ExitStack() as es:
        bank = [es.enter_context(nc.psum_tensor(f"bank{n}", [P, 512], F32)) for n in range(BANKS)]
        w = allocate(nc, es, t)
        with ExitStack() as layer0:
            w |= allocate_a(nc, layer0, t)
            setup(nc, t, w, bank)
            attention_phase(nc, t, w, bank, x1pre_d, cwT_d, 0)
        XT = es.enter_context(nc.sbuf_tensor("XT", [P, D // P, NB * NQ], F32))
        X3 = es.enter_context(nc.sbuf_tensor("X3", [NQ, NB, D], F32))
        attention_phase(nc, t, w, bank, x1pre_d, cwT_d, 1, XT, X3)
        expert_phase(nc, t, w, bank, cwT_d, XT, X3, out)


_INS = ['x', 'ctx_512', 'g_xattn', 'g_ffn', 'L0_xattn_Wq', 'L0_xattn_bq', 'L0_xattn_Wk', 'L0_xattn_bk', 'L0_xattn_Wv',
        'L0_xattn_bv', 'L0_xattn_Wo', 'L0_xattn_bo', 'L0_ffn_wf', 'L0_ffn_uf', 'L0_ffn_bf', 'L0_ffn_wi', 'L0_ffn_ui',
        'L0_ffn_bi', 'L0_ffn_wc', 'L0_ffn_uc', 'L0_ffn_bc', 'L0_ffn_wo', 'L0_ffn_uo', 'L0_ffn_bo', 'L0_ffn_in_c',
        'L1_xattn_Wq', 'L1_xattn_Wk', 'L1_xattn_Wv', 'L1_xattn_Wo', 'L1_xattn_bo', 'L1_ffn_centroids',
        'L1_ffn_expert_biases', 'L1_ffn_Ws_up', 'L1_ffn_Ws_down', 'L1_ffn_W_up', 'L1_ffn_W_down']


def kernel(**inputs):
    import numpy as _np
    import concourse.bacc as _bacc
    from concourse import mybir as _mybir
    from concourse.bass_utils import run_bass_kernel_spmd as _run

    nc = _bacc.Bacc("TRN2", target_bir_lowering=False, num_devices=1)
    arrays, t = {}, {}
    for name in _INS:
        a = _np.ascontiguousarray(inputs[name])
        arrays[f"in_{name}_dram"] = a
        t[name] = nc.dram_tensor(f"in_{name}_dram", a.shape, _mybir.dt.from_np(a.dtype), kind="ExternalInput").ap()
    out = nc.dram_tensor("out_0_dram", inputs["x"].shape, _mybir.dt.float32, kind="ExternalOutput").ap()
    build_kernel(nc, t, out)
    r = _run(nc, [arrays], core_ids=[0])
    return r.results[0]["out_0_dram"]
```

```python
from contextlib import ExitStack

import concourse.bass as bass
from concourse import mybir
from concourse.alu_op_type import AluOpType as ALU

F32 = mybir.dt.float32
U32 = mybir.dt.uint32
I32 = mybir.dt.int32
ACT = mybir.ActivationFunctionType
AX = mybir.AxisListType.X

P = 128
LN_EPS = 1e-5
TOP_K = 8
GONE = -3.0e38
BANKS = 8
RING = 4
LEAD = 2
GH = 4

ORDER_A = [
    (1, "post", "wo"), (4, "post", "lnT"), (5, "post", "gates_fi"), (6, "post", "gate_g"), (7, "post", "h_in"),
    (8, "pre", "xT"), (9, "pre", "q"), (10, "pre", "ctxT"), (11, "pre", "k0"), (12, "pre", "k1"),
    (13, "pre", "v01"), (14, "pre", "v2"),
]
ORDER_C = [
    (2, "post", "ho3"), (3, "post", "wo"), (4, "pre", "xT"), (5, "pre", "q0"), (6, "own", "ho0"),
    (7, "post", "lnT"), (8, "post", "router"), (8, "post", "shared_up"), (9, "pre", "q1"), (10, "own", "ho1"),
    (11, "pre", "q2"), (11, "pre", "ctxT"), (12, "pre", "q3"), (13, "post", "rank"), (13, "post", "shared_down"),
    (14, "own", "ho2"),
]


def wait(eng, sem, value):
    if isinstance(value, int) and value <= 0:
        return
    eng.wait_ge(sem, value)


def wait_apart(eng, sem, value, spare):
    wait(eng, sem, value)
    eng.tensor_copy(spare[:, 0:1], spare[:, 1:2])


def pool_wait_apart(pool, sem, value, spare, n):
    wait(pool, sem, value)
    return pool.tensor_tensor(spare[:, 2 + n:3 + n], spare[:, 0:1], spare[:, 1:2], ALU.add)


class Uses:

    def __init__(self, order, n_seq):
        self.order, self.n_seq = order, n_seq
        self.n = {k: sum(x[1] == k for x in order) for k in ("pre", "post", "own")}

    def before(self, i, name):
        n, const = self.n, isinstance(i, int)
        if const and i < 0:
            base, has = 0, {"pre"}
        elif const and i == 0:
            base, has = n["pre"], {"pre", "own"}
        elif const and i == self.n_seq:
            base, has = self.n_seq * (n["pre"] + n["own"]) + (i - 1) * n["post"], {"post"}
        else:
            base = i * (n["pre"] + n["own"] + n["post"]) + (n["pre"] - n["post"])
            has = {"own", "post"} | ({"pre"} if not (const and i == self.n_seq - 1) else set())
        k = 0
        for _, kind, x in self.order:
            if x == name:
                return base + k
            k += kind in has
        raise KeyError(name)

    def out(self, j, name):
        if isinstance(j, int) and j < 0:
            return 0
        kind = next(k for _, k, x in self.order if x == name)
        return self.before(j + {"pre": -1, "post": 1, "own": 0}[kind], name) + 1

    def run(self, hooks, i, h, par, first=False, last=False):
        for slot, kind, name in self.order:
            if (h is not None and slot != h) or name not in hooks:
                continue
            if (kind == "post" and first) or (kind == "pre" and last):
                continue
            if h is None and kind != ("pre" if first else "post"):
                continue
            j = i + {"pre": 1, "post": -1, "own": 0}[kind]
            hooks[name](j, par if kind == "own" else 1 - par, self.before(i, name))


def walk(eng, n_seq, body):
    body(0, 0, True, False)
    body(1, 1, False, False)
    with eng.Fori(1, n_seq // 2 - 1) as pair:
        body(pair * 2, 0, False, False)
        body(pair * 2 + 1, 1, False, False)
    body(n_seq - 2, 0, False, False)
    body(n_seq - 1, 1, False, True)


def bcast(v, n, p=P):
    return v.rearrange("(o n) -> o n", o=1).to_broadcast([p, n])


def seq(a, j):
    return a[bass.ds(j, 1)].rearrange("o q d -> (o q) d")


def flat(a):
    return a.rearrange("p a b -> p (a b)")


def experts_shape(t):
    NB, NQ, _ = t["x"].shape
    E = t["L1_ffn_W_up"].shape[0]
    cap = -(-NB * NQ // P) * P + P
    tiles = (TOP_K * NB * NQ + (P - 1) * E) // P
    return cap, -(-tiles // 8) * 8


def allocate(nc, es, t):
    def sb(name, shape):
        return es.enter_context(nc.sbuf_tensor(name, shape, F32))

    NB, NQ, D = t["x"].shape
    H = 16
    INNER = t["L1_xattn_Wq"].shape[1]
    E = t["L1_ffn_W_up"].shape[0]
    CC = D // P
    w = dict(
        ident=sb("ident", [P, P]),
        g_tanh=sb("g_tanh", [P, 4]),
        neg_half=sb("neg_half", [P, 1]),
        head_mask=sb("head_mask", [P, 8]),
        tgbo=[sb(f"tgbo{n}", [P, D]) for n in range(2)],
        cf=sb("cf", [P, D]),
        cenT=sb("cenT", [P, CC, E]),
        ebias=sb("ebias", [P, E]),
        mqk=sb("mqk", [P, CC, H, P]),
        wv1=sb("wv1", [P, INNER]),
        wo1=sb("wo1", [P, INNER // P, D]),
        ones=sb("ones", [P, P]),
        earlier=sb("earlier", [P, P]),
        region=sb("region", [P, E]),
        chosen=sb("chosen", [NQ, E]),
        sup=sb("sup", [P, CC, P]), sdn=sb("sdn", [P, D]),
    )
    return w


def allocate_a(nc, es, t):
    def sb(name, shape):
        return es.enter_context(nc.sbuf_tensor(name, shape, F32))

    NB, NQ, D = t["x"].shape
    CC = D // P
    w = dict(
        wq0=sb("wq0", [P, CC, D]), wk0=sb("wk0", [P, D]), wv0=sb("wv0", [P, D]),
        wo0=sb("wo0", [P, 16 // GH, D]),
        bq0=sb("bq0", [P, CC]), bk0=sb("bk0", [P, CC]), bv0=sb("bv0", [P, 2 * D]),
        gate_bias=sb("gate_bias", [P, 3, CC]), bo_ffn=sb("bo_ffn", [P, D]),
        cT=sb("cT", [P, CC, NQ]),
    )
    for n in GATE_WEIGHTS:
        w[n + "T"] = sb(n + "T", [P, CC, D])
    return w


GATE_WEIGHTS = ["wf", "wi", "wc", "wo", "uf", "ui", "uc", "uo"]


def setup(nc, t, w, bank):
    NB, NQ, D = t["x"].shape
    H, CC = 16, D // P
    DK0 = D // H
    INNER = t["L1_xattn_Wq"].shape[1]
    DK1 = INNER // H
    PAIRS = INNER // P
    E = t["L1_ffn_W_up"].shape[0]
    with ExitStack() as es:
        def sb(name, shape):
            return es.enter_context(nc.sbuf_tensor(name, shape, F32))

        def sem(name):
            return es.enter_context(nc.semaphore(name))

        wq1, wk1 = sb("wq1", [P, CC, INNER]), sb("wk1", [P, INNER])
        wq1T, wk1T = sb("wq1T", [P, PAIRS, D]), sb("wk1T", [P, PAIRS, P])
        cen, bo_raw, g_raw = sb("cen", [E, D]), sb("bo_raw", [P, 2, D]), sb("g_raw", [P, 4])
        CAP, _ = experts_shape(t)
        region_i = es.enter_context(nc.sbuf_tensor("region_i", [P, E], I32))
        more = sem("more_consts")
        in_c, nat = sb("in_c", [P, CC]), sb("nat", [P, 2, CC, D])
        loaded, consts, wo0_zeroed = sem("loaded"), sem("consts"), sem("wo0_zeroed")
        g_ready, scaled = sem("g_ready"), sem("scaled")
        nat_in = [sem(f"nat_in{n}") for n in range(2)]
        written, evacuated, state = sem("set_written"), sem("set_evacuated"), sem("state_zeroed")

        chunked = "(c p) n -> p c n"
        column = "(c p) -> p c"
        loads = [
            (g_raw[:, 0:2], bcast(t["g_xattn"], 2)), (g_raw[:, 2:4], bcast(t["g_ffn"], 2)),
            (w["wq0"][:], t["L0_xattn_Wq"].rearrange(chunked, p=P)),
            (w["wk0"][:], t["L0_xattn_Wk"]), (w["wv0"][:], t["L0_xattn_Wv"]),
            (w["bv0"][:, 0:D], bcast(t["L0_xattn_bv"], D)), (w["bv0"][:, D:2 * D], bcast(t["L0_xattn_bv"], D)),
            (bo_raw[:, 0, :], bcast(t["L0_xattn_bo"], D)), (bo_raw[:, 1, :], bcast(t["L1_xattn_bo"], D)),
            (w["bo_ffn"][:], bcast(t["L0_ffn_bo"], D)), (w["ebias"][:], bcast(t["L1_ffn_expert_biases"], E)),
            (wq1[:], t["L1_xattn_Wq"].rearrange(chunked, p=P)),
            (wk1[:], t["L1_xattn_Wk"]), (w["wv1"][:], t["L1_xattn_Wv"]),
            (w["wo1"][:], t["L1_xattn_Wo"].rearrange(chunked, p=P)), (cen[:], t["L1_ffn_centroids"]),
            (w["sup"][:], t["L1_ffn_Ws_up"].rearrange(chunked, p=P)), (w["sdn"][:], t["L1_ffn_Ws_down"]),
        ]
        columns = [
            (w["bq0"], "L0_xattn_bq"), (w["bk0"], "L0_xattn_bk"), (w["gate_bias"][:, 0, :], "L0_ffn_bf"),
            (w["gate_bias"][:, 1, :], "L0_ffn_bi"), (w["gate_bias"][:, 2, :], "L0_ffn_bc"), (in_c, "L0_ffn_in_c"),
        ]
        wo0_rows = t["L0_xattn_Wo"].rearrange("(g j d) n -> j d g n", g=H // GH, j=GH)
        n_loads = len(loads) + CC * len(columns) + GH

        with nc.Block() as block:

            @block.sync
            def _(sp):
                for n, name in enumerate(GATE_WEIGHTS):
                    if n >= 2:
                        sp.wait_ge(written, n - 1)
                    sp.dma_start(nat[:, n % 2], t[f"L0_ffn_{name}"].rearrange(chunked, p=P)).then_inc(nat_in[n % 2], 16)
                    if n == 1:
                        for dst, src in loads:
                            sp.dma_start(dst, src).then_inc(loaded, 16)
                        for dst, name2 in columns:
                            for c in range(CC):
                                sp.dma_start(dst[:, c:c + 1], t[name2][c * P:(c + 1) * P].rearrange("(p o) -> p o", o=1)).then_inc(loaded, 16)
                        sp.wait_ge(wo0_zeroed, 1)
                        for j in range(GH):
                            sp.dma_start(w["wo0"][32 * j:32 * j + DK0, :, :], wo0_rows[j]).then_inc(loaded, 16)

            @block.gpsimd
            def _(pool):
                ident, mask = w["ident"], w["head_mask"]
                nc.gpsimd.memset(ident[:], 0.0).then_inc(consts, 1)
                nc.gpsimd.memset(mask[:], 1.0).then_inc(consts, 1)
                nc.gpsimd.memset(w["neg_half"][:], -0.5).then_inc(consts, 1)
                nc.gpsimd.memset(w["ones"][:], 1.0).then_inc(more, 1)
                nc.gpsimd.memset(w["earlier"][:], 1.0).then_inc(more, 1)
                nc.gpsimd.memset(w["chosen"][:], 0.0).then_inc(more, 1)
                nc.gpsimd.iota(region_i[:], pattern=[[CAP // 8, 64]], base=0, channel_multiplier=0).then_inc(more, 1)
                pool.wait_ge(consts, 3)
                nc.gpsimd.affine_select(out=ident[:], in_=ident[:], compare_op=ALU.not_equal, fill=1.0, base=0,
                                        pattern=[[-1, P]], channel_multiplier=1).then_inc(consts, 1)
                nc.gpsimd.affine_select(out=mask[:], in_=mask[:], compare_op=ALU.is_ge, fill=0.0, base=0,
                                        pattern=[[-DK0, 8]], channel_multiplier=1).then_inc(consts, 1)
                pool.wait_ge(consts, 5)
                nc.gpsimd.affine_select(out=mask[:], in_=mask[:], compare_op=ALU.is_ge, fill=0.0, base=DK0 - 1,
                                        pattern=[[DK0, 8]], channel_multiplier=-1).then_inc(consts, 1)
                pool.wait_ge(more, 4)
                nc.gpsimd.affine_select(out=w["earlier"][:], in_=w["earlier"][:], compare_op=ALU.is_gt, fill=0.0, base=0,
                                        pattern=[[1, P]], channel_multiplier=-1).then_inc(more, 1)

            @block.scalar
            def _(act):
                act.wait_ge(loaded, 16 * n_loads)
                nc.scalar.activation(w["g_tanh"][:], g_raw[:], ACT.Tanh).then_inc(g_ready, 1)

            @block.tensor
            def _(pe):
                used = [0]

                def start():
                    n = used[0]
                    used[0] += 1
                    if n >= BANKS:
                        pe.wait_ge(evacuated, n - BANKS + 1)
                    return bank[n % BANKS]

                ident = w["ident"]
                pe.wait_ge(consts, 6)
                for n in range(len(GATE_WEIGHTS)):
                    b = start()
                    pe.wait_ge(nat_in[n % 2], 16 * (n // 2 + 1))
                    for ic in range(CC):
                        for mc in range(CC):
                            mm = pe.transpose(b[:, ic * D + mc * P:ic * D + mc * P + P],
                                              nat[:, n % 2, mc, ic * P:(ic + 1) * P], ident[:])
                    mm.then_inc(written, 1)
                pe.wait_ge(loaded, 16 * n_loads)
                b = start()
                for ic in range(CC):
                    mm = pe.transpose(b[:, ic * E:(ic + 1) * E], cen[:, ic * P:(ic + 1) * P], ident[:E, :E])
                mm.then_inc(written, 1)
                for j in range(0, PAIRS, 2):
                    b = start()
                    for jj in range(2):
                        for cc in range(CC):
                            mm = pe.transpose(b[:, jj * D + cc * P:jj * D + cc * P + P],
                                              wq1[:, cc, (j + jj) * P:(j + jj + 1) * P], ident[:])
                    mm.then_inc(written, 1)
                for j in range(0, PAIRS, 4):
                    b = start()
                    for jj in range(4):
                        mm = pe.transpose(b[:, jj * P:(jj + 1) * P], wk1[:, (j + jj) * P:(j + jj + 1) * P], ident[:])
                    mm.then_inc(written, 1)
                pe.wait_ge(evacuated, used[0])
                for j in range(0, PAIRS, 2):
                    for hh in range(2):
                        b = start()
                        r = slice(DK1 * hh, DK1 * (hh + 1))
                        for cc in range(CC):
                            for jj in range(2):
                                mm = pe.matmul(b[:, (cc * 2 + jj) * P:(cc * 2 + jj + 1) * P],
                                               wq1T[r, j + jj, cc * P:(cc + 1) * P], wk1T[r, j + jj, :], start=True, stop=True)
                        mm.then_inc(written, 1)

            @block.vector
            def _(dve):
                nc.vector.memset(w["wo0"][:], 0.0).then_inc(wo0_zeroed, 1)
                nc.vector.memset(w["cT"][:], 0.0).then_inc(state, 1)
                used = [0]

                def evacuate(dst, n, parts=()):
                    b = bank[used[0] % BANKS]
                    used[0] += 1
                    dve.wait_ge(written, used[0])
                    src = b[:, 0:n]
                    if parts:
                        src = src.rearrange("p (c j d) -> p c j d", c=parts[0], j=parts[1])
                    nc.vector.tensor_copy(dst, src).then_inc(evacuated, 1)

                for name in GATE_WEIGHTS:
                    evacuate(flat(w[name + "T"][:]), CC * D)
                evacuate(flat(w["cenT"][:]), CC * E)
                for j in range(0, PAIRS, 2):
                    evacuate(flat(wq1T[:, j:j + 2, :]), 2 * D)
                for j in range(0, PAIRS, 4):
                    evacuate(flat(wk1T[:, j:j + 4, :]), 4 * P)
                for j in range(0, PAIRS, 2):
                    for hh in range(2):
                        evacuate(w["mqk"][:, :, 2 * j + hh:2 * j + hh + 3:2, :], 512, (CC, 2))
                dve.wait_ge(g_ready, 1)
                for n in range(2):
                    nc.vector.tensor_scalar(w["tgbo"][n][:], bo_raw[:, n, :], w["g_tanh"][:, n:n + 1], None, ALU.mult).then_inc(scaled, 1)
                nc.vector.tensor_scalar(w["gate_bias"][:, 0:2, :], w["gate_bias"][:, 0:2, :], 0.5, None, ALU.mult).then_inc(scaled, 1)
                nc.vector.tensor_scalar(w["bq0"][:], w["bq0"][:], float(DK0) ** -0.5, None, ALU.mult).then_inc(scaled, 1)
                dve.wait_ge(state, 1)
                for c in range(CC):
                    nc.vector.tensor_scalar(w["cT"][:, c, :], w["cT"][:, c, :], in_c[:, c:c + 1], None, ALU.add).then_inc(scaled, 1)
                dve.wait_ge(more, 5)
                nc.vector.tensor_scalar(w["region"][:], region_i[:], 8.0, 1.0, ALU.mult, ALU.add).then_inc(scaled, 1)
                dve.wait_ge(scaled, 5 + CC)


def attention_phase(nc, t, w, bank, x1pre_d, layer, rows_d=None, X3=None, wdn=None):
    A = layer == 0
    x, ctx = t["x"], t["ctx_512"]
    NB, NQ, D = x.shape
    NK = ctx.shape[1]
    H, CC = 16, D // P
    DK0, DK1 = D // H, t["L1_xattn_Wq"].shape[1] // H
    PAIRS = H * DK1 // P
    KP = 125
    KC = NK // KP
    E = t["L1_ffn_W_up"].shape[0]
    NG = H // GH
    assert D == 2 * P and ctx.shape[2] == P and KP * KC == NK and GH * NQ <= 512 and DK1 == 64
    uses = Uses(ORDER_A if A else ORDER_C, NB)
    s_bank, pt_bank, pv_bank, misc = bank[0:3], bank[3:5], bank[5:7], bank[7]
    S_OF = [h % 3 for h in range(H - 1)] + [1]
    ident, g_tanh = w["ident"], w["g_tanh"]
    N_ROUTER = 11
    N_PLACED = 5 + TOP_K

    def loads(j, par):
        return (j - par) * 8 + 16

    def scores_bank_last(h):
        before = [k for k in range(h) if S_OF[k] == S_OF[h]]
        return before[-1] if before else max(k for k in range(H) if S_OF[k] == S_OF[h]) - H

    with ExitStack() as es:
        def sb(name, shape):
            return es.enter_context(nc.sbuf_tensor(f"{name}_{layer}", shape, F32))

        def sem(name):
            return es.enter_context(nc.semaphore(f"{name}_{layer}"))

        qs = [sb(f"qs{n}", [P, H, NQ]) for n in range(2)]
        kT = [sb(f"kT{n}", [P, 2 if A else 1, NK]) for n in range(2)]
        ctxn = [sb(f"ctxn{n}", [KP, KC, P]) for n in range(2)]
        xt = [sb(f"xt{n}", [NQ, D if A else 2 * D]) for n in range(2)]
        xres = [sb(f"xres{n}", [NQ, D]) for n in range(2)]
        xln, x1ln = sb("xln", [NQ, D]), sb("x1ln", [NQ, D])
        xT, x1T = sb("xT", [P, CC, NQ]), sb("x1T", [P, CC, NQ])
        stage = sb("stage", [NQ, 2 * D])
        prob = sb("prob", [NQ, RING, NK + 1])
        pT = sb("pT", [KP, RING, KC * NQ])
        oT = [sb(f"oT{n}", [P, NG if A else PAIRS, NQ]) for n in range(2)]
        stats, spare = sb("stats", [NQ, 2, 16]), sb("spare", [NQ, 2])
        nmax, rsum, rinv = sb("nmax", [NQ, RING]), sb("rsum", [NQ, RING]), sb("rinv", [NQ, RING])
        if A:
            vals = [sb(f"vals{n}", [KP, KC, H, 32]) for n in range(2)]
            ctxT, qT = sb("ctxT", [P, NK]), sb("qT", [P, CC, NQ])
            gates, upd = sb("gates", [P, 3, CC, NQ]), sb("upd", [P, 3, CC * NQ])
        else:
            agg = [sb(f"agg{n}", [P, GH * NQ]) for n in range(2)]
            h_in, h_out = sb("h_in", [NQ, D]), sb("h_out", [NQ, D])
            rt, rts = sb("rt", [NQ, 8, E]), sb("rts", [NQ, 16])
            z, sig, hs = sb("z", [P, NQ]), sb("sig", [P, 2, NQ]), sb("hs", [P, NQ])
            placing, w8 = sb("placing", [NQ, 2 + TOP_K, E]), sb("w8", [NQ, 2 * TOP_K])
            slot_w = sb("slot_w", [NQ, TOP_K])
            ids = es.enter_context(nc.sbuf_tensor("ids", [NQ, TOP_K], U32))
            pool_spare = sb("pool_spare", [NQ, 7])
            numbers = es.enter_context(nc.sbuf_tensor("numbers", [NQ, TOP_K], I32))
            pool_spare_set = sem("pool_spare_set")
            rows = sb("rows", [NQ, TOP_K, D + 2])

        x_in, ctx_in = ([sem(f"{a}{n}") for n in range(2)] for a in ("x_in", "ctx_in"))
        stored = sem("stored")
        scored, maxed, exped, inverted, normed = sem("scored"), sem("maxed"), sem("exped"), sem("inverted"), sem("normed")
        turned, pT_ready, valued, group_out = sem("turned"), sem("pT_ready"), sem("valued"), sem("group_out")
        misc_full, misc_free = sem("misc_full"), sem("misc_free")
        x_stats, x_rstd, x_normed, xres_ready = sem("x_stats"), sem("x_rstd"), sem("x_normed"), sem("xres_ready")
        y_stats, y_rstd, y_normed = sem("y_stats"), sem("y_rstd"), sem("y_normed")
        spare_set = sem("spare_set")
        masked, updated, padded = sem("masked"), sem("updated"), sem("padded")
        h_in_ready, h_ready, x2_ready = sem("h_in_ready"), sem("h_ready"), sem("x2_ready")
        routed, sig_exp, kept = sem("routed"), sem("sig_exp"), sem("kept")
        placed, scattered, shared, shared_exp = sem("placed"), sem("scattered"), sem("shared"), sem("shared_exp")
        wdn_in, numbered, renumbered, weighted = sem("wdn_in"), sem("numbered"), sem("renumbered"), sem("weighted")

        with nc.Block() as block:

            @block.sync
            def _(sp):
                def load(j, par):
                    wait(sp, x_normed, j - 1)
                    wait(sp, xres_ready, j - 1)
                    sp.dma_start(xt[par][:], seq(x if A else x1pre_d, j)).then_inc(x_in[par], 16)
                    if A:
                        wait(sp, misc_free, uses.out(j - 2, "ctxT"))
                    else:
                        wait(sp, valued, H * (j - 1))
                    sp.dma_start(ctxn[par][:], ctx[bass.ds(j, 1)].rearrange("o (c p) d -> p (o c) d", p=KP)).then_inc(ctx_in[par], 16)

                def store(p):
                    sp.wait_ge(misc_free, uses.out(p, "h_in"))
                    sp.dma_start(seq(x1pre_d, p), stage[:]).then_inc(stored, 16)

                load(0, 0)
                load(1, 1)
                if not A:
                    for e in range(0, E, 8):
                        sp.dma_start(wdn[:, e:e + 8, :], t["L1_ffn_W_down"][e:e + 8].rearrange("e p d -> p e d")).then_inc(wdn_in, 16)

                def body(i, par, first, last):
                    if A and not first:
                        store(i - 1)
                    if not (isinstance(i, int) and i + 2 >= NB):
                        load(i + 2, par)

                walk(nc.sync, NB, body)
                if A:
                    store(NB - 1)
                    sp.wait_ge(stored, 16 * NB)
                else:
                    sp.wait_ge(wdn_in, 16 * (E // 8))

            @block.tensor
            def _(pe):
                def scores(i, par, h):
                    wait(pe, exped, H * i + scores_bank_last(h) + 1)
                    if h == 0:
                        if A:
                            pe.wait_ge(masked, CC * (i + 1))
                            pe.wait_ge(misc_free, uses.out(i, "k1"))
                        else:
                            pe.wait_ge(misc_free, uses.out(i, "q3"))
                    pe.matmul(s_bank[S_OF[h]][:NQ, :NK], qs[par][:, h, :], kT[par][:, h // 8 if A else 0, :],
                              start=True, stop=True).then_inc(scored, 1)

                def turn(i, h):
                    wait(pe, pT_ready, H * i + h - 1)
                    pe.wait_ge(normed, H * i + h + 1)
                    for c in range(KC):
                        mm = pe.transpose(pt_bank[h % 2][:KP, c * NQ:(c + 1) * NQ],
                                          prob[:, h % RING, c * KP:(c + 1) * KP], ident[:NQ, :NQ])
                    mm.then_inc(turned, 1)

                def values(i, par, h):
                    g = h // GH
                    b = pv_bank[g % 2]
                    if h % GH == 0:
                        wait(pe, group_out, NG * i + g - 1)
                    if h == 0 and A:
                        pe.wait_ge(misc_free, uses.out(i, "v2"))
                    pe.wait_ge(pT_ready, H * i + h + 1)
                    for c in range(KC):
                        rhs = pT[:, h % RING, c * NQ:(c + 1) * NQ]
                        if A:
                            o = 32 * (h % GH)
                            mm = pe.matmul(b[o:o + 32, 0:NQ], vals[par][:, c, h, :], rhs, start=(c == 0), stop=(c == KC - 1))
                        else:
                            mm = pe.matmul(b[:, (h % GH) * NQ:(h % GH + 1) * NQ], ctxn[par][:, c, :], rhs,
                                           start=(c == 0), stop=(c == KC - 1))
                    mm.then_inc(valued, 1)

                def use(n):
                    wait(pe, misc_free, n)

                def transposed(src, ready):
                    def f(j, par, n):
                        use(n)
                        pe.wait_ge(ready, j + 1)
                        for c in range(CC):
                            mm = pe.transpose(misc[:, c * NQ:(c + 1) * NQ], src[:, c * P:(c + 1) * P], ident[:NQ, :NQ])
                        mm.then_inc(misc_full, 1)
                    return f

                def q(j, par, n):
                    use(n)
                    for m in range(CC):
                        for c in range(CC):
                            mm = pe.matmul(misc[:, m * NQ:(m + 1) * NQ], w["wq0"][:, c, m * P:(m + 1) * P], xT[:, c, :],
                                           start=(c == 0), stop=(c == CC - 1))
                    mm.then_inc(misc_full, 1)

                def ctx_transposed(j, par, n):
                    use(n)
                    pe.wait_ge(ctx_in[par], loads(j, par))
                    for c in range(KC):
                        mm = pe.transpose(misc[:, c * KP:(c + 1) * KP], ctxn[par][:, c, :], ident[:KP, :KP])
                    mm.then_inc(misc_full, 1)

                def k(m):
                    def f(j, par, n):
                        use(n)
                        pe.matmul(misc[:, :NK], w["wk0"][:, m * P:(m + 1) * P], ctxT[:], start=True, stop=True).then_inc(misc_full, 1)
                    return f

                def v(cs):
                    def f(j, par, n):
                        use(n)
                        for a, c in enumerate(cs):
                            mm = pe.matmul(misc[:KP, a * D:(a + 1) * D], ctxT[:, c * KP:(c + 1) * KP], w["wv0"][:],
                                           start=True, stop=True)
                        mm.then_inc(misc_full, 1)
                    return f

                def wo(p, par, n):
                    use(n)
                    if A:
                        pe.wait_ge(group_out, NG * (p + 1))
                    weights, parts = (w["wo0"], NG) if A else (w["wo1"], PAIRS)
                    for c in range(parts):
                        mm = pe.matmul(misc[:NQ, :D], oT[par][:, c, :], weights[:, c, :], start=(c == 0), stop=(c == parts - 1))
                    mm.then_inc(misc_full, 1)

                def gate(names):
                    def f(p, par, n):
                        use(n)
                        wait(pe, updated, 4 * p)
                        for a, g in enumerate(names):
                            for m in range(CC):
                                o = misc[:, (a * CC + m) * NQ:(a * CC + m + 1) * NQ]
                                for c in range(CC):
                                    pe.matmul(o, w[f"w{g}T"][:, c, m * P:(m + 1) * P], x1T[:, c, :], start=(c == 0), stop=False)
                                for c in range(CC):
                                    mm = pe.matmul(o, w[f"u{g}T"][:, c, m * P:(m + 1) * P], w["cT"][:, c, :], start=False, stop=(c == CC - 1))
                        mm.then_inc(misc_full, 1)
                    return f

                def h_into(p, par, n):
                    use(n)
                    for c in range(CC):
                        mm = pe.matmul(misc[:NQ, :D], x1T[:, c, :], w["woT"][:, c, :], start=(c == 0), stop=(c == CC - 1))
                    mm.then_inc(misc_full, 1)

                def qh(g):
                    def f(j, par, n):
                        use(n)
                        for a in range(GH):
                            for c in range(CC):
                                mm = pe.matmul(misc[:, a * NQ:(a + 1) * NQ], w["mqk"][:, c, g * GH + a, :], xT[:, c, :],
                                               start=(c == 0), stop=(c == CC - 1))
                        mm.then_inc(misc_full, 1)
                    return f

                def head_out(g):
                    def f(i, par, n):
                        use(n)
                        pe.wait_ge(group_out, NG * i + g + 1)
                        for a in range(GH):
                            h, o = g * GH + a, DK1 * (a % 2)
                            mm = pe.matmul(misc[o:o + DK1, (a // 2) * NQ:(a // 2 + 1) * NQ], w["wv1"][:, h * DK1:(h + 1) * DK1],
                                           agg[g % 2][:, a * NQ:(a + 1) * NQ], start=True, stop=True)
                        mm.then_inc(misc_full, 1)
                    return f

                def router(p, par, n):
                    use(n)
                    for c in range(CC):
                        mm = pe.matmul(misc[:NQ, :E], x1T[:, c, :], w["cenT"][:, c, :], start=(c == 0), stop=(c == CC - 1))
                    mm.then_inc(misc_full, 1)

                def rank(p, par, n):
                    use(n)
                    pe.wait_ge(routed, N_ROUTER * (p + 1))
                    wait(pe, placed, N_PLACED * p)
                    pe.matmul(misc[:NQ, :E], w["earlier"][:NQ, :NQ], rt[:, 4, :], start=True, stop=False)
                    pe.matmul(misc[:NQ, :E], w["ones"][:NQ, :NQ], w["chosen"][:], start=False, stop=True).then_inc(misc_full, 1)

                def shared_up(p, par, n):
                    use(n)
                    for c in range(CC):
                        mm = pe.matmul(misc[:, :NQ], w["sup"][:, c, :], x1T[:, c, :], start=(c == 0), stop=(c == CC - 1))
                    mm.then_inc(misc_full, 1)

                def shared_down(p, par, n):
                    use(n)
                    pe.wait_ge(shared, 3 * (p + 1))
                    pe.matmul(misc[:NQ, :D], hs[:], w["sdn"][:], start=True, stop=True).then_inc(misc_full, 1)

                hooks = {"xT": transposed(xln, x_normed), "ctxT": ctx_transposed, "wo": wo, "lnT": transposed(x1ln, y_normed)}
                if A:
                    hooks |= {"q": q, "k0": k(0), "k1": k(1), "v01": v((0, 1)), "v2": v((2,)),
                              "gates_fi": gate("fi"), "gate_g": gate("c"), "h_in": h_into}
                else:
                    hooks |= {"router": router, "rank": rank, "shared_up": shared_up, "shared_down": shared_down}
                    hooks |= {f"q{g}": qh(g) for g in range(NG)} | {f"ho{g}": head_out(g) for g in range(NG)}

                uses.run(hooks, -1, None, 1, first=True)
                if A:
                    pe.wait_ge(padded, 2)
                for h in range(LEAD):
                    scores(0, 0, h)

                def body(i, par, first, last):
                    for h in range(H):
                        if h + LEAD < H:
                            scores(i, par, h + LEAD)
                        elif not last:
                            scores(i + 1, 1 - par, h + LEAD - H)
                        turn(i, h)
                        if h:
                            values(i, par, h - 1)
                        elif not first:
                            values(i - 1, 1 - par, H - 1)
                        uses.run(hooks, i, h, par, first, last)

                walk(nc.tensor, NB, body)
                values(NB - 1, 1, H - 1)
                uses.run(hooks, NB, None, 0, last=True)
                if A:
                    pe.wait_ge(updated, 4 * NB)
                    use(uses.out(NB - 1, "h_in"))
                    for c in range(CC):
                        mm = pe.matmul(misc[:NQ, :D], w["cT"][:, c, :], w["uoT"][:, c, :], start=(c == 0), stop=(c == CC - 1))
                    mm.then_inc(misc_full, 1)

            def full(eng, n):
                eng.wait_ge(misc_full, n + 1)

            @block.scalar
            def _(act):
                def exponentials(i, h):
                    r = h % RING
                    act.wait_ge(maxed, H * i + h + 1)
                    wait(act, turned, H * i + h + 1 - RING)
                    nc.scalar.activation(prob[:, r, :NK], s_bank[S_OF[h]][:NQ, :NK], ACT.Exp, bias=nmax[:, r:r + 1],
                                         accum_out=rsum[:, r:r + 1]).then_inc(exped, 1)

                def keep_turned(i, h):
                    act.wait_ge(turned, H * i + h + 1)
                    wait(act, valued, H * i + h + 1 - RING)
                    nc.scalar.copy(pT[:, h % RING, :], pt_bank[h % 2][:KP, :KC * NQ]).then_inc(pT_ready, 1)

                def group(i, par, g):
                    act.wait_ge(valued, H * i + GH * (g + 1))
                    if A:
                        wait(act, misc_free, uses.out(i - 2, "wo"))
                        nc.scalar.copy(oT[par][:, g, :], pv_bank[g % 2][:, :NQ]).then_inc(group_out, 1)
                    else:
                        wait(act, misc_free, uses.out(i - 1, f"ho{g + 2}") if g < 2 else uses.out(i, f"ho{g - 2}"))
                        nc.scalar.copy(agg[g % 2][:], pv_bank[g % 2][:, :GH * NQ]).then_inc(group_out, 1)

                def q(j, par, n):
                    full(act, n)
                    wait(act, masked, CC * j)
                    for c in range(CC):
                        a = nc.scalar.activation(qT[:, c, :], misc[:, c * NQ:(c + 1) * NQ], ACT.Identity,
                                                 bias=w["bq0"][:, c:c + 1], scale=float(DK0) ** -0.5)
                    a.then_inc(misc_free, 1)

                def k(m):
                    def f(j, par, n):
                        full(act, n)
                        wait(act, scored, H * (j - 1))
                        nc.scalar.activation(kT[par][:, m, :], misc[:, :NK], ACT.Identity, bias=w["bk0"][:, m:m + 1]).then_inc(misc_free, 1)
                    return f

                def gates_fi(p, par, n):
                    full(act, n)
                    wait(act, updated, 4 * p)
                    for a in range(2):
                        for m in range(CC):
                            ins = nc.scalar.activation(gates[:, a, m, :], misc[:, (a * CC + m) * NQ:(a * CC + m + 1) * NQ],
                                                       ACT.Tanh, bias=w["gate_bias"][:, a, m:m + 1], scale=0.5)
                    ins.then_inc(misc_free, 1)

                def gate_g(p, par, n):
                    full(act, n)
                    for m in range(CC):
                        ins = nc.scalar.activation(gates[:, 2, m, :], misc[:, m * NQ:(m + 1) * NQ], ACT.Tanh,
                                                   bias=w["gate_bias"][:, 2, m:m + 1])
                    ins.then_inc(misc_free, 1)

                def h_into(p, par, n):
                    full(act, n)
                    wait(act, stored, 16 * p)
                    nc.scalar.copy(stage[:, D:2 * D], misc[:NQ, :D]).then_inc(misc_free, 1)

                def qh(g):
                    def f(j, par, n):
                        full(act, n)
                        wait(act, scored, H * (j - 1))
                        nc.scalar.activation(flat(qs[par][:, g * GH:(g + 1) * GH, :]), misc[:, :GH * NQ], ACT.Copy,
                                             scale=float(DK1) ** -0.5).then_inc(misc_free, 1)
                    return f

                def tanh_h(j):
                    act.wait_ge(h_in_ready, j + 1)
                    wait(act, x2_ready, j)
                    nc.scalar.activation(h_out[:], h_in[:], ACT.Tanh).then_inc(h_ready, 1)

                def sigmoid_exp(p):
                    act.wait_ge(routed, N_ROUTER * p + 1)
                    nc.scalar.activation(rt[:, 1, :], rt[:, 0, :], ACT.Exp, scale=-1.0).then_inc(sig_exp, 1)

                def shared_exps(p, par, n):
                    full(act, n)
                    wait(act, shared, 3 * p)
                    nc.scalar.copy(z[:], misc[:, :NQ]).then_inc(misc_free, 1)
                    act.wait_ge(misc_free, n + 1)
                    nc.scalar.activation(sig[:, 0, :], z[:], ACT.Exp, scale=-1.0).then_inc(shared_exp, 1)

                if A:
                    hooks = {"q": q, "k0": k(0), "k1": k(1), "gates_fi": gates_fi, "gate_g": gate_g, "h_in": h_into}
                else:
                    hooks = {f"q{g}": qh(g) for g in range(NG)}
                    hooks["router"] = lambda p, par, n: sigmoid_exp(p)
                    hooks["shared_up"] = shared_exps
                    tanh_h(0)
                uses.run(hooks, -1, None, 1, first=True)
                for h in range(LEAD):
                    exponentials(0, h)

                def body(i, par, first, last):
                    for h in range(H):
                        if h + LEAD < H:
                            exponentials(i, h + LEAD)
                        elif not last:
                            exponentials(i + 1, h + LEAD - H)
                        keep_turned(i, h)
                        if h and h % GH == 0:
                            group(i, par, h // GH - 1)
                        if h == 0 and not first:
                            group(i - 1, 1 - par, NG - 1)
                        if not A and h == 0 and not last:
                            tanh_h(i + 1)
                        uses.run(hooks, i, h, par, first, last)

                walk(nc.scalar, NB, body)
                group(NB - 1, 1, NG - 1)
                uses.run(hooks, NB, None, 0, last=True)

            @block.vector
            def _(dve):
                def maximum(i, h):
                    r = h % RING
                    dve.wait_ge(scored, H * i + h + 1)
                    nc.vector.tensor_reduce(nmax[:, r:r + 1], s_bank[S_OF[h]][:NQ, :NK], AX, ALU.max, negate=True).then_inc(maxed, 1)

                def normalise(i, h):
                    r = h % RING
                    dve.wait_ge(exped, H * i + h + 1)
                    nc.vector.reciprocal(rinv[:, r:r + 1], rsum[:, r:r + 1]).then_inc(inverted, 1)
                    dve.wait_ge(inverted, H * i + h + 1)
                    nc.vector.tensor_scalar(prob[:, r, :NK], prob[:, r, :NK], rinv[:, r:r + 1], None, ALU.mult).then_inc(normed, 1)

                def norm(src, dst, st, j, counted, rstd, done):
                    nc.vector.bn_stats(st[:, 0:6], src).then_inc(counted, 1)
                    wait_apart(dve, counted, 3 * j + 1, spare)
                    nc.vector.bn_aggr(st[:, 6:8], st[:, 0:6]).then_inc(counted, 1)
                    dve.wait_ge(counted, 3 * j + 2)
                    nc.vector.tensor_scalar(st[:, 8:9], st[:, 7:8], LN_EPS, None, ALU.add).then_inc(counted, 1)
                    dve.wait_ge(rstd, j + 1)
                    nc.vector.tensor_scalar(dst[:], src, st[:, 6:7], st[:, 9:10], ALU.subtract, ALU.mult).then_inc(done, 1)

                def norm_x(j, par):
                    src = xt[par][:, 0:D]
                    dve.wait_ge(x_in[par], loads(j, par))
                    if not A:
                        wait(dve, h_ready, j)
                        nc.vector.tensor_tensor(h_in[:], xt[par][:, D:2 * D], w["cf"][:NQ, :], ALU.add).then_inc(h_in_ready, 1)
                        dve.wait_ge(h_ready, j + 1)
                        nc.vector.scalar_tensor_tensor(out=src, in0=h_out[:], scalar=g_tanh[:NQ, 2:3], in1=src,
                                                       op0=ALU.mult, op1=ALU.add).then_inc(x2_ready, 1)
                        dve.wait_ge(x2_ready, j + 1)
                    norm(src, xln, stats[:, 0, :], j, x_stats, x_rstd, x_normed)

                def norm_y(p):
                    dve.wait_ge(misc_free, uses.out(p, "wo"))
                    if not A:
                        wait(dve, kept, p)
                    norm(stage[:, 0:D], x1ln, stats[:, 1, :], p, y_stats, y_rstd, y_normed)

                def keep_xT(j, par, n):
                    full(dve, n)
                    nc.vector.tensor_copy(flat(xT[:]), misc[:, :CC * NQ]).then_inc(misc_free, 1)

                def keep_ctxT(j, par, n):
                    full(dve, n)
                    if not A:
                        wait(dve, scored, H * (j - 1))
                    nc.vector.tensor_copy(ctxT[:] if A else kT[par][:, 0, :], misc[:, :NK]).then_inc(misc_free, 1)

                def keep_v(cs):
                    def f(j, par, n):
                        full(dve, n)
                        if isinstance(j, int) and j == 0:
                            dve.wait_ge(padded, 2)
                        wait(dve, valued, H * (j - 1))
                        for a, c in enumerate(cs):
                            ins = nc.vector.tensor_tensor(
                                vals[par][:, c, :, 0:DK0], misc[:KP, a * D:(a + 1) * D].rearrange("p (h d) -> p h d", h=H),
                                w["bv0"][:KP, 0:D].rearrange("p (h d) -> p h d", h=H), ALU.add)
                        ins.then_inc(misc_free, 1)
                    return f

                def residual(p, par, n):
                    full(dve, n)
                    dve.wait_ge(xres_ready, p + 1)
                    if A:
                        wait(dve, stored, 16 * p)
                    nc.vector.scalar_tensor_tensor(out=stage[:, 0:D], in0=misc[:NQ, :D], scalar=g_tanh[:NQ, layer:layer + 1],
                                                   in1=xres[par][:], op0=ALU.mult, op1=ALU.add).then_inc(misc_free, 1)

                def keep_lnT(p, par, n):
                    full(dve, n)
                    nc.vector.tensor_copy(flat(x1T[:]), misc[:, :CC * NQ]).then_inc(misc_free, 1)

                def update(p):
                    dve.wait_ge(misc_free, uses.out(p, "gate_g"))
                    f, i, g = (flat(gates[:, a]) for a in range(3))
                    c = flat(w["cT"][:])
                    nc.vector.scalar_tensor_tensor(out=upd[:, 0, :], in0=f, scalar=1.0, in1=c, op0=ALU.add, op1=ALU.mult).then_inc(updated, 1)
                    nc.vector.scalar_tensor_tensor(out=upd[:, 1, :], in0=i, scalar=1.0, in1=g, op0=ALU.add, op1=ALU.mult).then_inc(updated, 1)
                    dve.wait_ge(updated, 4 * p + 2)
                    nc.vector.tensor_tensor(upd[:, 2, :], upd[:, 0, :], upd[:, 1, :], ALU.add).then_inc(updated, 1)
                    dve.wait_ge(updated, 4 * p + 3)
                    nc.vector.tensor_scalar(c, upd[:, 2, :], 0.5, None, ALU.mult).then_inc(updated, 1)

                def keep_heads(g):
                    def f(i, par, n):
                        full(dve, n)
                        wait(dve, misc_free, uses.out(i - 2, "wo"))
                        nc.vector.tensor_copy(flat(oT[par][:, 2 * g:2 * g + 2, :]), misc[:, :2 * NQ]).then_inc(misc_free, 1)
                    return f

                def route(p):
                    done = [1]

                    def step(ins):
                        ins.then_inc(routed, 1)
                        done[0] += 1
                        wait_apart(dve, routed, N_ROUTER * p + done[0], spare)

                    dve.wait_ge(routed, N_ROUTER * p + 1)
                    step(nc.vector.tensor_tensor(rt[:, 2, :], rt[:, 0, :], w["ebias"][:NQ, :], ALU.add))
                    step(nc.vector.max(rts[:, 0:TOP_K], rt[:, 2, :]))
                    step(nc.vector.match_replace(rt[:, 3, :], rts[:, 0:TOP_K], rt[:, 2, :], GONE))
                    step(nc.vector.tensor_tensor(rt[:, 4, :], rt[:, 3, :], rt[:, 2, :], ALU.not_equal))
                    dve.wait_ge(sig_exp, p + 1)
                    step(nc.vector.tensor_scalar(rt[:, 5, :], rt[:, 1, :], 1.0, None, ALU.add))
                    step(nc.vector.reciprocal(rt[:, 7, :], rt[:, 5, :]))
                    step(nc.vector.scalar_tensor_tensor(out=rt[:, 5, :], in0=rt[:, 7, :], scalar=1.0, in1=rt[:, 4, :],
                                                        op0=ALU.mult, op1=ALU.mult, accum_out=rts[:, 8:9]))
                    step(nc.vector.tensor_scalar(rts[:, 9:10], rts[:, 8:9], 1e-8, None, ALU.add))
                    step(nc.vector.reciprocal(rts[:, 10:11], rts[:, 9:10]))
                    nc.vector.tensor_scalar(rt[:, 6, :], rt[:, 5, :], rts[:, 10:11], None, ALU.mult).then_inc(routed, 1)

                def keep_affinity(p, par, n):
                    full(dve, n)
                    nc.vector.tensor_copy(rt[:, 0, :], misc[:NQ, :E]).then_inc(misc_free, 1)
                    dve.wait_ge(misc_free, n + 1)
                    nc.vector.tensor_copy(rts[:, 11:12], rt[:, 0, 0:1]).then_inc(routed, 1)
                    route(p)

                def place(p, par, n):
                    done = [0]

                    def step(ins, apart=False):
                        ins.then_inc(placed, 1)
                        done[0] += 1
                        if apart:
                            wait_apart(dve, placed, N_PLACED * p + done[0], spare)
                        else:
                            dve.wait_ge(placed, N_PLACED * p + done[0])

                    full(dve, n)
                    nc.vector.tensor_tensor(placing[:, 0, :], misc[:NQ, :E], w["region"][:NQ, :], ALU.add).then_inc(misc_free, 1)
                    dve.wait_ge(misc_free, n + 1)
                    step(nc.vector.tensor_tensor(placing[:, 1, :], placing[:, 0, :], rt[:, 4, :], ALU.mult), True)
                    step(nc.vector.max(w8[:, 0:TOP_K], placing[:, 1, :]))
                    wait(dve, scattered, 16 * TOP_K * p)
                    nc.vector.tensor_scalar(ids[:], w8[:, 0:TOP_K], -1.0, None, ALU.add).then_inc(placed, 1)
                    for k in range(TOP_K):
                        nc.vector.scalar_tensor_tensor(out=placing[:, 2 + k, :], in0=placing[:, 1, :], scalar=w8[:, k:k + 1], in1=rt[:, 6, :],
                                                       op0=ALU.is_equal, op1=ALU.mult,
                                                       accum_out=w8[:, TOP_K + k:TOP_K + k + 1]).then_inc(placed, 1)
                    nc.vector.tensor_tensor(w["chosen"][:], w["chosen"][:], rt[:, 4, :], ALU.add).then_inc(placed, 1)
                    dve.wait_ge(placed, N_PLACED * p + N_PLACED - 1)
                    nc.vector.tensor_scalar(slot_w[:], w8[:, TOP_K:], g_tanh[:NQ, 3:4], None, ALU.mult).then_inc(placed, 1)

                def shared_silu(p, par, n):
                    dve.wait_ge(shared_exp, p + 1)
                    wait(dve, misc_free, uses.out(p - 1, "shared_down"))
                    nc.vector.tensor_scalar(sig[:, 1, :], sig[:, 0, :], 1.0, None, ALU.add).then_inc(shared, 1)
                    dve.wait_ge(shared, 3 * p + 1)
                    nc.vector.reciprocal(hs[:], sig[:, 1, :]).then_inc(shared, 1)
                    dve.wait_ge(shared, 3 * p + 2)
                    nc.vector.tensor_tensor(hs[:], hs[:], z[:], ALU.mult).then_inc(shared, 1)

                def keep_x3(p, par, n):
                    full(dve, n)
                    nc.vector.scalar_tensor_tensor(out=X3[:, bass.ds(p, 1), :].rearrange("q o d -> q (o d)"), in0=misc[:NQ, :D],
                                                   scalar=g_tanh[:NQ, 3:4], in1=stage[:, 0:D], op0=ALU.mult, op1=ALU.add).then_inc(misc_free, 1)

                hooks = {"xT": keep_xT, "ctxT": keep_ctxT, "wo": residual, "lnT": keep_lnT}
                if A:
                    hooks |= {"v01": keep_v((0, 1)), "v2": keep_v((2,))}
                else:
                    hooks |= {"router": keep_affinity, "rank": place, "shared_up": shared_silu, "shared_down": keep_x3} | {f"ho{g}": keep_heads(g) for g in range(NG)}
                x_slot, y_slot = (5, 1) if A else (0, 3)

                nc.vector.memset(spare[:], 0.0).then_inc(spare_set, 1)
                dve.wait_ge(spare_set, 1)
                norm_x(0, 0)
                uses.run(hooks, -1, None, 1, first=True)
                for h in range(LEAD):
                    maximum(0, h)
                normalise(0, 0)

                def body(i, par, first, last):
                    for h in range(H):
                        if h + LEAD < H:
                            maximum(i, h + LEAD)
                        elif not last:
                            maximum(i + 1, h + LEAD - H)
                        if h + 1 < H:
                            normalise(i, h + 1)
                        elif not last:
                            normalise(i + 1, 0)
                        uses.run(hooks, i, h, par, first, last)
                        if h == y_slot and not first:
                            norm_y(i - 1)
                        if h == x_slot and not last:
                            norm_x(i + 1, 1 - par)
                        if A and h == 7 and not first:
                            update(i - 1)

                walk(nc.vector, NB, body)
                for _, kind, name in uses.order:
                    if kind == "post":
                        if name in hooks:
                            hooks[name](NB - 1, 1, uses.before(NB, name))
                        if name == "wo":
                            norm_y(NB - 1)
                        if name == "gate_g":
                            update(NB - 1)
                if A:
                    n = uses.out(NB - 1, "h_in")
                    full(dve, n)
                    nc.vector.tensor_tensor(w["cf"][:NQ, :], misc[:NQ, :D], w["bo_ffn"][:NQ, :], ALU.add).then_inc(misc_free, 1)
                    dve.wait_ge(misc_free, n + 1)

            @block.gpsimd
            def _(pool):
                def power(st, j, counted, rstd):
                    pool.wait_ge(counted, 3 * j + 3)
                    nc.gpsimd.tensor_tensor(st[:, 9:10], st[:, 8:9], w["neg_half"][:NQ, :], ALU.pow).then_inc(rstd, 1)

                def residual_x(j, par):
                    if A:
                        pool.wait_ge(x_in[par], loads(j, par))
                    else:
                        pool.wait_ge(x2_ready, j + 1)
                    wait(pool, misc_free, uses.out(j - 2, "wo"))
                    nc.gpsimd.tensor_tensor(xres[par][:], xt[par][:, 0:D], w["tgbo"][layer][:NQ, :], ALU.add).then_inc(xres_ready, 1)

                def mask(j, par):
                    pool.wait_ge(misc_free, uses.out(j, "q"))
                    wait(pool, scored, H * (j - 1))
                    for c in range(CC):
                        nc.gpsimd.tensor_tensor(qs[par][:, 8 * c:8 * c + 8, :],
                                                qT[:, c, :].unsqueeze(1).to_broadcast([P, 8, NQ]),
                                                w["head_mask"][:].unsqueeze(2).to_broadcast([P, 8, NQ]), ALU.mult).then_inc(masked, 1)

                def scatter(p):
                    pool.wait_ge(y_normed, p + 1)
                    pool_wait_apart(pool, scattered, 16 * TOP_K * p, pool_spare, 0)
                    nc.gpsimd.tensor_copy(rows[:, :, 0:D], x1ln[:].unsqueeze(1).to_broadcast([NQ, TOP_K, D])).then_inc(kept, 1)
                    if not (isinstance(p, int) and p == 0):
                        nc.gpsimd.tensor_scalar(rows[:, :, D], rows[:, :, D], float(NQ * TOP_K), None, ALU.add).then_inc(renumbered, 1)
                        pool_wait_apart(pool, renumbered, p, pool_spare, 1)
                    pool_wait_apart(pool, kept, p + 1, pool_spare, 2)
                    pool_wait_apart(pool, placed, N_PLACED * (p + 1), pool_spare, 3)
                    nc.gpsimd.tensor_copy(rows[:, :, D + 1], slot_w[:]).then_inc(weighted, 1)
                    pool_wait_apart(pool, weighted, p + 1, pool_spare, 4)
                    for k in range(TOP_K):
                        nc.gpsimd.indirect_dma_start(rows_d, bass.IndirectOffsetOnAxis(ap=ids[:, k:k + 1], axis=0),
                                                     rows[:, k, :], None).then_inc(scattered, 16)

                def before(j, par):
                    power(stats[:, 0, :], j, x_stats, x_rstd)
                    residual_x(j, par)
                    if A:
                        mask(j, par)

                def after(p):
                    power(stats[:, 1, :], p, y_stats, y_rstd)
                    if not A:
                        scatter(p)

                if A:
                    for n in range(2):
                        nc.gpsimd.memset(vals[n][:], 0.0).then_inc(padded, 1)
                else:
                    nc.gpsimd.memset(pool_spare[:], 0.0).then_inc(pool_spare_set, 1)
                    nc.gpsimd.iota(numbers[:], pattern=[[1, TOP_K]], base=0, channel_multiplier=TOP_K).then_inc(numbered, 1)
                    pool.wait_ge(numbered, 1)
                    nc.gpsimd.tensor_copy(rows[:, :, D], numbers[:]).then_inc(numbered, 1)
                    pool.wait_ge(numbered, 2)
                    pool.wait_ge(pool_spare_set, 1)
                before(0, 0)

                def body(i, par, first, last):
                    if A and not first:
                        after(i - 1)
                    if not last:
                        before(i + 1, 1 - par)
                    if not A and not first:
                        after(i - 1)

                walk(nc.gpsimd, NB, body)
                after(NB - 1)
                if not A:
                    pool.wait_ge(scattered, 16 * TOP_K * NB)


def tables(nc, t, w, bank, table_d, rows_d, table, starts_pad, wup):
    NB, NQ, D = t["x"].shape
    E = t["L1_ffn_W_up"].shape[0]
    CAP, N = experts_shape(t)
    CH = -(-N // P)
    with ExitStack() as es:
        def sb(name, shape, dt=F32):
            return es.enter_context(nc.sbuf_tensor(name, shape, dt))

        def sem(name):
            return es.enter_context(nc.semaphore(name))

        count, tiles_i = sb("count", [P, E]), sb("tiles_i", [P, 2, E], I32)
        tiles, upto, picked = sb("tiles", [P, E]), sb("upto", [P, E]), sb("picked", [P, E])
        tau_i, tau = sb("tau_i", [P, CH], I32), sb("tau", [P, CH])
        found = sb("found", [P, 4, CH])
        tab = sb("tab", [P, CH, 2], I32)
        zeros, beyond = sb("zeros", [P, D + 2]), sb("beyond", [P, 1], I32)
        counted, made, tau_made, zeroed = sem("counted"), sem("made"), sem("tau_made"), sem("zeroed")
        tab_out, tab_in, padded, wup_in = sem("tab_out"), sem("tab_in"), sem("pads_written"), sem("wup_in")
        padded_too = sem("pads_written_too")
        N_MADE = 6 + 6 * CH

        with nc.Block() as block:

            @block.tensor
            def _(pe):
                pe.matmul(bank[0][:, :E], w["ones"][:NQ, :], w["chosen"][:], start=True, stop=True).then_inc(counted, 1)

            @block.gpsimd
            def _(pool):
                nc.gpsimd.iota(tau_i[:], pattern=[[P, CH]], base=0, channel_multiplier=1).then_inc(tau_made, 1)
                nc.gpsimd.memset(zeros[:], 0.0).then_inc(zeroed, 1)
                nc.gpsimd.iota(beyond[:], pattern=[[0, 1]], base=NB * NQ * TOP_K, channel_multiplier=1).then_inc(zeroed, 1)
                pool.wait_ge(zeroed, 2)
                nc.gpsimd.tensor_copy(zeros[:, D:D + 1], beyond[:]).then_inc(zeroed, 1)

            @block.vector
            def _(dve):
                done = [0]

                def step(ins):
                    ins.then_inc(made, 1)
                    done[0] += 1
                    dve.wait_ge(made, done[0])

                dve.wait_ge(counted, 1)
                dve.wait_ge(tau_made, 1)
                step(nc.vector.tensor_copy(tau[:], tau_i[:]))
                step(nc.vector.tensor_scalar(tiles_i[:, 0, :], bank[0][:, :E], float(P - 1), None, ALU.add))
                step(nc.vector.scalar_tensor_tensor(out=starts_pad[:], in0=bank[0][0:1, :E], scalar=-1.0, in1=w["region"][0:1, :],
                                                    op0=ALU.add, op1=ALU.add))
                step(nc.vector.tensor_scalar(tiles_i[:, 1, :], tiles_i[:, 0, :], P.bit_length() - 1, None, ALU.arith_shift_right))
                step(nc.vector.tensor_copy(tiles[:], tiles_i[:, 1, :]))
                step(nc.vector.tensor_tensor_scan(upto[:], w["ones"][:, :E], tiles[:], 0.0, ALU.mult, ALU.add))
                for c in range(CH):
                    step(nc.vector.scalar_tensor_tensor(out=picked[:], in0=upto[:], scalar=tau[:, c:c + 1], in1=w["ones"][:, :E],
                                                        op0=ALU.is_le, op1=ALU.mult, accum_out=found[:, 0, c:c + 1]))
                    step(nc.vector.scalar_tensor_tensor(out=picked[:], in0=upto[:], scalar=tau[:, c:c + 1], in1=tiles[:],
                                                        op0=ALU.is_le, op1=ALU.mult, accum_out=found[:, 1, c:c + 1]))
                    step(nc.vector.tensor_scalar(found[:, 2, c:c + 1], tau[:, c:c + 1], found[:, 1, c:c + 1], float(P), ALU.subtract, ALU.mult))
                    step(nc.vector.scalar_tensor_tensor(out=found[:, 3, c:c + 1], in0=found[:, 0, c:c + 1], scalar=float(CAP), in1=found[:, 2, c:c + 1],
                                                        op0=ALU.mult, op1=ALU.add))
                    step(nc.vector.tensor_scalar(tab[:, c, 1:2], found[:, 3, c:c + 1], float(E * CAP), None, ALU.min))
                    step(nc.vector.tensor_scalar(tab[:, c, 0:1], found[:, 0, c:c + 1], float(E - 1), None, ALU.min))
                

            def pad(eng, kind, first, semaphore):
                eng.wait_ge(zeroed, 3)
                eng.wait_ge(made, 3)
                with eng.Fori(0, E // 8) as m:
                    for k in range(4):
                        row = nc.values_load(starts_pad[0:1, bass.ds(m * 4 + (first + k), 1)], engines=(kind,), min_val=0, max_val=E * CAP - P,
                                             skip_runtime_bounds_check_because="a region has a tile's rows more than there are tokens")
                        eng.dma_start(rows_d[bass.ds(row, P), :], zeros[:]).then_inc(semaphore, 16)

            @block.scalar
            def _(act):
                for e in range(0, E, 16):
                    for c in range(D // P):
                        act.dma_start(wup[:, e:e + 16, c * P:(c + 1) * P],
                                      t["L1_ffn_W_up"][e:e + 16, c * P:(c + 1) * P, :].rearrange("e p f -> p e f")).then_inc(wup_in, 16)
                pad(nc.scalar, mybir.EngineType.Activation, E // 2, padded_too)
                act.wait_ge(wup_in, 16 * (E // 16) * (D // P))
                act.wait_ge(padded_too, 16 * (E // 2))

            @block.sync
            def _(sp):
                sp.wait_ge(zeroed, 3)
                sp.dma_start(rows_d[E * CAP:E * CAP + P, :], zeros[:]).then_inc(padded, 16)
                pad(nc.sync, mybir.EngineType.SP, 0, padded)
                sp.wait_ge(made, N_MADE)
                sp.dma_start(table_d.rearrange("(c p) k -> p c k", p=P), tab[:]).then_inc(tab_out, 16)
                sp.wait_ge(tab_out, 16)
                sp.dma_start(table[:], table_d.rearrange("(o n) k -> o (n k)", o=1)).then_inc(tab_in, 16)
                sp.wait_ge(tab_in, 16)
                sp.wait_ge(padded, 16 * (E // 2 + 1))


def expert_phase(nc, t, w, bank, rows_d, results_d, table, wup, wdn):
    D = t["x"].shape[2]
    E = t["L1_ffn_W_up"].shape[0]
    CAP, N = experts_shape(t)
    RB = 8
    RES = 4
    CC = D // P
    with ExitStack() as es:
        def sem(name):
            return es.enter_context(nc.semaphore(name))

        def buffers(weights, a, b, first=0):
            return weights[:, first:first + a * b].rearrange("p (a b) -> p a b", a=a)

        mqk = w["mqk"][:].rearrange("p c h k -> p (c h k)")
        xr = buffers(mqk, RB, D + 2)
        xrT = buffers(mqk, 2, D, RB * (D + 2))
        hid, hidT = buffers(mqk, 2, P, (RB + 2) * (D + 2)), buffers(mqk, 2, P, (RB + 3) * (D + 2))
        res = buffers(w["wo1"][:].rearrange("p c d -> p (c d)"), RES, D)
        x_in = [sem(f"rows_in{b}") for b in range(RB)]
        res_out = [sem(f"results_out{b}") for b in range(RES)]
        x_turned, xT_out, upped, silued = sem("x_turned"), sem("xT_out"), sem("upped"), sem("silued")
        h_turned, hT_out, downed, res_made = sem("h_turned"), sem("hT_out"), sem("downed"), sem("res_made")
        spare_set, carried = sem("spare_set"), sem("carried")
        dest = es.enter_context(nc.sbuf_tensor("dest", [P, RB], U32))
        spare = es.enter_context(nc.sbuf_tensor("spare", [P, 2 + RES], F32))
        ident = w["ident"]

        def tiles(body):
            def f(eng):
                for b in range(RB):
                    body(b, b)
                with eng.Fori(1, N // RB - 1) as m:
                    for b in range(RB):
                        body(m * RB + b, b)
                for b in range(RB):
                    body(N - RB + b, b)
            return f

        def inside(n):
            return not isinstance(n, int) or 0 <= n < N

        def passes(n, b, ring):
            return (n - b % ring) * (16 // ring)

        def from_table(engine, n, column, most):
            return nc.values_load(table[0:1, bass.ds(n * 2 + column, 1)], engines=(engine,), min_val=0, max_val=most,
                                  skip_runtime_bounds_check_because="the table is made with a minimum against this bound")

        with nc.Block() as block:

            @block.sync
            def _(sp):
                def load(n, b):
                    wait(sp, res_made, n - RB + 1)
                    row = from_table(mybir.EngineType.SP, n, 1, E * CAP)
                    sp.dma_start(xr[:, b, :], rows_d[bass.ds(row, P), :]).then_inc(x_in[b], 16)

                tiles(load)(nc.sync)

            @block.gpsimd
            def _(pool):
                nc.gpsimd.memset(spare[:], 0.0).then_inc(spare_set, 1)
                pool.wait_ge(spare_set, 1)

                def body(n, b):
                    wait(pool, carried, n - RES + 1)
                    pool_wait_apart(pool, res_made, n + 1, spare, b % RES).then_inc(carried, 1)
                    nc.gpsimd.indirect_dma_start(results_d, bass.IndirectOffsetOnAxis(ap=dest[:, b:b + 1], axis=0),
                                                 res[:, b % RES, :], None, bounds_check=results_d.shape[0] - 1,
                                                 oob_is_err=False).then_inc(res_out[b % RES], 16)

                tiles(body)(nc.gpsimd)
                for b in range(RES):
                    pool.wait_ge(res_out[b], 16 * (N // RES))

            @block.tensor
            def _(pe):
                def turn_rows(n, b):
                    pe.wait_ge(x_in[b], passes(n, b, RB) + 16)
                    for c in range(CC):
                        mm = pe.transpose(bank[b % 2][:, c * P:(c + 1) * P], xr[:, b, c * P:(c + 1) * P], ident[:])
                    mm.then_inc(x_turned, 1)

                def up(n, b, e):
                    pe.wait_ge(xT_out, n + 1)
                    for c in range(CC):
                        mm = pe.matmul(bank[2 + b % 2][:, :P], xrT[:, b % 2, c * P:(c + 1) * P],
                                       wup[:, bass.ds(e, 1), c * P:(c + 1) * P].rearrange("p o f -> p (o f)"),
                                       start=(c == 0), stop=(c == CC - 1))
                    mm.then_inc(upped, 1)

                def turn_hidden(n, b):
                    pe.wait_ge(silued, n + 1)
                    pe.transpose(bank[4 + b % 2][:, :P], hid[:, b % 2, :], ident[:]).then_inc(h_turned, 1)

                def down(n, b, e):
                    pe.wait_ge(hT_out, n + 1)
                    pe.matmul(bank[6 + b % 2][:, :D], hidT[:, b % 2, :], wdn[:, bass.ds(e, 1), :].rearrange("p o d -> p (o d)"),
                              start=True, stop=True).then_inc(downed, 1)

                def body(n, b, experts):
                    if inside(n + 2):
                        turn_rows(n + 2, (b + 2) % RB)
                    if inside(n - 2):
                        down(n - 2, (b - 2) % RB, experts[0])
                    if inside(n + 1):
                        up(n + 1, (b + 1) % RB, experts[3])
                    turn_hidden(n, b)

                def round(base, first=False, last=False):
                    def expert(n):
                        return from_table(mybir.EngineType.PE, n, 0, E - 1) if inside(n) else None
                    e = [expert(base + k) for k in range(-2, 2)]
                    for b in range(RB):
                        following = expert(base + b + 2) if b < RB - 1 else None
                        body(base + b, b, e)
                        e = e[1:] + [following]

                turn_rows(0, 0)
                turn_rows(1, 1)
                up(0, 0, from_table(mybir.EngineType.PE, 0, 0, E - 1))
                round(0)
                with nc.tensor.Fori(1, N // RB - 1) as m:
                    round(m * RB)
                round(N - RB)
                for n in (N - 2, N - 1):
                    pe.wait_ge(res_made, n - 1)
                    down(n, n % RB, from_table(mybir.EngineType.PE, n, 0, E - 1))

            @block.vector
            def _(dve):
                def keep_xT(n, b):
                    dve.wait_ge(x_turned, n + 1)
                    nc.vector.tensor_copy(xrT[:, b % 2, :], bank[b % 2][:, :D]).then_inc(xT_out, 1)

                def keep_hT(n, b):
                    dve.wait_ge(h_turned, n + 1)
                    nc.vector.tensor_copy(dest[:, b:b + 1], xr[:, b, D:D + 1])
                    nc.vector.tensor_copy(hidT[:, b % 2, :], bank[4 + b % 2][:, :P]).then_inc(hT_out, 1)

                keep_xT(0, 0)
                keep_xT(1, 1)

                def body(n, b):
                    if inside(n + 2):
                        keep_xT(n + 2, (b + 2) % RB)
                    keep_hT(n, b)

                tiles(body)(nc.vector)

            @block.scalar
            def _(act):
                def silu(n, b):
                    act.wait_ge(upped, n + 1)
                    nc.scalar.activation(hid[:, b % 2, :], bank[2 + b % 2][:, :P], ACT.Silu).then_inc(silued, 1)

                def keep_result(n, b):
                    wait(act, res_out[b % RES], passes(n, b, RES))
                    act.wait_ge(downed, n + 1)
                    nc.scalar.activation(res[:, b % RES, :], bank[6 + b % 2][:, :D], ACT.Copy, scale=xr[:, b, D + 1:D + 2]).then_inc(res_made, 1)

                silu(0, 0)

                def body(n, b):
                    if inside(n - 2):
                        keep_result(n - 2, (b - 2) % RB)
                    if inside(n + 1):
                        silu(n + 1, (b + 1) % RB)

                tiles(body)(nc.scalar)
                keep_result(N - 2, RB - 2)
                keep_result(N - 1, RB - 1)


def combine_phase(nc, t, w, results_d, X3, out):
    NB, NQ, D = t["x"].shape
    RB = 4
    with ExitStack() as es:
        def sb(name, shape, dt=F32):
            return es.enter_context(nc.sbuf_tensor(name, shape, dt))

        def sem(name):
            return es.enter_context(nc.semaphore(name))

        got = [sb(f"got{n}", [NQ, TOP_K, D]) for n in range(RB)]
        total, acc = ([sb(f"{a}{n}", [NQ, D]) for n in range(RB)] for a in ("total", "acc"))
        summed, added = sem("summed"), sem("added")
        arrived = [sem(f"arrived{n}") for n in range(RB)]
        written = [sem(f"written{n}") for n in range(RB)]
        results = results_d.rearrange("(b q k) d -> b q (k d)", b=NB, q=NQ)

        def rounds(eng, body):
            for b in range(RB):
                body(b, b)
            with eng.Fori(1, NB // RB) as m:
                for b in range(RB):
                    body(m * RB + b, b)

        with nc.Block() as block:

            @block.sync
            def _(sp):
                def load(i, b):
                    wait(sp, summed, i - RB + 1)
                    sp.dma_start(flat(got[b]), seq(results, i)).then_inc(arrived[b], 16)

                rounds(nc.sync, load)

            @block.vector
            def _(dve):
                def body(i, b):
                    dve.wait_ge(arrived[b], (i - b) * (16 // RB) + 16)
                    wait(dve, added, i - RB + 1)
                    nc.vector.tensor_reduce(total[b][:], got[b][:].rearrange("q k d -> q d k"), AX, ALU.add).then_inc(summed, 1)

                rounds(nc.vector, body)

            @block.gpsimd
            def _(pool):
                def body(i, b):
                    wait(pool, written[b], (i - b) * (16 // RB))
                    pool.wait_ge(summed, i + 1)
                    nc.gpsimd.tensor_tensor(acc[b][:], total[b][:], X3[:, bass.ds(i, 1), :].rearrange("q o d -> q (o d)"), ALU.add).then_inc(added, 1)

                rounds(nc.gpsimd, body)

            @block.scalar
            def _(act):
                def body(i, b):
                    act.wait_ge(added, i + 1)
                    act.dma_start(seq(out, i), acc[b][:]).then_inc(written[b], 16)

                rounds(nc.scalar, body)
                for b in range(RB):
                    act.wait_ge(written[b], 16 * (NB // RB))


def build_kernel(nc, t, out):
    NB, NQ, D = t["x"].shape
    E = t["L1_ffn_W_up"].shape[0]
    CAP, N = experts_shape(t)
    x1pre_d = nc.dram_tensor("x1_and_h_in", [NB, NQ, 2 * D], F32).ap()
    rows_d = nc.dram_tensor("expert_rows", [E * CAP + P, D + 2], F32).ap()
    results_d = nc.dram_tensor("expert_results", [NB * NQ * TOP_K, D], F32).ap()
    table_d = nc.dram_tensor("tile_table", [-(-N // P) * P, 2], I32).ap()
    with ExitStack() as es:
        def sb(name, shape, dt=F32):
            return es.enter_context(nc.sbuf_tensor(name, shape, dt))

        bank = [es.enter_context(nc.psum_tensor(f"bank{n}", [P, 512], F32)) for n in range(BANKS)]
        w = allocate(nc, es, t)
        with ExitStack() as layer0:
            w |= allocate_a(nc, layer0, t)
            setup(nc, t, w, bank)
            attention_phase(nc, t, w, bank, x1pre_d, 0)
        X3 = sb("X3", [NQ, NB, D])
        with ExitStack() as weights:
            wdn = weights.enter_context(nc.sbuf_tensor("wdn", [P, E, D], F32))
            attention_phase(nc, t, w, bank, x1pre_d, 1, rows_d, X3, wdn)
            wup = weights.enter_context(nc.sbuf_tensor("wup", [P, E, D], F32))
            table = weights.enter_context(nc.sbuf_tensor("table", [1, table_d.shape[0] * 2], I32))
            starts_pad = weights.enter_context(nc.sbuf_tensor("starts_pad", [1, E], I32))
            tables(nc, t, w, bank, table_d, rows_d, table, starts_pad, wup)
            expert_phase(nc, t, w, bank, rows_d, results_d, table, wup, wdn)
        combine_phase(nc, t, w, results_d, X3, out)


_INS = ['x', 'ctx_512', 'g_xattn', 'g_ffn', 'L0_xattn_Wq', 'L0_xattn_bq', 'L0_xattn_Wk', 'L0_xattn_bk', 'L0_xattn_Wv',
        'L0_xattn_bv', 'L0_xattn_Wo', 'L0_xattn_bo', 'L0_ffn_wf', 'L0_ffn_uf', 'L0_ffn_bf', 'L0_ffn_wi', 'L0_ffn_ui',
        'L0_ffn_bi', 'L0_ffn_wc', 'L0_ffn_uc', 'L0_ffn_bc', 'L0_ffn_wo', 'L0_ffn_uo', 'L0_ffn_bo', 'L0_ffn_in_c',
        'L1_xattn_Wq', 'L1_xattn_Wk', 'L1_xattn_Wv', 'L1_xattn_Wo', 'L1_xattn_bo', 'L1_ffn_centroids',
        'L1_ffn_expert_biases', 'L1_ffn_Ws_up', 'L1_ffn_Ws_down', 'L1_ffn_W_up', 'L1_ffn_W_down']


def kernel(**inputs):
    import numpy as _np
    import concourse.bacc as _bacc
    from concourse import mybir as _mybir
    from concourse.bass_utils import run_bass_kernel_spmd as _run

    nc = _bacc.Bacc("TRN2", target_bir_lowering=False, num_devices=1)
    arrays, t = {}, {}
    for name in _INS:
        a = _np.ascontiguousarray(inputs[name])
        arrays[f"in_{name}_dram"] = a
        t[name] = nc.dram_tensor(f"in_{name}_dram", a.shape, _mybir.dt.from_np(a.dtype), kind="ExternalInput").ap()
    out = nc.dram_tensor("out_0_dram", inputs["x"].shape, _mybir.dt.float32, kind="ExternalOutput").ap()
    build_kernel(nc, t, out)
    r = _run(nc, [arrays], core_ids=[0])
    return r.results[0]["out_0_dram"]
```

```python
from contextlib import ExitStack

import concourse.bass as bass
from concourse import mybir
from concourse.alu_op_type import AluOpType as ALU

F32 = mybir.dt.float32
BF16 = mybir.dt.bfloat16
U32 = mybir.dt.uint32
I32 = mybir.dt.int32
ACT = mybir.ActivationFunctionType
AX = mybir.AxisListType.X

P = 128
LN_EPS = 1e-5
TOP_K = 8
GONE = -3.0e38
BANKS = 8
RING = 4
LEAD = 2
GH = 4
PARTS = 3
STACK = [(0, 0), (0, 1), (1, 0), (1, 1), (0, 2), (2, 0), (1, 2), (2, 1)]

ORDER_A = [
    (0, "pre", "ctxT"), (1, "pre", "k0"), (3, "post", "wo"), (4, "pre", "k1"), (5, "pre", "xT"), (6, "pre", "q"),
    (7, "post", "lnT"), (8, "post", "gate_f"), (9, "pre", "v01"), (10, "post", "gate_i"), (11, "pre", "v2"),
    (12, "post", "gate_g"), (14, "post", "h_in"),
]
ORDER_C = [
    (0, "own", "q2"), (1, "own", "q3"), (2, "post", "ho3"), (3, "post", "wo"), (4, "pre", "ctxT"), (5, "pre", "xT"),
    (6, "own", "ho0"), (7, "post", "lnT"), (8, "post", "router"), (9, "post", "shared_up"), (10, "own", "ho1"),
    (11, "pre", "q0"), (12, "pre", "q1"), (13, "post", "rank"), (14, "own", "ho2"), (15, "post", "shared_down"),
]


def wait(eng, sem, value):
    if isinstance(value, int) and value <= 0:
        return
    eng.wait_ge(sem, value)


def wait_apart(eng, sem, value, spare):
    wait(eng, sem, value)
    eng.tensor_copy(spare[:, 0:1], spare[:, 1:2])


def pool_wait_apart(pool, sem, value, spare, n):
    wait(pool, sem, value)
    return pool.tensor_tensor(spare[:, 2 + n:3 + n], spare[:, 0:1], spare[:, 1:2], ALU.add)


class Uses:

    def __init__(self, order, n_seq):
        self.order, self.n_seq = order, n_seq
        self.n = {k: sum(x[1] == k for x in order) for k in ("pre", "post", "own")}

    def before(self, i, name):
        n, const = self.n, isinstance(i, int)
        if const and i < 0:
            base, has = 0, {"pre"}
        elif const and i == 0:
            base, has = n["pre"], {"pre", "own"}
        elif const and i == self.n_seq:
            base, has = self.n_seq * (n["pre"] + n["own"]) + (i - 1) * n["post"], {"post"}
        else:
            base = i * (n["pre"] + n["own"] + n["post"]) + (n["pre"] - n["post"])
            has = {"own", "post"} | ({"pre"} if not (const and i == self.n_seq - 1) else set())
        k = 0
        for _, kind, x in self.order:
            if x == name:
                return base + k
            k += kind in has
        raise KeyError(name)

    def out(self, j, name):
        if isinstance(j, int) and j < 0:
            return 0
        kind = next(k for _, k, x in self.order if x == name)
        return self.before(j + {"pre": -1, "post": 1, "own": 0}[kind], name) + 1

    def run(self, hooks, i, h, par, first=False, last=False, then=(None, None)):
        for slot, kind, name in self.order:
            if name == then[0]:
                then[1]()
            if (h is not None and slot != h) or name not in hooks:
                continue
            if (kind == "post" and first) or (kind == "pre" and last):
                continue
            if h is None and kind != ("pre" if first else "post"):
                continue
            j = i + {"pre": 1, "post": -1, "own": 0}[kind]
            hooks[name](j, par if kind == "own" else 1 - par, self.before(i, name))


def walk(eng, n_seq, body):
    body(0, 0, True, False)
    body(1, 1, False, False)
    with eng.Fori(1, n_seq // 2 - 1) as pair:
        body(pair * 2, 0, False, False)
        body(pair * 2 + 1, 1, False, False)
    body(n_seq - 2, 0, False, False)
    body(n_seq - 1, 1, False, True)


def bcast(v, n, p=P):
    return v.rearrange("(o n) -> o n", o=1).to_broadcast([p, n])


def seq(a, j):
    return a[bass.ds(j, 1)].rearrange("o q d -> (o q) d")


def flat(a):
    return a.rearrange("p a b -> p (a b)")


def experts_shape(t):
    NB, NQ, _ = t["x"].shape
    E = t["L1_ffn_W_up"].shape[0]
    cap = -(-NB * NQ // P) * P + P
    tiles = (TOP_K * NB * NQ + (P - 1) * E) // P
    return cap, -(-tiles // 16) * 16


def allocate(nc, es, t):
    def sb(name, shape):
        return es.enter_context(nc.sbuf_tensor(name, shape, F32))

    NB, NQ, D = t["x"].shape
    H = 16
    INNER = t["L1_xattn_Wq"].shape[1]
    E = t["L1_ffn_W_up"].shape[0]
    CC = D // P
    w = dict(
        ident=sb("ident", [P, P]),
        g_tanh=sb("g_tanh", [P, 4]),
        neg_half=sb("neg_half", [P, 1]),
        tgbo=[sb(f"tgbo{n}", [P, D]) for n in range(2)],
        cf=sb("cf", [P, D]),
        cenT=sb("cenT", [P, CC, E]),
        ebias=sb("ebias", [P, E]),
        mqk=sb("mqk", [P, CC, H, P]),
        wv1=sb("wv1", [P, INNER]),
        wo1=sb("wo1", [P, INNER // P, D]),
        ones=sb("ones", [P, P]),
        earlier=sb("earlier", [P, P]),
        region=sb("region", [P, E]),
        chosen=sb("chosen", [NQ, E]),
        sup=sb("sup", [P, CC, P]), sdn=sb("sdn", [P, D]),
    )
    return w


def allocate_a(nc, es, t):
    def sb(name, shape):
        return es.enter_context(nc.sbuf_tensor(name, shape, F32))

    NB, NQ, D = t["x"].shape
    CC = D // P
    w = dict(
        wq0=sb("wq0", [P, CC, D]), wk0=sb("wk0", [P, D]), wv0=sb("wv0", [P, D]),
        wo0=sb("wo0", [P, CC, D]),
        bq0=sb("bq0", [P, CC]), bk0=sb("bk0", [P, CC]), bv0=sb("bv0", [P, 2 * D]),
        gate_bias=sb("gate_bias", [P, 3, CC]), bo_ffn=sb("bo_ffn", [P, D]),
        cT=sb("cT", [P, CC, NQ]),
    )
    for n in GATE_WEIGHTS:
        w[n + "T"] = sb(n + "T", [P, CC, D])
    return w


GATE_WEIGHTS = ["wf", "wi", "wc", "wo", "uf", "ui", "uc", "uo"]


def setup(nc, t, w, bank):
    NB, NQ, D = t["x"].shape
    H, CC = 16, D // P
    DK0 = D // H
    INNER = t["L1_xattn_Wq"].shape[1]
    DK1 = INNER // H
    PAIRS = INNER // P
    E = t["L1_ffn_W_up"].shape[0]
    with ExitStack() as es:
        def sb(name, shape):
            return es.enter_context(nc.sbuf_tensor(name, shape, F32))

        def sem(name):
            return es.enter_context(nc.semaphore(name))

        wq1, wk1 = sb("wq1", [P, CC, INNER]), sb("wk1", [P, INNER])
        wq1T, wk1T = sb("wq1T", [P, PAIRS, D]), sb("wk1T", [P, PAIRS, P])
        cen, bo_raw, g_raw = sb("cen", [E, D]), sb("bo_raw", [P, 2, D]), sb("g_raw", [P, 4])
        CAP, _ = experts_shape(t)
        region_i = es.enter_context(nc.sbuf_tensor("region_i", [P, E], I32))
        more = sem("more_consts")
        in_c, nat = sb("in_c", [P, CC]), sb("nat", [P, 2, CC, D])
        loaded, consts = sem("loaded"), sem("consts")
        g_ready, scaled = sem("g_ready"), sem("scaled")
        nat_in = [sem(f"nat_in{n}") for n in range(2)]
        written, evacuated, state = sem("set_written"), sem("set_evacuated"), sem("state_zeroed")

        chunked = "(c p) n -> p c n"
        column = "(c p) -> p c"
        loads = [
            (g_raw[:, 0:2], bcast(t["g_xattn"], 2)), (g_raw[:, 2:4], bcast(t["g_ffn"], 2)),
            (w["wq0"][:], t["L0_xattn_Wq"].rearrange(chunked, p=P)),
            (w["wo0"][:], t["L0_xattn_Wo"].rearrange(chunked, p=P)),
            (w["wk0"][:], t["L0_xattn_Wk"]), (w["wv0"][:], t["L0_xattn_Wv"]),
            (w["bv0"][:, 0:D], bcast(t["L0_xattn_bv"], D)), (w["bv0"][:, D:2 * D], bcast(t["L0_xattn_bv"], D)),
            (bo_raw[:, 0, :], bcast(t["L0_xattn_bo"], D)), (bo_raw[:, 1, :], bcast(t["L1_xattn_bo"], D)),
            (w["bo_ffn"][:], bcast(t["L0_ffn_bo"], D)), (w["ebias"][:], bcast(t["L1_ffn_expert_biases"], E)),
            (wq1[:], t["L1_xattn_Wq"].rearrange(chunked, p=P)),
            (wk1[:], t["L1_xattn_Wk"]), (w["wv1"][:], t["L1_xattn_Wv"]),
            (w["wo1"][:], t["L1_xattn_Wo"].rearrange(chunked, p=P)), (cen[:], t["L1_ffn_centroids"]),
            (w["sup"][:], t["L1_ffn_Ws_up"].rearrange(chunked, p=P)), (w["sdn"][:], t["L1_ffn_Ws_down"]),
        ]
        columns = [
            (w["bq0"], "L0_xattn_bq"), (w["bk0"], "L0_xattn_bk"), (w["gate_bias"][:, 0, :], "L0_ffn_bf"),
            (w["gate_bias"][:, 1, :], "L0_ffn_bi"), (w["gate_bias"][:, 2, :], "L0_ffn_bc"), (in_c, "L0_ffn_in_c"),
        ]
        n_loads = len(loads) + CC * len(columns)

        with nc.Block() as block:

            @block.sync
            def _(sp):
                for n, name in enumerate(GATE_WEIGHTS):
                    if n >= 2:
                        sp.wait_ge(written, n - 1)
                    sp.dma_start(nat[:, n % 2], t[f"L0_ffn_{name}"].rearrange(chunked, p=P)).then_inc(nat_in[n % 2], 16)
                    if n == 1:
                        for dst, src in loads:
                            sp.dma_start(dst, src).then_inc(loaded, 16)
                        for dst, name2 in columns:
                            for c in range(CC):
                                sp.dma_start(dst[:, c:c + 1], t[name2][c * P:(c + 1) * P].rearrange("(p o) -> p o", o=1)).then_inc(loaded, 16)

            @block.gpsimd
            def _(pool):
                ident = w["ident"]
                nc.gpsimd.memset(ident[:], 0.0).then_inc(consts, 1)
                nc.gpsimd.memset(w["neg_half"][:], -0.5).then_inc(consts, 1)
                nc.gpsimd.memset(w["ones"][:], 1.0).then_inc(more, 1)
                nc.gpsimd.memset(w["earlier"][:], 1.0).then_inc(more, 1)
                nc.gpsimd.memset(w["chosen"][:], 0.0).then_inc(more, 1)
                nc.gpsimd.iota(region_i[:], pattern=[[CAP // 8, 64]], base=0, channel_multiplier=0).then_inc(more, 1)
                pool.wait_ge(consts, 2)
                nc.gpsimd.affine_select(out=ident[:], in_=ident[:], compare_op=ALU.not_equal, fill=1.0, base=0,
                                        pattern=[[-1, P]], channel_multiplier=1).then_inc(consts, 1)
                pool.wait_ge(more, 4)
                nc.gpsimd.affine_select(out=w["earlier"][:], in_=w["earlier"][:], compare_op=ALU.is_gt, fill=0.0, base=0,
                                        pattern=[[1, P]], channel_multiplier=-1).then_inc(more, 1)

            @block.scalar
            def _(act):
                act.wait_ge(loaded, 16 * n_loads)
                nc.scalar.activation(w["g_tanh"][:], g_raw[:], ACT.Tanh).then_inc(g_ready, 1)

            @block.tensor
            def _(pe):
                used = [0]

                def start():
                    n = used[0]
                    used[0] += 1
                    if n >= BANKS:
                        pe.wait_ge(evacuated, n - BANKS + 1)
                    return bank[n % BANKS]

                ident = w["ident"]
                pe.wait_ge(consts, 3)
                for n in range(len(GATE_WEIGHTS)):
                    b = start()
                    pe.wait_ge(nat_in[n % 2], 16 * (n // 2 + 1))
                    for ic in range(CC):
                        for mc in range(CC):
                            mm = pe.transpose(b[:, ic * D + mc * P:ic * D + mc * P + P],
                                              nat[:, n % 2, mc, ic * P:(ic + 1) * P], ident[:])
                    mm.then_inc(written, 1)
                pe.wait_ge(loaded, 16 * n_loads)
                b = start()
                for ic in range(CC):
                    mm = pe.transpose(b[:, ic * E:(ic + 1) * E], cen[:, ic * P:(ic + 1) * P], ident[:E, :E])
                mm.then_inc(written, 1)
                for j in range(0, PAIRS, 2):
                    b = start()
                    for jj in range(2):
                        for cc in range(CC):
                            mm = pe.transpose(b[:, jj * D + cc * P:jj * D + cc * P + P],
                                              wq1[:, cc, (j + jj) * P:(j + jj + 1) * P], ident[:])
                    mm.then_inc(written, 1)
                for j in range(0, PAIRS, 4):
                    b = start()
                    for jj in range(4):
                        mm = pe.transpose(b[:, jj * P:(jj + 1) * P], wk1[:, (j + jj) * P:(j + jj + 1) * P], ident[:])
                    mm.then_inc(written, 1)
                pe.wait_ge(evacuated, used[0])
                for j in range(0, PAIRS, 2):
                    for hh in range(2):
                        b = start()
                        r = slice(DK1 * hh, DK1 * (hh + 1))
                        for cc in range(CC):
                            for jj in range(2):
                                mm = pe.matmul(b[:, (cc * 2 + jj) * P:(cc * 2 + jj + 1) * P],
                                               wq1T[r, j + jj, cc * P:(cc + 1) * P], wk1T[r, j + jj, :], start=True, stop=True)
                        mm.then_inc(written, 1)

            @block.vector
            def _(dve):
                nc.vector.memset(w["cT"][:], 0.0).then_inc(state, 1)
                used = [0]

                def evacuate(dst, n, parts=()):
                    b = bank[used[0] % BANKS]
                    used[0] += 1
                    dve.wait_ge(written, used[0])
                    src = b[:, 0:n]
                    if parts:
                        src = src.rearrange("p (c j d) -> p c j d", c=parts[0], j=parts[1])
                    nc.vector.tensor_copy(dst, src).then_inc(evacuated, 1)

                for name in GATE_WEIGHTS:
                    evacuate(flat(w[name + "T"][:]), CC * D)
                evacuate(flat(w["cenT"][:]), CC * E)
                for j in range(0, PAIRS, 2):
                    evacuate(flat(wq1T[:, j:j + 2, :]), 2 * D)
                for j in range(0, PAIRS, 4):
                    evacuate(flat(wk1T[:, j:j + 4, :]), 4 * P)
                for j in range(0, PAIRS, 2):
                    for hh in range(2):
                        evacuate(w["mqk"][:, :, 2 * j + hh:2 * j + hh + 3:2, :], 512, (CC, 2))
                dve.wait_ge(g_ready, 1)
                for n in range(2):
                    nc.vector.tensor_scalar(w["tgbo"][n][:], bo_raw[:, n, :], w["g_tanh"][:, n:n + 1], None, ALU.mult).then_inc(scaled, 1)
                nc.vector.tensor_scalar(w["gate_bias"][:, 0:2, :], w["gate_bias"][:, 0:2, :], 0.5, None, ALU.mult).then_inc(scaled, 1)
                nc.vector.tensor_scalar(w["bq0"][:], w["bq0"][:], float(DK0) ** -0.5, None, ALU.mult).then_inc(scaled, 1)
                dve.wait_ge(state, 1)
                for c in range(CC):
                    nc.vector.tensor_scalar(w["cT"][:, c, :], w["cT"][:, c, :], in_c[:, c:c + 1], None, ALU.add).then_inc(scaled, 1)
                dve.wait_ge(more, 5)
                nc.vector.tensor_scalar(w["region"][:], region_i[:], 8.0, 1.0, ALU.mult, ALU.add).then_inc(scaled, 1)
                dve.wait_ge(scaled, 5 + CC)


def attention_phase(nc, t, w, bank, x1pre_d, layer, parts_d=None, rows_d=None, X3=None, wdn=None):
    A = layer == 0
    x, ctx = t["x"], t["ctx_512"]
    NB, NQ, D = x.shape
    NK = ctx.shape[1]
    H, CC = 16, D // P
    DK0, DK1 = D // H, t["L1_xattn_Wq"].shape[1] // H
    PAIRS = H * DK1 // P
    KP = 125
    KC = NK // KP
    E = t["L1_ffn_W_up"].shape[0]
    NG = H // GH
    GV = 8 if A else GH
    NV = H // GV
    assert D == 2 * P and ctx.shape[2] == P and KP * KC == NK and GH * NQ <= 512 and DK1 == 64
    uses = Uses(ORDER_A if A else ORDER_C, NB)
    s_bank, pt_bank, pv_bank, misc = bank[0:3], bank[3:5], bank[5:7], bank[7]
    S_OF = [h % 3 for h in range(H - 1)] + [1]
    ident, g_tanh = w["ident"], w["g_tanh"]
    N_ROUTER = 11
    N_PLACED = 5 + TOP_K

    def loads(j, par):
        return (j - par) * 8 + 16

    def scores_bank_last(h):
        before = [k for k in range(h) if S_OF[k] == S_OF[h]]
        return before[-1] if before else max(k for k in range(H) if S_OF[k] == S_OF[h]) - H

    with ExitStack() as es:
        def sb(name, shape):
            return es.enter_context(nc.sbuf_tensor(f"{name}_{layer}", shape, F32))

        def sem(name):
            return es.enter_context(nc.semaphore(f"{name}_{layer}"))

        if A:
            NKP = -(-NK // 8) * 8
            kS = [es.enter_context(nc.sbuf_tensor(f"kS{n}", [P, H, NKP], BF16)) for n in range(2)]
            qS = [es.enter_context(nc.sbuf_tensor(f"qS{n}", [P, H, NQ], BF16)) for n in range(2)]
            kT, qT = sb("kT", [P, CC, NK]), sb("qT", [P, CC, NQ])
            k_rest, q_rest = sb("k_rest", [P, CC, NK]), sb("q_rest", [P, CC, NQ])
            k_parts = es.enter_context(nc.sbuf_tensor("k_parts", [P, PARTS, CC, NKP], BF16))
            q_parts = es.enter_context(nc.sbuf_tensor("q_parts", [P, PARTS, CC, NQ], BF16))
            k_parts_d, q_parts_d = parts_d
        else:
            qs = [sb(f"qs{n}", [P, H, NQ]) for n in range(2)]
            kT = [sb(f"kT{n}", [P, NK]) for n in range(2)]
        ctxn = [sb(f"ctxn{n}", [KP, KC, P]) for n in range(2)]
        xt = [sb(f"xt{n}", [NQ, D if A else 2 * D]) for n in range(2)]
        xres = [sb(f"xres{n}", [NQ, D]) for n in range(2)]
        xln, x1ln = sb("xln", [NQ, D]), sb("x1ln", [NQ, D])
        xT, x1T = sb("xT", [P, CC, NQ]), sb("x1T", [P, CC, NQ])
        stage = sb("stage", [NQ, 2 * D])
        prob = sb("prob", [NQ, RING, NK + 1])
        pT = sb("pT", [KP, RING, KC * NQ])
        oT = [sb(f"oT{n}", [P, NV if A else PAIRS, NQ]) for n in range(2)]
        stats, spare = sb("stats", [NQ, 2, 16]), sb("spare", [NQ, 2])
        pool_spare, pool_spare_set = sb("pool_spare", [NQ, 8]), sem("pool_spare_set")
        nmax, rsum, rinv = sb("nmax", [NQ, RING]), sb("rsum", [NQ, RING]), sb("rinv", [NQ, RING])
        if A:
            vals = [sb(f"vals{n}", [KP, KC, H, 32]) for n in range(2)]
            ctxT = sb("ctxT", [P, NK])
            gates, upd = sb("gates", [P, 3, CC, NQ]), sb("upd", [P, 3, CC * NQ])
        else:
            agg = [sb(f"agg{n}", [P, GH * NQ]) for n in range(2)]
            h_in, h_out = sb("h_in", [NQ, D]), sb("h_out", [NQ, D])
            rt, rts = sb("rt", [NQ, 8, E]), sb("rts", [NQ, 16])
            z, sig, hs = sb("z", [P, NQ]), sb("sig", [P, 2, NQ]), sb("hs", [P, NQ])
            placing, w8 = sb("placing", [NQ, 2 + TOP_K, E]), sb("w8", [NQ, 2 * TOP_K])
            slot_w = sb("slot_w", [NQ, TOP_K])
            ids = es.enter_context(nc.sbuf_tensor("ids", [NQ, TOP_K], U32))
            numbers = es.enter_context(nc.sbuf_tensor("numbers", [NQ, TOP_K], I32))
            rows = sb("rows", [NQ, TOP_K, D + 2])

        x_in, ctx_in = ([sem(f"{a}{n}") for n in range(2)] for a in ("x_in", "ctx_in"))
        stored = sem("stored")
        scored, maxed, exped, inverted, normed = sem("scored"), sem("maxed"), sem("exped"), sem("inverted"), sem("normed")
        turned, pT_ready, valued, group_out = sem("turned"), sem("pT_ready"), sem("valued"), sem("group_out")
        misc_full, misc_free = sem("misc_full"), sem("misc_free")
        x_stats, x_rstd, x_normed, xres_ready = sem("x_stats"), sem("x_rstd"), sem("x_normed"), sem("xres_ready")
        y_stats, y_rstd, y_normed = sem("y_stats"), sem("y_rstd"), sem("y_normed")
        spare_set = sem("spare_set")
        k_split, q_split, updated, padded = sem("k_split"), sem("q_split"), sem("updated"), sem("padded")
        k_out, q_out = [sem(f"k_out{c}") for c in range(CC)], sem("q_out")
        k_in, q_in = [[sem(f"k_in{c}{n}") for n in range(2)] for c in range(CC)], [sem(f"q_in{n}") for n in range(2)]
        h_in_ready, h_ready, x2_ready = sem("h_in_ready"), sem("h_ready"), sem("x2_ready")
        routed, sig_exp, kept = sem("routed"), sem("sig_exp"), sem("kept")
        placed, scattered, shared, shared_exp = sem("placed"), sem("scattered"), sem("shared"), sem("shared_exp")
        wdn_in, numbered, renumbered, weighted = sem("wdn_in"), sem("numbered"), sem("renumbered"), sem("weighted")

        with nc.Block() as block:

            @block.sync
            def _(sp):
                def load(j, par):
                    wait(sp, x_normed, j - 1)
                    wait(sp, xres_ready, j - 1)
                    sp.dma_start(xt[par][:], seq(x if A else x1pre_d, j)).then_inc(x_in[par], 16)
                    if A:
                        wait(sp, misc_free, uses.out(j - 2, "ctxT"))
                    else:
                        wait(sp, valued, H * (j - 1))
                    sp.dma_start(ctxn[par][:], ctx[bass.ds(j, 1)].rearrange("o (c p) d -> p (o c) d", p=KP)).then_inc(ctx_in[par], 16)

                def store(p):
                    sp.wait_ge(misc_free, uses.out(p, "h_in"))
                    sp.dma_start(seq(x1pre_d, p), stage[:]).then_inc(stored, 16)

                def stack_k(j, par, c):
                    sp.wait_ge(k_split, 6 * j + (3 * c + 3))
                    sp.dma_start(k_parts_d[par][:, c].rearrange("a p n -> p a n")[:, :, :NK], k_parts[:, :, c, :NK]).then_inc(k_out[c], 16)
                    sp.wait_ge(k_out[c], 16 * j + 16)
                    for k, (part, _) in enumerate(STACK):
                        sp.dma_start(kS[par][DK0 * k:DK0 * (k + 1), 8 * c:8 * c + 8, :NK],
                                     k_parts_d[par][part, c].rearrange("(h d) n -> d h n", d=DK0)[:, :, :NK]).then_inc(k_in[c][par], 16)

                def stack_q(j, par):
                    sp.wait_ge(q_split, 3 * j + 3)
                    sp.dma_start(q_parts_d[par].rearrange("a c p n -> p (a c) n"), q_parts[:].rearrange("p a c n -> p (a c) n")).then_inc(q_out, 16)
                    sp.wait_ge(q_out, 16 * j + 16)
                    for k, (_, part) in enumerate(STACK):
                        sp.dma_start(qS[par][DK0 * k:DK0 * (k + 1), :, :],
                                     q_parts_d[par][part].rearrange("c (h d) n -> d (c h) n", d=DK0)).then_inc(q_in[par], 16)

                def stack_all(j, par):
                    wait(sp, scored, H * j - H)
                    stack_k(j, par, 0)
                    stack_q(j, par)
                    stack_k(j, par, 1)

                load(0, 0)
                load(1, 1)
                if A:
                    stack_all(0, 0)
                if not A:
                    for e in range(0, E, 8):
                        sp.dma_start(wdn[:, e:e + 8, :], t["L1_ffn_W_down"][e:e + 8].rearrange("e p d -> p e d")).then_inc(wdn_in, 16)

                def body(i, par, first, last):
                    if not (isinstance(i, int) and i + 2 >= NB):
                        load(i + 2, par)
                    if A and not last:
                        stack_all(i + 1, 1 - par)
                    if A and not first:
                        store(i - 1)

                walk(nc.sync, NB, body)
                if A:
                    store(NB - 1)
                    sp.wait_ge(stored, 16 * NB)
                else:
                    sp.wait_ge(wdn_in, 16 * (E // 8))

            @block.tensor
            def _(pe):
                def scores(i, par, h):
                    wait(pe, exped, H * i + scores_bank_last(h) + 1)
                    if h and h % GH == 0 and not A:
                        pe.wait_ge(misc_free, uses.out(i, f"q{h // GH}"))
                    if A and h == H // 2:
                        pe.wait_ge(k_in[1][par], (i - par) * (8 * len(STACK)) + 16 * len(STACK))
                    if h == 0:
                        if A:
                            for arrived in (q_in[par], k_in[0][par]):
                                pe.wait_ge(arrived, (i - par) * (8 * len(STACK)) + 16 * len(STACK))
                        else:
                            pe.wait_ge(misc_free, uses.out(i, "q0"))
                    pe.matmul(s_bank[S_OF[h]][:NQ, :NK], (qS if A else qs)[par][:, h, :], kS[par][:, h, :NK] if A else kT[par][:],
                              start=True, stop=True).then_inc(scored, 1)

                def turn(i, h):
                    wait(pe, pT_ready, H * i + h - 1)
                    pe.wait_ge(normed, H * i + h + 1)
                    for c in range(KC):
                        mm = pe.transpose(pt_bank[h % 2][:KP, c * NQ:(c + 1) * NQ],
                                          prob[:, h % RING, c * KP:(c + 1) * KP], ident[:NQ, :NQ])
                    mm.then_inc(turned, 1)

                def values(i, par, h):
                    g = h // GV
                    b = pv_bank[g % 2]
                    if h % GV == 0:
                        wait(pe, group_out, NV * i + g - 1)
                    if h == 0 and A:
                        pe.wait_ge(misc_free, uses.out(i, "v2"))
                    pe.wait_ge(pT_ready, H * i + h + 1)
                    for c in range(KC):
                        rhs = pT[:, h % RING, c * NQ:(c + 1) * NQ]
                        if A:
                            o = 32 * (h % GV // 2)
                            mm = pe.matmul(b[o:o + 32, 0:NQ], vals[par][:, c, h, :], rhs,
                                           start=(c == 0 and h % 2 == 0), stop=(c == KC - 1 and h % 2 == 1))
                        else:
                            mm = pe.matmul(b[:, (h % GH) * NQ:(h % GH + 1) * NQ], ctxn[par][:, c, :], rhs,
                                           start=(c == 0), stop=(c == KC - 1))
                    mm.then_inc(valued, 1)

                def use(n):
                    wait(pe, misc_free, n)

                def transposed(src, ready):
                    def f(j, par, n):
                        use(n)
                        pe.wait_ge(ready, j + 1)
                        for c in range(CC):
                            mm = pe.transpose(misc[:, c * NQ:(c + 1) * NQ], src[:, c * P:(c + 1) * P], ident[:NQ, :NQ])
                        mm.then_inc(misc_full, 1)
                    return f

                def q(j, par, n):
                    use(n)
                    for m in range(CC):
                        for c in range(CC):
                            mm = pe.matmul(misc[:, m * NQ:(m + 1) * NQ], w["wq0"][:, c, m * P:(m + 1) * P], xT[:, c, :],
                                           start=(c == 0), stop=(c == CC - 1))
                    mm.then_inc(misc_full, 1)

                def ctx_transposed(j, par, n):
                    use(n)
                    pe.wait_ge(ctx_in[par], loads(j, par))
                    for c in range(KC):
                        mm = pe.transpose(misc[:, c * KP:(c + 1) * KP], ctxn[par][:, c, :], ident[:KP, :KP])
                    mm.then_inc(misc_full, 1)

                def k(m):
                    def f(j, par, n):
                        use(n)
                        pe.matmul(misc[:, :NK], w["wk0"][:, m * P:(m + 1) * P], ctxT[:], start=True, stop=True).then_inc(misc_full, 1)
                    return f

                def v(cs):
                    def f(j, par, n):
                        use(n)
                        for a, c in enumerate(cs):
                            mm = pe.matmul(misc[:KP, a * D:(a + 1) * D], ctxT[:, c * KP:(c + 1) * KP], w["wv0"][:],
                                           start=True, stop=True)
                        mm.then_inc(misc_full, 1)
                    return f

                def wo(p, par, n):
                    use(n)
                    if A:
                        pe.wait_ge(group_out, NV * (p + 1))
                    weights, parts = (w["wo0"], NV) if A else (w["wo1"], PAIRS)
                    for c in range(parts):
                        mm = pe.matmul(misc[:NQ, :D], oT[par][:, c, :], weights[:, c, :], start=(c == 0), stop=(c == parts - 1))
                    mm.then_inc(misc_full, 1)

                def gate(g):
                    def f(p, par, n):
                        use(n)
                        wait(pe, updated, 4 * p)
                        for m in range(CC):
                            o = misc[:, m * NQ:(m + 1) * NQ]
                            for c in range(CC):
                                pe.matmul(o, w[f"w{g}T"][:, c, m * P:(m + 1) * P], x1T[:, c, :], start=(c == 0), stop=False)
                            for c in range(CC):
                                mm = pe.matmul(o, w[f"u{g}T"][:, c, m * P:(m + 1) * P], w["cT"][:, c, :], start=False, stop=(c == CC - 1))
                        mm.then_inc(misc_full, 1)
                    return f

                def h_into(p, par, n):
                    use(n)
                    for c in range(CC):
                        mm = pe.matmul(misc[:NQ, :D], x1T[:, c, :], w["woT"][:, c, :], start=(c == 0), stop=(c == CC - 1))
                    mm.then_inc(misc_full, 1)

                def qh(g):
                    def f(j, par, n):
                        use(n)
                        for a in range(GH):
                            for c in range(CC):
                                mm = pe.matmul(misc[:, a * NQ:(a + 1) * NQ], w["mqk"][:, c, g * GH + a, :], xT[:, c, :],
                                               start=(c == 0), stop=(c == CC - 1))
                        mm.then_inc(misc_full, 1)
                    return f

                def head_out(g):
                    def f(i, par, n):
                        use(n)
                        pe.wait_ge(group_out, NG * i + g + 1)
                        for a in range(GH):
                            h, o = g * GH + a, DK1 * (a % 2)
                            mm = pe.matmul(misc[o:o + DK1, (a // 2) * NQ:(a // 2 + 1) * NQ], w["wv1"][:, h * DK1:(h + 1) * DK1],
                                           agg[g % 2][:, a * NQ:(a + 1) * NQ], start=True, stop=True)
                        mm.then_inc(misc_full, 1)
                    return f

                def router(p, par, n):
                    use(n)
                    for c in range(CC):
                        mm = pe.matmul(misc[:NQ, :E], x1T[:, c, :], w["cenT"][:, c, :], start=(c == 0), stop=(c == CC - 1))
                    mm.then_inc(misc_full, 1)

                def rank(p, par, n):
                    use(n)
                    pe.wait_ge(routed, N_ROUTER * (p + 1))
                    wait(pe, placed, N_PLACED * p)
                    pe.matmul(misc[:NQ, :E], w["earlier"][:NQ, :NQ], rt[:, 4, :], start=True, stop=False)
                    pe.matmul(misc[:NQ, :E], w["ones"][:NQ, :NQ], w["chosen"][:], start=False, stop=True).then_inc(misc_full, 1)

                def shared_up(p, par, n):
                    use(n)
                    for c in range(CC):
                        mm = pe.matmul(misc[:, :NQ], w["sup"][:, c, :], x1T[:, c, :], start=(c == 0), stop=(c == CC - 1))
                    mm.then_inc(misc_full, 1)

                def shared_down(p, par, n):
                    use(n)
                    pe.wait_ge(shared, 3 * (p + 1))
                    pe.matmul(misc[:NQ, :D], hs[:], w["sdn"][:], start=True, stop=True).then_inc(misc_full, 1)

                hooks = {"xT": transposed(xln, x_normed), "ctxT": ctx_transposed, "wo": wo, "lnT": transposed(x1ln, y_normed)}
                if A:
                    hooks |= {"q": q, "k0": k(0), "k1": k(1), "v01": v((0, 1)), "v2": v((2,)),
                              "gate_f": gate("f"), "gate_i": gate("i"), "gate_g": gate("c"), "h_in": h_into}
                else:
                    hooks |= {"router": router, "rank": rank, "shared_up": shared_up, "shared_down": shared_down}
                    hooks |= {f"q{g}": qh(g) for g in range(NG)} | {f"ho{g}": head_out(g) for g in range(NG)}

                uses.run(hooks, -1, None, 1, first=True)
                if A:
                    pe.wait_ge(padded, 2)
                for h in range(LEAD):
                    scores(0, 0, h)

                def body(i, par, first, last):
                    for h in range(H):
                        if h + LEAD < H:
                            scores(i, par, h + LEAD)
                        elif not last:
                            scores(i + 1, 1 - par, h + LEAD - H)
                        turn(i, h)
                        if A:
                            uses.run(hooks, i, h, par, first, last)
                        if h:
                            values(i, par, h - 1)
                        elif not first:
                            values(i - 1, 1 - par, H - 1)
                        if not A:
                            uses.run(hooks, i, h, par, first, last)

                walk(nc.tensor, NB, body)
                values(NB - 1, 1, H - 1)
                uses.run(hooks, NB, None, 0, last=True)
                if A:
                    pe.wait_ge(updated, 4 * NB)
                    use(uses.out(NB - 1, "h_in"))
                    for c in range(CC):
                        mm = pe.matmul(misc[:NQ, :D], w["cT"][:, c, :], w["uoT"][:, c, :], start=(c == 0), stop=(c == CC - 1))
                    mm.then_inc(misc_full, 1)

            def full(eng, n):
                eng.wait_ge(misc_full, n + 1)

            @block.scalar
            def _(act):
                def exponentials(i, h):
                    r = h % RING
                    act.wait_ge(maxed, H * i + h + 1)
                    wait(act, turned, H * i + h + 1 - RING)
                    nc.scalar.activation(prob[:, r, :NK], s_bank[S_OF[h]][:NQ, :NK], ACT.Exp, bias=nmax[:, r:r + 1],
                                         accum_out=rsum[:, r:r + 1]).then_inc(exped, 1)

                def keep_turned(i, h):
                    act.wait_ge(turned, H * i + h + 1)
                    wait(act, valued, H * i + h + 1 - RING)
                    nc.scalar.copy(pT[:, h % RING, :], pt_bank[h % 2][:KP, :KC * NQ]).then_inc(pT_ready, 1)

                def group(i, par, g):
                    act.wait_ge(valued, H * i + GV * (g + 1))
                    if A:
                        wait(act, misc_free, uses.out(i - 2, "wo"))
                        nc.scalar.copy(oT[par][:, g, :], pv_bank[g % 2][:, :NQ]).then_inc(group_out, 1)
                    else:
                        wait(act, misc_free, uses.out(i - 1, f"ho{g + 2}") if g < 2 else uses.out(i, f"ho{g - 2}"))
                        nc.scalar.copy(agg[g % 2][:], pv_bank[g % 2][:, :GH * NQ]).then_inc(group_out, 1)

                def q(j, par, n):
                    full(act, n)
                    wait(act, q_out, 16 * j)
                    for c in range(CC):
                        for dst in (qT[:, c, :], q_parts[:, 0, c, :]):
                            a = nc.scalar.activation(dst, misc[:, c * NQ:(c + 1) * NQ], ACT.Identity,
                                                     bias=w["bq0"][:, c:c + 1], scale=float(DK0) ** -0.5)
                    a.then_inc(misc_free, 1)

                def k(m):
                    def f(j, par, n):
                        full(act, n)
                        wait(act, k_out[m], 16 * j)
                        for dst in (kT[:, m, :], k_parts[:, 0, m, :NK]):
                            ins = nc.scalar.activation(dst, misc[:, :NK], ACT.Identity, bias=w["bk0"][:, m:m + 1])
                        ins.then_inc(misc_free, 1)
                    return f

                def gate(g):
                    def f(p, par, n):
                        full(act, n)
                        wait(act, updated, 4 * p)
                        for m in range(CC):
                            ins = nc.scalar.activation(gates[:, g, m, :], misc[:, m * NQ:(m + 1) * NQ], ACT.Tanh,
                                                       bias=w["gate_bias"][:, g, m:m + 1], scale=0.5 if g < 2 else 1.0)
                        ins.then_inc(misc_free, 1)
                    return f

                def h_into(p, par, n):
                    full(act, n)
                    wait(act, stored, 16 * p)
                    nc.scalar.copy(stage[:, D:2 * D], misc[:NQ, :D]).then_inc(misc_free, 1)

                def qh(g):
                    def f(j, par, n):
                        full(act, n)
                        wait(act, scored, H * (j - 1))
                        nc.scalar.activation(flat(qs[par][:, g * GH:(g + 1) * GH, :]), misc[:, :GH * NQ], ACT.Copy,
                                             scale=float(DK1) ** -0.5).then_inc(misc_free, 1)
                    return f

                def tanh_h(j):
                    act.wait_ge(h_in_ready, j + 1)
                    wait(act, x2_ready, j)
                    nc.scalar.activation(h_out[:], h_in[:], ACT.Tanh).then_inc(h_ready, 1)

                def sigmoid_exp(p):
                    act.wait_ge(routed, N_ROUTER * p + 1)
                    nc.scalar.activation(rt[:, 1, :], rt[:, 0, :], ACT.Exp, scale=-1.0).then_inc(sig_exp, 1)

                def shared_exps(p, par, n):
                    full(act, n)
                    wait(act, shared, 3 * p)
                    nc.scalar.copy(z[:], misc[:, :NQ]).then_inc(misc_free, 1)
                    act.wait_ge(misc_free, n + 1)
                    nc.scalar.activation(sig[:, 0, :], z[:], ACT.Exp, scale=-1.0).then_inc(shared_exp, 1)

                if A:
                    hooks = {"q": q, "k0": k(0), "k1": k(1), "gate_f": gate(0), "gate_i": gate(1), "gate_g": gate(2), "h_in": h_into}
                else:
                    hooks = {f"q{g}": qh(g) for g in range(NG)}
                    hooks["router"] = lambda p, par, n: sigmoid_exp(p)
                    hooks["shared_up"] = shared_exps
                    tanh_h(0)
                uses.run(hooks, -1, None, 1, first=True)
                for h in range(LEAD):
                    exponentials(0, h)

                def body(i, par, first, last):
                    for h in range(H):
                        keep_turned(i, h)
                        if h + LEAD < H:
                            exponentials(i, h + LEAD)
                        elif not last:
                            exponentials(i + 1, h + LEAD - H)
                        if h and h % GV == 0:
                            group(i, par, h // GV - 1)
                        if h == 0 and not first:
                            group(i - 1, 1 - par, NV - 1)
                        if not A and h == 1 and not last:
                            tanh_h(i + 1)
                        uses.run(hooks, i, h, par, first, last)

                walk(nc.scalar, NB, body)
                group(NB - 1, 1, NV - 1)
                uses.run(hooks, NB, None, 0, last=True)

            @block.vector
            def _(dve):
                def maximum(i, h):
                    r = h % RING
                    dve.wait_ge(scored, H * i + h + 1)
                    nc.vector.tensor_reduce(nmax[:, r:r + 1], s_bank[S_OF[h]][:NQ, :NK], AX, ALU.max, negate=True).then_inc(maxed, 1)

                def normalise(i, h):
                    r = h % RING
                    dve.wait_ge(exped, H * i + h + 1)
                    nc.vector.reciprocal(rinv[:, r:r + 1], rsum[:, r:r + 1]).then_inc(inverted, 1)
                    dve.wait_ge(inverted, H * i + h + 1)
                    nc.vector.tensor_scalar(prob[:, r, :NK], prob[:, r, :NK], rinv[:, r:r + 1], None, ALU.mult).then_inc(normed, 1)

                def moments(src, st, j, counted):
                    nc.vector.bn_stats(st[:, 0:6], src).then_inc(counted, 1)
                    wait_apart(dve, counted, 3 * j + 1, spare)
                    nc.vector.bn_aggr(st[:, 6:8], st[:, 0:6]).then_inc(counted, 1)
                    dve.wait_ge(counted, 3 * j + 2)
                    nc.vector.tensor_scalar(st[:, 8:9], st[:, 7:8], LN_EPS, None, ALU.add).then_inc(counted, 1)

                def norm(src, dst, st, j, rstd, done):
                    dve.wait_ge(rstd, j + 1)
                    nc.vector.tensor_scalar(dst[:], src, st[:, 6:7], st[:, 9:10], ALU.subtract, ALU.mult).then_inc(done, 1)

                def h_sum(j, par):
                    dve.wait_ge(x_in[par], loads(j, par))
                    wait(dve, h_ready, j)
                    nc.vector.tensor_tensor(h_in[:], xt[par][:, D:2 * D], w["cf"][:NQ, :], ALU.add).then_inc(h_in_ready, 1)

                def moments_x(j, par):
                    src = xt[par][:, 0:D]
                    if A:
                        dve.wait_ge(x_in[par], loads(j, par))
                    else:
                        dve.wait_ge(h_ready, j + 1)
                        nc.vector.scalar_tensor_tensor(out=src, in0=h_out[:], scalar=g_tanh[:NQ, 2:3], in1=src,
                                                       op0=ALU.mult, op1=ALU.add).then_inc(x2_ready, 1)
                        dve.wait_ge(x2_ready, j + 1)
                    moments(src, stats[:, 0, :], j, x_stats)

                def norm_x(j, par):
                    norm(xt[par][:, 0:D], xln, stats[:, 0, :], j, x_rstd, x_normed)

                def moments_y(p):
                    dve.wait_ge(misc_free, uses.out(p, "wo"))
                    moments(stage[:, 0:D], stats[:, 1, :], p, y_stats)

                def norm_y(p):
                    if not A:
                        wait(dve, kept, p)
                    norm(stage[:, 0:D], x1ln, stats[:, 1, :], p, y_rstd, y_normed)

                def split_q(j, par):
                    dve.wait_ge(misc_free, uses.out(j, "q"))
                    for dst in (q_rest[:], q_parts[:, 1]):
                        nc.vector.tensor_tensor(dst, qT[:], q_parts[:, 0], ALU.subtract).then_inc(q_split, 1)
                    dve.wait_ge(q_split, 3 * j + 2)
                    nc.vector.tensor_tensor(q_parts[:, 2], q_rest[:], q_parts[:, 1], ALU.subtract).then_inc(q_split, 1)

                def keep_xT(j, par, n):
                    full(dve, n)
                    nc.vector.tensor_copy(flat(xT[:]), misc[:, :CC * NQ]).then_inc(misc_free, 1)

                def keep_ctxT(j, par, n):
                    full(dve, n)
                    if not A:
                        wait(dve, scored, H * (j - 1))
                    nc.vector.tensor_copy(ctxT[:] if A else kT[par][:], misc[:, :NK]).then_inc(misc_free, 1)

                def keep_v(cs):
                    def f(j, par, n):
                        full(dve, n)
                        if isinstance(j, int) and j == 0:
                            dve.wait_ge(padded, 2)
                        wait(dve, valued, H * (j - 1))
                        for a, c in enumerate(cs):
                            for odd in range(2):
                                def heads(v):
                                    return v.rearrange("p (h two d) -> p h two d", two=2, d=DK0)[:, :, odd, :]
                                ins = nc.vector.tensor_tensor(vals[par][:, c, odd:H:2, DK0 * odd:DK0 * (odd + 1)],
                                                              heads(misc[:KP, a * D:(a + 1) * D]), heads(w["bv0"][:KP, 0:D]), ALU.add)
                        ins.then_inc(misc_free, 1)
                    return f

                def residual(p, par, n):
                    full(dve, n)
                    dve.wait_ge(xres_ready, p + 1)
                    if A:
                        wait(dve, stored, 16 * p)
                    nc.vector.scalar_tensor_tensor(out=stage[:, 0:D], in0=misc[:NQ, :D], scalar=g_tanh[:NQ, layer:layer + 1],
                                                   in1=xres[par][:], op0=ALU.mult, op1=ALU.add).then_inc(misc_free, 1)

                def keep_lnT(p, par, n):
                    full(dve, n)
                    nc.vector.tensor_copy(flat(x1T[:]), misc[:, :CC * NQ]).then_inc(misc_free, 1)

                def update_terms(p):
                    dve.wait_ge(misc_free, uses.out(p, "gate_g"))
                    f, i, g = (flat(gates[:, a]) for a in range(3))
                    c = flat(w["cT"][:])
                    nc.vector.scalar_tensor_tensor(out=upd[:, 0, :], in0=f, scalar=1.0, in1=c, op0=ALU.add, op1=ALU.mult).then_inc(updated, 1)
                    nc.vector.scalar_tensor_tensor(out=upd[:, 1, :], in0=i, scalar=1.0, in1=g, op0=ALU.add, op1=ALU.mult).then_inc(updated, 1)

                def update(p):
                    dve.wait_ge(updated, 4 * p + 2)
                    nc.vector.tensor_tensor(upd[:, 2, :], upd[:, 0, :], upd[:, 1, :], ALU.add).then_inc(updated, 1)
                    dve.wait_ge(updated, 4 * p + 3)
                    nc.vector.tensor_scalar(flat(w["cT"][:]), upd[:, 2, :], 0.5, None, ALU.mult).then_inc(updated, 1)

                def keep_heads(g):
                    def f(i, par, n):
                        full(dve, n)
                        wait(dve, misc_free, uses.out(i - 2, "wo"))
                        nc.vector.tensor_copy(flat(oT[par][:, 2 * g:2 * g + 2, :]), misc[:, :2 * NQ]).then_inc(misc_free, 1)
                    return f

                def counter(semaphore, total, p, before):
                    done = [before]

                    def step(ins, apart=True):
                        ins.then_inc(semaphore, 1)
                        done[0] += 1
                        if apart:
                            wait_apart(dve, semaphore, total * p + done[0], spare)
                        else:
                            dve.wait_ge(semaphore, total * p + done[0])
                    return step

                def keep_affinity(p, par, n):
                    full(dve, n)
                    nc.vector.tensor_copy(rt[:, 0, :], misc[:NQ, :E]).then_inc(misc_free, 1)
                    dve.wait_ge(misc_free, n + 1)
                    nc.vector.tensor_copy(rts[:, 11:12], rt[:, 0, 0:1]).then_inc(routed, 1)
                    step = counter(routed, N_ROUTER, p, 1)
                    dve.wait_ge(routed, N_ROUTER * p + 1)
                    step(nc.vector.tensor_tensor(rt[:, 2, :], rt[:, 0, :], w["ebias"][:NQ, :], ALU.add))

                def choose(p):
                    step = counter(routed, N_ROUTER, p, 2)
                    step(nc.vector.max(rts[:, 0:TOP_K], rt[:, 2, :]))
                    step(nc.vector.match_replace(rt[:, 3, :], rts[:, 0:TOP_K], rt[:, 2, :], GONE))
                    step(nc.vector.tensor_tensor(rt[:, 4, :], rt[:, 3, :], rt[:, 2, :], ALU.not_equal), False)

                def sigmoids(p):
                    step = counter(routed, N_ROUTER, p, 5)
                    dve.wait_ge(sig_exp, p + 1)
                    step(nc.vector.tensor_scalar(rt[:, 5, :], rt[:, 1, :], 1.0, None, ALU.add), False)
                    step(nc.vector.reciprocal(rt[:, 7, :], rt[:, 5, :]), False)
                    step(nc.vector.scalar_tensor_tensor(out=rt[:, 5, :], in0=rt[:, 7, :], scalar=1.0, in1=rt[:, 4, :],
                                                        op0=ALU.mult, op1=ALU.mult, accum_out=rts[:, 8:9]), False)

                def weigh(p):
                    step = counter(routed, N_ROUTER, p, 8)
                    step(nc.vector.tensor_scalar(rts[:, 9:10], rts[:, 8:9], 1e-8, None, ALU.add), False)
                    step(nc.vector.reciprocal(rts[:, 10:11], rts[:, 9:10]), False)
                    nc.vector.tensor_scalar(rt[:, 6, :], rt[:, 5, :], rts[:, 10:11], None, ALU.mult).then_inc(routed, 1)

                def place(p, par, n):
                    full(dve, n)
                    nc.vector.tensor_tensor(placing[:, 0, :], misc[:NQ, :E], w["region"][:NQ, :], ALU.add).then_inc(misc_free, 1)
                    dve.wait_ge(misc_free, n + 1)
                    step = counter(placed, N_PLACED, p, 0)
                    step(nc.vector.tensor_tensor(placing[:, 1, :], placing[:, 0, :], rt[:, 4, :], ALU.mult))
                    step(nc.vector.max(w8[:, 0:TOP_K], placing[:, 1, :]), False)

                def pick(p, ks):
                    for k in ks:
                        nc.vector.scalar_tensor_tensor(out=placing[:, 2 + k, :], in0=placing[:, 1, :], scalar=w8[:, k:k + 1], in1=rt[:, 6, :],
                                                       op0=ALU.is_equal, op1=ALU.mult,
                                                       accum_out=w8[:, TOP_K + k:TOP_K + k + 1]).then_inc(placed, 1)

                def place_end(p):
                    nc.vector.tensor_tensor(w["chosen"][:], w["chosen"][:], rt[:, 4, :], ALU.add).then_inc(placed, 1)
                    wait(dve, scattered, 16 * TOP_K * p)
                    nc.vector.tensor_scalar(ids[:], w8[:, 0:TOP_K], -1.0, None, ALU.add).then_inc(placed, 1)
                    dve.wait_ge(placed, N_PLACED * p + N_PLACED - 1)
                    nc.vector.tensor_scalar(slot_w[:], w8[:, TOP_K:], g_tanh[:NQ, 3:4], None, ALU.mult).then_inc(placed, 1)

                def shared_silu(p):
                    dve.wait_ge(shared_exp, p + 1)
                    wait(dve, misc_free, uses.out(p - 1, "shared_down"))
                    nc.vector.tensor_scalar(sig[:, 1, :], sig[:, 0, :], 1.0, None, ALU.add).then_inc(shared, 1)
                    dve.wait_ge(shared, 3 * p + 1)
                    nc.vector.reciprocal(hs[:], sig[:, 1, :]).then_inc(shared, 1)
                    dve.wait_ge(shared, 3 * p + 2)
                    nc.vector.tensor_tensor(hs[:], hs[:], z[:], ALU.mult).then_inc(shared, 1)

                def keep_x3(p, par, n):
                    full(dve, n)
                    nc.vector.scalar_tensor_tensor(out=X3[:, bass.ds(p, 1), :].rearrange("q o d -> q (o d)"), in0=misc[:NQ, :D],
                                                   scalar=g_tanh[:NQ, 3:4], in1=stage[:, 0:D], op0=ALU.mult, op1=ALU.add).then_inc(misc_free, 1)

                hooks = {"xT": keep_xT, "ctxT": keep_ctxT, "wo": residual, "lnT": keep_lnT}
                if A:
                    hooks |= {"v01": keep_v((0, 1)), "v2": keep_v((2,))}
                else:
                    hooks |= {"router": keep_affinity, "rank": place, "shared_down": keep_x3} | {f"ho{g}": keep_heads(g) for g in range(NG)}
                if A:
                    parts_x = {0: moments_x, 2: norm_x, 7: split_q}
                    parts_y = {4: [moments_y], 5: [norm_y], 13: [update_terms], 15: [update]}
                else:
                    parts_x = {0: h_sum, 2: moments_x, 3: norm_x}
                    parts_y = {4: [moments_y], 5: [norm_y], 9: [choose], 10: [sigmoids], 11: [weigh], 12: [shared_silu],
                               14: [lambda p: pick(p, range(0, 4))], 15: [lambda p: pick(p, range(4, 8)), place_end]}

                def parts(i, h, par, first, last):
                    if h in parts_y and not first:
                        for part in parts_y[h]:
                            part(i - 1)
                    if h in parts_x and not last:
                        parts_x[h](i + 1, 1 - par)

                nc.vector.memset(spare[:], 0.0).then_inc(spare_set, 1)
                dve.wait_ge(spare_set, 1)
                for h in sorted(parts_x)[:3 - A]:
                    parts_x[h](0, 0)
                uses.run(hooks, -1, None, 1, first=True, **({"then": ("q", lambda: split_q(0, 0))} if A else {}))
                for h in range(LEAD):
                    maximum(0, h)
                normalise(0, 0)

                def body(i, par, first, last):
                    for h in range(H):
                        if h + LEAD < H:
                            maximum(i, h + LEAD)
                        elif not last:
                            maximum(i + 1, h + LEAD - H)
                        if h + 1 < H:
                            normalise(i, h + 1)
                        elif not last:
                            normalise(i + 1, 0)
                        uses.run(hooks, i, h, par, first, last)
                        parts(i, h, par, first, last)

                walk(nc.vector, NB, body)
                for h in range(H):
                    for slot, kind, name in uses.order:
                        if slot == h and kind == "post" and name in hooks:
                            hooks[name](NB - 1, 1, uses.before(NB, name))
                    parts(NB, h, 0, False, True)
                if A:
                    n = uses.out(NB - 1, "h_in")
                    full(dve, n)
                    nc.vector.tensor_tensor(w["cf"][:NQ, :], misc[:NQ, :D], w["bo_ffn"][:NQ, :], ALU.add).then_inc(misc_free, 1)
                    dve.wait_ge(misc_free, n + 1)

            @block.gpsimd
            def _(pool):
                def power(st, j, counted, rstd):
                    pool.wait_ge(counted, 3 * j + 3)
                    nc.gpsimd.tensor_tensor(st[:, 9:10], st[:, 8:9], w["neg_half"][:NQ, :], ALU.pow).then_inc(rstd, 1)

                def residual_x(j, par):
                    if A:
                        pool.wait_ge(x_in[par], loads(j, par))
                    else:
                        pool.wait_ge(x2_ready, j + 1)
                    wait(pool, misc_free, uses.out(j - 2, "wo"))
                    nc.gpsimd.tensor_tensor(xres[par][:], xt[par][:, 0:D], w["tgbo"][layer][:NQ, :], ALU.add).then_inc(xres_ready, 1)

                def split_k(j, c):
                    pool.wait_ge(misc_free, uses.out(j, f"k{c}"))
                    for dst in (k_rest[:, c, :], k_parts[:, 1, c, :NK]):
                        nc.gpsimd.tensor_tensor(dst, kT[:, c, :], k_parts[:, 0, c, :NK], ALU.subtract).then_inc(k_split, 1)
                    pool.wait_ge(k_split, 6 * j + (3 * c + 2))
                    nc.gpsimd.tensor_tensor(k_parts[:, 2, c, :NK], k_rest[:, c, :], k_parts[:, 1, c, :NK], ALU.subtract).then_inc(k_split, 1)

                def fill(p):
                    pool.wait_ge(y_normed, p + 1)
                    pool_wait_apart(pool, scattered, 16 * TOP_K * p, pool_spare, 0)
                    nc.gpsimd.tensor_copy(rows[:, :, 0:D], x1ln[:].unsqueeze(1).to_broadcast([NQ, TOP_K, D])).then_inc(kept, 1)
                    if not (isinstance(p, int) and p == 0):
                        nc.gpsimd.tensor_scalar(rows[:, :, D], rows[:, :, D], float(NQ * TOP_K), None, ALU.add).then_inc(renumbered, 1)

                def scatter(p):
                    if not (isinstance(p, int) and p == 0):
                        pool_wait_apart(pool, renumbered, p, pool_spare, 1)
                    pool_wait_apart(pool, kept, p + 1, pool_spare, 2)
                    pool_wait_apart(pool, placed, N_PLACED * (p + 1), pool_spare, 3)
                    nc.gpsimd.tensor_copy(rows[:, :, D + 1], slot_w[:]).then_inc(weighted, 1)
                    pool_wait_apart(pool, weighted, p + 1, pool_spare, 4)
                    for k in range(TOP_K):
                        nc.gpsimd.indirect_dma_start(rows_d, bass.IndirectOffsetOnAxis(ap=ids[:, k:k + 1], axis=0),
                                                     rows[:, k, :], None).then_inc(scattered, 16)

                def before(j, par):
                    power(stats[:, 0, :], j, x_stats, x_rstd)
                    if A:
                        split_k(j, 0)
                    residual_x(j, par)

                def after(p):
                    power(stats[:, 1, :], p, y_stats, y_rstd)
                    if not A:
                        if not (isinstance(p, int) and p == 0):
                            scatter(p - 1)
                        fill(p)

                nc.gpsimd.memset(pool_spare[:], 0.0).then_inc(pool_spare_set, 1)
                pool.wait_ge(pool_spare_set, 1)
                if A:
                    for n in range(2):
                        nc.gpsimd.memset(vals[n][:], 0.0).then_inc(padded, 1)
                else:
                    nc.gpsimd.iota(numbers[:], pattern=[[1, TOP_K]], base=0, channel_multiplier=TOP_K).then_inc(numbered, 1)
                    pool.wait_ge(numbered, 1)
                    nc.gpsimd.tensor_copy(rows[:, :, D], numbers[:]).then_inc(numbered, 1)
                    pool.wait_ge(numbered, 2)
                before(0, 0)
                if A:
                    split_k(0, 1)

                def body(i, par, first, last):
                    if not last:
                        before(i + 1, 1 - par)
                    if not first:
                        after(i - 1)
                    if A and not last:
                        split_k(i + 1, 1)

                walk(nc.gpsimd, NB, body)
                after(NB - 1)
                if not A:
                    scatter(NB - 1)
                    pool.wait_ge(scattered, 16 * TOP_K * NB)


def tables(nc, t, w, bank, table_d, rows_d, table, starts_pad, wup):
    NB, NQ, D = t["x"].shape
    E = t["L1_ffn_W_up"].shape[0]
    CAP, N = experts_shape(t)
    CH = -(-N // P)
    with ExitStack() as es:
        def sb(name, shape, dt=F32):
            return es.enter_context(nc.sbuf_tensor(name, shape, dt))

        def sem(name):
            return es.enter_context(nc.semaphore(name))

        count, tiles_i = sb("count", [P, E]), sb("tiles_i", [P, 2, E], I32)
        tiles, upto, picked = sb("tiles", [P, E]), sb("upto", [P, E]), sb("picked", [P, E])
        tau_i, tau = sb("tau_i", [P, CH], I32), sb("tau", [P, CH])
        found = sb("found", [P, 4, CH])
        tab = sb("tab", [P, CH, 2], I32)
        zeros, beyond = sb("zeros", [P, D + 2]), sb("beyond", [P, 1], I32)
        counted, made, tau_made, zeroed = sem("counted"), sem("made"), sem("tau_made"), sem("zeroed")
        tab_out, tab_in, padded, wup_in = sem("tab_out"), sem("tab_in"), sem("pads_written"), sem("wup_in")
        padded_too = sem("pads_written_too")
        N_MADE = 6 + 6 * CH

        with nc.Block() as block:

            @block.tensor
            def _(pe):
                pe.matmul(bank[0][:, :E], w["ones"][:NQ, :], w["chosen"][:], start=True, stop=True).then_inc(counted, 1)

            @block.gpsimd
            def _(pool):
                nc.gpsimd.iota(tau_i[:], pattern=[[P, CH]], base=0, channel_multiplier=1).then_inc(tau_made, 1)
                nc.gpsimd.memset(zeros[:], 0.0).then_inc(zeroed, 1)
                nc.gpsimd.iota(beyond[:], pattern=[[0, 1]], base=NB * NQ * TOP_K, channel_multiplier=1).then_inc(zeroed, 1)
                pool.wait_ge(zeroed, 2)
                nc.gpsimd.tensor_copy(zeros[:, D:D + 1], beyond[:]).then_inc(zeroed, 1)

            @block.vector
            def _(dve):
                done = [0]

                def step(ins):
                    ins.then_inc(made, 1)
                    done[0] += 1
                    dve.wait_ge(made, done[0])

                dve.wait_ge(counted, 1)
                dve.wait_ge(tau_made, 1)
                step(nc.vector.tensor_copy(tau[:], tau_i[:]))
                step(nc.vector.tensor_scalar(tiles_i[:, 0, :], bank[0][:, :E], float(P - 1), None, ALU.add))
                step(nc.vector.scalar_tensor_tensor(out=starts_pad[:], in0=bank[0][0:1, :E], scalar=-1.0, in1=w["region"][0:1, :],
                                                    op0=ALU.add, op1=ALU.add))
                step(nc.vector.tensor_scalar(tiles_i[:, 1, :], tiles_i[:, 0, :], P.bit_length() - 1, None, ALU.arith_shift_right))
                step(nc.vector.tensor_copy(tiles[:], tiles_i[:, 1, :]))
                step(nc.vector.tensor_tensor_scan(upto[:], w["ones"][:, :E], tiles[:], 0.0, ALU.mult, ALU.add))
                for c in range(CH):
                    step(nc.vector.scalar_tensor_tensor(out=picked[:], in0=upto[:], scalar=tau[:, c:c + 1], in1=w["ones"][:, :E],
                                                        op0=ALU.is_le, op1=ALU.mult, accum_out=found[:, 0, c:c + 1]))
                    step(nc.vector.scalar_tensor_tensor(out=picked[:], in0=upto[:], scalar=tau[:, c:c + 1], in1=tiles[:],
                                                        op0=ALU.is_le, op1=ALU.mult, accum_out=found[:, 1, c:c + 1]))
                    step(nc.vector.tensor_scalar(found[:, 2, c:c + 1], tau[:, c:c + 1], found[:, 1, c:c + 1], float(P), ALU.subtract, ALU.mult))
                    step(nc.vector.scalar_tensor_tensor(out=found[:, 3, c:c + 1], in0=found[:, 0, c:c + 1], scalar=float(CAP), in1=found[:, 2, c:c + 1],
                                                        op0=ALU.mult, op1=ALU.add))
                    step(nc.vector.tensor_scalar(tab[:, c, 1:2], found[:, 3, c:c + 1], float(E * CAP), None, ALU.min))
                    step(nc.vector.tensor_scalar(tab[:, c, 0:1], found[:, 0, c:c + 1], float(E - 1), None, ALU.min))
                

            def pad(eng, kind, first, semaphore):
                eng.wait_ge(zeroed, 3)
                eng.wait_ge(made, 3)
                with eng.Fori(0, E // 8) as m:
                    for k in range(4):
                        row = nc.values_load(starts_pad[0:1, bass.ds(m * 4 + (first + k), 1)], engines=(kind,), min_val=0, max_val=E * CAP - P,
                                             skip_runtime_bounds_check_because="a region has a tile's rows more than there are tokens")
                        eng.dma_start(rows_d[bass.ds(row, P), :], zeros[:]).then_inc(semaphore, 16)

            @block.scalar
            def _(act):
                for e in range(0, E, 16):
                    for c in range(D // P):
                        act.dma_start(wup[:, e:e + 16, c * P:(c + 1) * P],
                                      t["L1_ffn_W_up"][e:e + 16, c * P:(c + 1) * P, :].rearrange("e p f -> p e f")).then_inc(wup_in, 16)
                pad(nc.scalar, mybir.EngineType.Activation, E // 2, padded_too)
                act.wait_ge(wup_in, 16 * (E // 16) * (D // P))
                act.wait_ge(padded_too, 16 * (E // 2))

            @block.sync
            def _(sp):
                sp.wait_ge(zeroed, 3)
                sp.dma_start(rows_d[E * CAP:E * CAP + P, :], zeros[:]).then_inc(padded, 16)
                pad(nc.sync, mybir.EngineType.SP, 0, padded)
                sp.wait_ge(made, N_MADE)
                sp.dma_start(table_d.rearrange("(c p) k -> p c k", p=P), tab[:]).then_inc(tab_out, 16)
                sp.wait_ge(tab_out, 16)
                sp.dma_start(table[:], table_d.rearrange("(o n) k -> o (n k)", o=1)).then_inc(tab_in, 16)
                sp.wait_ge(tab_in, 16)
                sp.wait_ge(padded, 16 * (E // 2 + 1))


def expert_phase(nc, t, w, bank, rows_d, results_d, table, wup, wdn):
    D = t["x"].shape[2]
    E = t["L1_ffn_W_up"].shape[0]
    CAP, N = experts_shape(t)
    RB = 8
    TURN = 16
    RES = 4
    CC = D // P
    with ExitStack() as es:
        def sem(name):
            return es.enter_context(nc.semaphore(name))

        def buffers(weights, a, b, first=0):
            return weights[:, first:first + a * b].rearrange("p (a b) -> p a b", a=a)

        mqk = w["mqk"][:].rearrange("p c h k -> p (c h k)")
        xr = buffers(mqk, RB, D + 2)
        xrT = buffers(mqk, 2, D, RB * (D + 2))
        hid, hidT = buffers(mqk, 2, P, (RB + 2) * (D + 2)), buffers(mqk, 2, P, (RB + 3) * (D + 2))
        res = buffers(w["wo1"][:].rearrange("p c d -> p (c d)"), RES, D)
        x_in = [sem(f"rows_in{b}") for b in range(RB)]
        res_out = [sem(f"results_out{b}") for b in range(RES)]
        x_turned, xT_out, upped, silued = sem("x_turned"), sem("xT_out"), sem("upped"), sem("silued")
        h_turned, hT_out, downed, res_made = sem("h_turned"), sem("hT_out"), sem("downed"), sem("res_made")
        spare_set, carried = sem("spare_set"), sem("carried")
        dest = es.enter_context(nc.sbuf_tensor("dest", [P, RB], U32))
        spare = es.enter_context(nc.sbuf_tensor("spare", [P, 2 + RES], F32))
        ident = w["ident"]

        def tiles(body):
            def f(eng):
                for b in range(TURN):
                    body(b, b % RB)
                with eng.Fori(1, N // TURN - 1) as m:
                    for b in range(TURN):
                        body(m * TURN + b, b % RB)
                for b in range(TURN):
                    body(N - TURN + b, b % RB)
            return f

        def inside(n):
            return not isinstance(n, int) or 0 <= n < N

        def passes(n, b, ring):
            return (n - b % ring) * (16 // ring)

        def from_table(engine, n, column, most):
            return nc.values_load(table[0:1, bass.ds(n * 2 + column, 1)], engines=(engine,), min_val=0, max_val=most,
                                  skip_runtime_bounds_check_because="the table is made with a minimum against this bound")

        with nc.Block() as block:

            @block.sync
            def _(sp):
                def load(n, b):
                    wait(sp, res_made, n - RB + 1)
                    row = from_table(mybir.EngineType.SP, n, 1, E * CAP)
                    sp.dma_start(xr[:, b, :], rows_d[bass.ds(row, P), :]).then_inc(x_in[b], 16)

                tiles(load)(nc.sync)

            @block.gpsimd
            def _(pool):
                nc.gpsimd.memset(spare[:], 0.0).then_inc(spare_set, 1)
                pool.wait_ge(spare_set, 1)

                def body(n, b):
                    wait(pool, carried, n - RES + 1)
                    pool_wait_apart(pool, res_made, n + 1, spare, b % RES).then_inc(carried, 1)
                    nc.gpsimd.indirect_dma_start(results_d, bass.IndirectOffsetOnAxis(ap=dest[:, b:b + 1], axis=0),
                                                 res[:, b % RES, :], None, bounds_check=results_d.shape[0] - 1,
                                                 oob_is_err=False).then_inc(res_out[b % RES], 16)

                tiles(body)(nc.gpsimd)
                for b in range(RES):
                    pool.wait_ge(res_out[b], 16 * (N // RES))

            @block.tensor
            def _(pe):
                def turn_rows(n, b):
                    pe.wait_ge(x_in[b], passes(n, b, RB) + 16)
                    for c in range(CC):
                        mm = pe.transpose(bank[b % 2][:, c * P:(c + 1) * P], xr[:, b, c * P:(c + 1) * P], ident[:])
                    mm.then_inc(x_turned, 1)

                def up(n, b, e):
                    pe.wait_ge(xT_out, n + 1)
                    for c in range(CC):
                        mm = pe.matmul(bank[2 + b % 2][:, :P], xrT[:, b % 2, c * P:(c + 1) * P],
                                       wup[:, bass.ds(e, 1), c * P:(c + 1) * P].rearrange("p o f -> p (o f)"),
                                       start=(c == 0), stop=(c == CC - 1))
                    mm.then_inc(upped, 1)

                def turn_hidden(n, b):
                    pe.wait_ge(silued, n + 1)
                    pe.transpose(bank[4 + b % 2][:, :P], hid[:, b % 2, :], ident[:]).then_inc(h_turned, 1)

                def down(n, b, e):
                    pe.wait_ge(hT_out, n + 1)
                    pe.matmul(bank[6 + b % 2][:, :D], hidT[:, b % 2, :], wdn[:, bass.ds(e, 1), :].rearrange("p o d -> p (o d)"),
                              start=True, stop=True).then_inc(downed, 1)

                def round(base):
                    experts = {}

                    def expert(b):
                        if b not in experts:
                            experts[b] = from_table(mybir.EngineType.PE, base + b, 0, E - 1)
                        return experts[b]

                    for b in range(TURN):
                        n = base + b
                        if inside(n + 1):
                            expert(b + 1)
                        if inside(n - 2):
                            expert(b - 2)
                        if inside(n + 2):
                            turn_rows(n + 2, (b + 2) % RB)
                        if inside(n - 2):
                            down(n - 2, (b - 2) % RB, expert(b - 2))
                        if inside(n + 1):
                            up(n + 1, (b + 1) % RB, expert(b + 1))
                        turn_hidden(n, b % RB)

                turn_rows(0, 0)
                turn_rows(1, 1)
                up(0, 0, from_table(mybir.EngineType.PE, 0, 0, E - 1))
                round(0)
                with nc.tensor.Fori(1, N // TURN - 1) as m:
                    round(m * TURN)
                round(N - TURN)
                for n in (N - 2, N - 1):
                    pe.wait_ge(res_made, n - 1)
                    down(n, n % RB, from_table(mybir.EngineType.PE, n, 0, E - 1))

            @block.vector
            def _(dve):
                def keep_xT(n, b):
                    dve.wait_ge(x_turned, n + 1)
                    nc.vector.tensor_copy(xrT[:, b % 2, :], bank[b % 2][:, :D]).then_inc(xT_out, 1)

                def keep_hT(n, b):
                    dve.wait_ge(h_turned, n + 1)
                    nc.vector.tensor_copy(dest[:, b:b + 1], xr[:, b, D:D + 1])
                    nc.vector.tensor_copy(hidT[:, b % 2, :], bank[4 + b % 2][:, :P]).then_inc(hT_out, 1)

                keep_xT(0, 0)
                keep_xT(1, 1)

                def body(n, b):
                    if inside(n + 2):
                        keep_xT(n + 2, (b + 2) % RB)
                    keep_hT(n, b)

                tiles(body)(nc.vector)

            @block.scalar
            def _(act):
                def silu(n, b):
                    act.wait_ge(upped, n + 1)
                    nc.scalar.activation(hid[:, b % 2, :], bank[2 + b % 2][:, :P], ACT.Silu).then_inc(silued, 1)

                def keep_result(n, b):
                    wait(act, res_out[b % RES], passes(n, b, RES))
                    act.wait_ge(downed, n + 1)
                    nc.scalar.activation(res[:, b % RES, :], bank[6 + b % 2][:, :D], ACT.Copy, scale=xr[:, b, D + 1:D + 2]).then_inc(res_made, 1)

                silu(0, 0)

                def body(n, b):
                    if inside(n - 2):
                        keep_result(n - 2, (b - 2) % RB)
                    if inside(n + 1):
                        silu(n + 1, (b + 1) % RB)

                tiles(body)(nc.scalar)
                keep_result(N - 2, RB - 2)
                keep_result(N - 1, RB - 1)


def combine_phase(nc, t, w, results_d, X3, out):
    NB, NQ, D = t["x"].shape
    RB = 4
    with ExitStack() as es:
        def sb(name, shape, dt=F32):
            return es.enter_context(nc.sbuf_tensor(name, shape, dt))

        def sem(name):
            return es.enter_context(nc.semaphore(name))

        got = [sb(f"got{n}", [NQ, TOP_K, D]) for n in range(RB)]
        total, acc = ([sb(f"{a}{n}", [NQ, D]) for n in range(RB)] for a in ("total", "acc"))
        summed, added = sem("summed"), sem("added")
        arrived = [sem(f"arrived{n}") for n in range(RB)]
        written = [sem(f"written{n}") for n in range(RB)]
        results = results_d.rearrange("(b q k) d -> b q (k d)", b=NB, q=NQ)

        def rounds(eng, body):
            for b in range(RB):
                body(b, b)
            with eng.Fori(1, NB // RB) as m:
                for b in range(RB):
                    body(m * RB + b, b)

        with nc.Block() as block:

            @block.sync
            def _(sp):
                def load(i, b):
                    wait(sp, summed, i - RB + 1)
                    sp.dma_start(flat(got[b]), seq(results, i)).then_inc(arrived[b], 16)

                rounds(nc.sync, load)

            @block.vector
            def _(dve):
                def body(i, b):
                    dve.wait_ge(arrived[b], (i - b) * (16 // RB) + 16)
                    wait(dve, added, i - RB + 1)
                    nc.vector.tensor_reduce(total[b][:], got[b][:].rearrange("q k d -> q d k"), AX, ALU.add).then_inc(summed, 1)

                rounds(nc.vector, body)

            @block.gpsimd
            def _(pool):
                def body(i, b):
                    wait(pool, written[b], (i - b) * (16 // RB))
                    pool.wait_ge(summed, i + 1)
                    nc.gpsimd.tensor_tensor(acc[b][:], total[b][:], X3[:, bass.ds(i, 1), :].rearrange("q o d -> q (o d)"), ALU.add).then_inc(added, 1)

                rounds(nc.gpsimd, body)

            @block.scalar
            def _(act):
                def body(i, b):
                    act.wait_ge(added, i + 1)
                    act.dma_start(seq(out, i), acc[b][:]).then_inc(written[b], 16)

                rounds(nc.scalar, body)
                for b in range(RB):
                    act.wait_ge(written[b], 16 * (NB // RB))


def build_kernel(nc, t, out):
    NB, NQ, D = t["x"].shape
    E = t["L1_ffn_W_up"].shape[0]
    CAP, N = experts_shape(t)
    x1pre_d = nc.dram_tensor("x1_and_h_in", [NB, NQ, 2 * D], F32).ap()
    NK = t["ctx_512"].shape[1]
    parts_d = [[nc.dram_tensor(f"{name}_parts{n}", [PARTS, D // P, P, rows], BF16).ap() for n in range(2)]
               for name, rows in (("key", -(-NK // 8) * 8), ("query", NQ))]
    rows_d = nc.dram_tensor("expert_rows", [E * CAP + P, D + 2], F32).ap()
    results_d = nc.dram_tensor("expert_results", [NB * NQ * TOP_K, D], F32).ap()
    table_d = nc.dram_tensor("tile_table", [-(-N // P) * P, 2], I32).ap()
    with ExitStack() as es:
        def sb(name, shape, dt=F32):
            return es.enter_context(nc.sbuf_tensor(name, shape, dt))

        bank = [es.enter_context(nc.psum_tensor(f"bank{n}", [P, 512], F32)) for n in range(BANKS)]
        w = allocate(nc, es, t)
        with ExitStack() as layer0:
            w |= allocate_a(nc, layer0, t)
            setup(nc, t, w, bank)
            attention_phase(nc, t, w, bank, x1pre_d, 0, parts_d=parts_d)
        X3 = sb("X3", [NQ, NB, D])
        with ExitStack() as weights:
            wdn = weights.enter_context(nc.sbuf_tensor("wdn", [P, E, D], F32))
            attention_phase(nc, t, w, bank, x1pre_d, 1, rows_d=rows_d, X3=X3, wdn=wdn)
            wup = weights.enter_context(nc.sbuf_tensor("wup", [P, E, D], F32))
            table = weights.enter_context(nc.sbuf_tensor("table", [1, table_d.shape[0] * 2], I32))
            starts_pad = weights.enter_context(nc.sbuf_tensor("starts_pad", [1, E], I32))
            tables(nc, t, w, bank, table_d, rows_d, table, starts_pad, wup)
            expert_phase(nc, t, w, bank, rows_d, results_d, table, wup, wdn)
        combine_phase(nc, t, w, results_d, X3, out)


_INS = ['x', 'ctx_512', 'g_xattn', 'g_ffn', 'L0_xattn_Wq', 'L0_xattn_bq', 'L0_xattn_Wk', 'L0_xattn_bk', 'L0_xattn_Wv',
        'L0_xattn_bv', 'L0_xattn_Wo', 'L0_xattn_bo', 'L0_ffn_wf', 'L0_ffn_uf', 'L0_ffn_bf', 'L0_ffn_wi', 'L0_ffn_ui',
        'L0_ffn_bi', 'L0_ffn_wc', 'L0_ffn_uc', 'L0_ffn_bc', 'L0_ffn_wo', 'L0_ffn_uo', 'L0_ffn_bo', 'L0_ffn_in_c',
        'L1_xattn_Wq', 'L1_xattn_Wk', 'L1_xattn_Wv', 'L1_xattn_Wo', 'L1_xattn_bo', 'L1_ffn_centroids',
        'L1_ffn_expert_biases', 'L1_ffn_Ws_up', 'L1_ffn_Ws_down', 'L1_ffn_W_up', 'L1_ffn_W_down']


def kernel(**inputs):
    import numpy as _np
    import concourse.bacc as _bacc
    from concourse import mybir as _mybir
    from concourse.bass_utils import run_bass_kernel_spmd as _run

    nc = _bacc.Bacc("TRN2", target_bir_lowering=False, num_devices=1)
    arrays, t = {}, {}
    for name in _INS:
        a = _np.ascontiguousarray(inputs[name])
        arrays[f"in_{name}_dram"] = a
        t[name] = nc.dram_tensor(f"in_{name}_dram", a.shape, _mybir.dt.from_np(a.dtype), kind="ExternalInput").ap()
    out = nc.dram_tensor("out_0_dram", inputs["x"].shape, _mybir.dt.float32, kind="ExternalOutput").ap()
    build_kernel(nc, t, out)
    r = _run(nc, [arrays], core_ids=[0])
    return r.results[0]["out_0_dram"]
```
